# Optimizing a Trainium2 kernel written in Bass

```python
import numpy as np
import jax
import jax.numpy as jnp

def _softmax(x, axis=-1):
    return jax.nn.softmax(x, axis=axis)

def _gelu(x):
    return jax.nn.gelu(x, approximate=True)

def _silu(x):
    return jax.nn.silu(x)

def _sigmoid(x):
    return jax.nn.sigmoid(x)

def _layernorm(x, axis=-1, eps=1e-05):
    m = jnp.mean(x, axis=axis, keepdims=True)
    v = jnp.var(x, axis=axis, keepdims=True)
    return (x - m) / jnp.sqrt(v + eps)

def _scatter_add(tgt, idx, src, axis=0):
    return tgt.at[idx].add(src)

def _segment_sum(src, seg, n):
    return jax.ops.segment_sum(src, seg, n)
kernel_name = 'mk_decoder_postln_d1_seqx_r2_ef28ba'

def setup_inputs(seed: int=0):
    np.random.seed(seed)
    _w = jnp.asarray

    def _rec_inputs():
        import jax
        import jax.numpy as jnp
        _rk = jax.random.key(seed)
        x = -0.0002928 + 1 * jax.random.normal(jax.random.fold_in(_rk, 1), (8, 224, 512), jnp.float32)
        _lenS = 224 - jax.random.randint(jax.random.fold_in(_rk, 7), (8,), 0, max(1, 224 // 4) + 1, jnp.int32)
        _lenS2 = 750 - jax.random.randint(jax.random.fold_in(_rk, 8), (8,), 0, max(1, 750 // 4) + 1, jnp.int32)
        _ctx_1024P = jax.random.normal(jax.random.fold_in(_rk, 11), (8, 16, 512), jnp.float32)
        _ctx_1024c = jax.random.dirichlet(jax.random.fold_in(_rk, 511), 0.3 * jnp.ones((16,), jnp.float32), (8, 750))
        _ctx_1024t = jnp.einsum('bsk,bkd->bsd', _ctx_1024c, _ctx_1024P)
        _ctx_1024t = _ctx_1024t * jax.lax.rsqrt(jnp.mean(jnp.square(_ctx_1024t)) + 1e-12) * 0.953939
        ctx_1024 = -1.39393e-06 + 0.999914 * (_ctx_1024t + 0.3 * jax.random.normal(jax.random.fold_in(_rk, 611), (8, 750, 512), jnp.float32))
        _validS = jnp.arange(224)[None, :] < _lenS[:, None]
        _validS2 = jnp.arange(750)[None, :] < _lenS2[:, None]
        _causal = jnp.tril(jnp.ones((224, 224), dtype=bool))
        mask_BxSxS2_bf0 = jnp.logical_not(jnp.ones((8, 224, 750), dtype=bool))
        return (x, ctx_1024, mask_BxSxS2_bf0)
    x, ctx_1024, mask_BxSxS2_bf0 = _rec_inputs()

    def _L0_attn_setup():
        import jax, jax.numpy as jnp
        import numpy as np
        import math
        D_MODEL = 512
        NUM_HEADS = 16
        B, L = (2, 1024)
        PERIODS = (1.0, 30.0)
        WEIGHTS = (0.8, 0.4)
        SIGMAS = (0.5, 2.0)

        def _gaussian_mask(length):
            idx = jnp.arange(length, dtype=jnp.float32)
            delta = jnp.abs(idx[:, None] - idx[None, :])
            mask = jnp.zeros_like(delta)
            for p, w, sigma in zip(PERIODS, WEIGHTS, SIGMAS):
                if p < 0.2:
                    continue
                mask = mask + w * jnp.exp(-(delta - p) ** 2 / (2.0 * sigma ** 2))
            return mask
        key = jax.random.key(seed)
        ks = jax.random.split(key, 10)
        s = 1.0 / math.sqrt(D_MODEL)
        inp = {'x': jax.random.normal(ks[0], (B, L, D_MODEL), dtype=jnp.float32), 'Wq': jax.random.normal(ks[1], (D_MODEL, D_MODEL), dtype=jnp.float32) * s, 'bq': jax.random.normal(ks[2], (D_MODEL,), dtype=jnp.float32) * 0.01, 'Wk': jax.random.normal(ks[3], (D_MODEL, D_MODEL), dtype=jnp.float32) * s, 'bk': jax.random.normal(ks[4], (D_MODEL,), dtype=jnp.float32) * 0.01, 'Wv': jax.random.normal(ks[5], (D_MODEL, D_MODEL), dtype=jnp.float32) * s, 'bv': jax.random.normal(ks[6], (D_MODEL,), dtype=jnp.float32) * 0.01, 'Wo': jax.random.normal(ks[7], (D_MODEL, D_MODEL), dtype=jnp.float32) * s, 'bo': jax.random.normal(ks[8], (D_MODEL,), dtype=jnp.float32) * 0.01, 'prior_lambda': jnp.asarray(2.0, dtype=jnp.float32)}
        return inp
    _L0_attn_all = _L0_attn_setup()
    _L0_attn_in = {k: v for k, v in _L0_attn_all.items() if k in ('Wq', 'bq', 'Wk', 'bk', 'Wv', 'bv', 'Wo', 'bo', 'prior_lambda')}
    del _L0_attn_all

    def _L0_xattn_setup():
        import jax, jax.numpy as jnp
        import numpy as np
        NUM_HEADS = 16
        NEG_INF = float('-inf')
        key = jax.random.key(seed)
        ks = jax.random.split(key, 8)
        B, S, D = (2, 1024, 512)
        return {'query': jax.random.normal(ks[0], (B, S, D), jnp.float32), 'key': jax.random.normal(ks[1], (B, S, D), jnp.float32), 'value': jax.random.normal(ks[2], (B, S, D), jnp.float32), 'attention_mask': jnp.zeros((B, S, S), dtype=bool), 'Wq': jax.random.normal(ks[3], (D, D), jnp.float32) * D ** (-0.5), 'Wk': jax.random.normal(ks[4], (D, D), jnp.float32) * D ** (-0.5), 'Wv': jax.random.normal(ks[5], (D, D), jnp.float32) * D ** (-0.5), 'Wout': jax.random.normal(ks[6], (D, D), jnp.float32) * D ** (-0.5), 'b_out': jnp.zeros((D,), jnp.float32), 'is_causal': 1}
    _L0_xattn_all = _L0_xattn_setup()
    _L0_xattn_in = {k: v for k, v in _L0_xattn_all.items() if k in ('Wq', 'Wk', 'Wv', 'Wout', 'b_out')}
    del _L0_xattn_all

    def _L0_ffn_setup():
        import jax, jax.numpy as jnp
        import numpy as np
        D_MODEL = 512
        NUM_EXPERTS = 8
        TOP_K = 2
        key = jax.random.key(seed)
        ks = jax.random.split(key, 5)
        scale = 1.0 / np.sqrt(D_MODEL)
        x = jax.random.normal(ks[0], (4, 1024, D_MODEL), dtype=jnp.float32)
        We = jax.random.uniform(ks[1], (NUM_EXPERTS, D_MODEL, D_MODEL), jnp.float32, -scale, scale)
        be = jax.random.uniform(ks[2], (NUM_EXPERTS, D_MODEL), jnp.float32, -scale, scale)
        Wg = jax.random.uniform(ks[3], (NUM_EXPERTS, D_MODEL), jnp.float32, -scale, scale)
        bg = jax.random.uniform(ks[4], (NUM_EXPERTS,), jnp.float32, -scale, scale)
        return {'x': x, 'We': We, 'be': be, 'Wg': Wg, 'bg': bg}
    _L0_ffn_all = _L0_ffn_setup()
    _L0_ffn_in = {k: v for k, v in _L0_ffn_all.items() if k in ('We', 'be', 'Wg', 'bg')}
    del _L0_ffn_all
    return {'x': x, 'ctx_1024': ctx_1024, 'mask_BxSxS2_bf0': mask_BxSxS2_bf0, 'L0_attn_Wq': _L0_attn_in['Wq'], 'L0_attn_bq': _L0_attn_in['bq'], 'L0_attn_Wk': _L0_attn_in['Wk'], 'L0_attn_bk': _L0_attn_in['bk'], 'L0_attn_Wv': _L0_attn_in['Wv'], 'L0_attn_bv': _L0_attn_in['bv'], 'L0_attn_Wo': _L0_attn_in['Wo'], 'L0_attn_bo': _L0_attn_in['bo'], 'L0_attn_prior_lambda': _L0_attn_in['prior_lambda'], 'L0_xattn_Wq': _L0_xattn_in['Wq'], 'L0_xattn_Wk': _L0_xattn_in['Wk'], 'L0_xattn_Wv': _L0_xattn_in['Wv'], 'L0_xattn_Wout': _L0_xattn_in['Wout'], 'L0_xattn_b_out': _L0_xattn_in['b_out'], 'L0_ffn_We': _L0_ffn_in['We'], 'L0_ffn_be': _L0_ffn_in['be'], 'L0_ffn_Wg': _L0_ffn_in['Wg'], 'L0_ffn_bg': _L0_ffn_in['bg']}

def reference(x, ctx_1024, mask_BxSxS2_bf0, L0_attn_Wq, L0_attn_bq, L0_attn_Wk, L0_attn_bk, L0_attn_Wv, L0_attn_bv, L0_attn_Wo, L0_attn_bo, L0_attn_prior_lambda, L0_xattn_Wq, L0_xattn_Wk, L0_xattn_Wv, L0_xattn_Wout, L0_xattn_b_out, L0_ffn_We, L0_ffn_be, L0_ffn_Wg, L0_ffn_bg):
    import jax
    import jax.numpy as jnp

    def _L0_attn_ref(x, Wq, bq, Wk, bk, Wv, bv, Wo, bo, prior_lambda):
        import jax, jax.numpy as jnp
        import numpy as np
        import math
        D_MODEL = 512
        NUM_HEADS = 16
        B, L = (2, 1024)
        PERIODS = (1.0, 30.0)
        WEIGHTS = (0.8, 0.4)
        SIGMAS = (0.5, 2.0)

        def _gaussian_mask(length):
            idx = jnp.arange(length, dtype=jnp.float32)
            delta = jnp.abs(idx[:, None] - idx[None, :])
            mask = jnp.zeros_like(delta)
            for p, w, sigma in zip(PERIODS, WEIGHTS, SIGMAS):
                if p < 0.2:
                    continue
                mask = mask + w * jnp.exp(-(delta - p) ** 2 / (2.0 * sigma ** 2))
            return mask
        Bx, Lx, D = x.shape
        H = NUM_HEADS
        hd = D // H

        def split_heads(t):
            return t.reshape(Bx, Lx, H, hd).transpose(0, 2, 1, 3)
        Q = split_heads(x @ Wq.T + bq)
        K = split_heads(x @ Wk.T + bk)
        V = split_heads(x @ Wv.T + bv)
        scores = jnp.einsum('bhqd,bhkd->bhqk', Q, K) / math.sqrt(hd)
        scores = scores + prior_lambda * _gaussian_mask(Lx)[None, None, :, :]
        attn = jax.nn.softmax(scores, axis=-1)
        out = jnp.einsum('bhqk,bhkd->bhqd', attn, V)
        out = out.transpose(0, 2, 1, 3).reshape(Bx, Lx, D)
        return out @ Wo.T + bo

    def _L0_xattn_ref(query, key, value, attention_mask, Wq, Wk, Wv, Wout, b_out, is_causal):
        import jax, jax.numpy as jnp
        import numpy as np
        NUM_HEADS = 16
        NEG_INF = float('-inf')
        B, q_len, D = query.shape
        k_len = key.shape[1]
        H = NUM_HEADS
        dk = D // H
        q = (query @ Wq.T).reshape(B, q_len, H, dk).transpose(0, 2, 1, 3)
        k = (key @ Wk.T).reshape(B, k_len, H, dk).transpose(0, 2, 1, 3)
        v = (value @ Wv.T).reshape(B, k_len, H, dk).transpose(0, 2, 1, 3)
        scores = jnp.einsum('bhqd,bhkd->bhqk', q, k) / jnp.sqrt(jnp.float32(dk))
        if is_causal:
            causal = jnp.triu(jnp.ones((q_len, k_len), dtype=bool), k=1)
            scores = jnp.where(causal, NEG_INF, scores)
        scores = jnp.where(attention_mask[:, None, :, :], NEG_INF, scores)
        attn = jax.nn.softmax(scores, axis=-1)
        attn = jnp.where(jnp.isnan(attn), 0.0, attn)
        out = jnp.einsum('bhqk,bhkd->bhqd', attn, v)
        out = out.transpose(0, 2, 1, 3).reshape(B, q_len, D)
        return out @ Wout.T + b_out

    def _L0_ffn_ref(x, We, be, Wg, bg):
        import jax, jax.numpy as jnp
        import numpy as np
        D_MODEL = 512
        NUM_EXPERTS = 8
        TOP_K = 2
        B, S, D = x.shape
        xf = x.reshape(-1, D)
        gate_logits = xf @ Wg.T + bg
        topk_vals, topk_idx = jax.lax.top_k(gate_logits, TOP_K)
        gate_w = jax.nn.softmax(topk_vals, axis=-1)
        all_out = jnp.einsum('nd,ehd->neh', xf, We) + be
        sel = jnp.take_along_axis(all_out, topk_idx[:, :, None], axis=1)
        out = jnp.sum(sel * gate_w[:, :, None], axis=1)
        return out.reshape(B, S, D)
    x = _layernorm(x + _L0_attn_ref(x, L0_attn_Wq, L0_attn_bq, L0_attn_Wk, L0_attn_bk, L0_attn_Wv, L0_attn_bv, L0_attn_Wo, L0_attn_bo, L0_attn_prior_lambda), axis=-1)
    x = _layernorm(x + _L0_xattn_ref(x, ctx_1024, ctx_1024, mask_BxSxS2_bf0, L0_xattn_Wq, L0_xattn_Wk, L0_xattn_Wv, L0_xattn_Wout, L0_xattn_b_out, 1), axis=-1)
    x = _layernorm(x + _L0_ffn_ref(x, L0_ffn_We, L0_ffn_be, L0_ffn_Wg, L0_ffn_bg), axis=-1)
    return x

_drawn_inputs = setup_inputs


def setup_inputs(seed=0):
    import zlib

    import numpy as np

    out = dict(_drawn_inputs(seed))
    spreads = {'L0_xattn_b_out': (0.0, 0.1)}
    factors = {'L0_attn_bq': 3.749, 'L0_attn_bk': 8.0, 'L0_ffn_be': 3.354}
    for name, (base, spread) in spreads.items():
        noise = np.random.default_rng([zlib.crc32(name.encode()), seed]).standard_normal(out[name].shape)
        drawn = base * np.exp(spread * noise) if base else spread * noise
        out[name] = jnp.asarray(drawn.astype(out[name].dtype))
    for name, factor in factors.items():
        out[name] = (out[name] * factor).astype(out[name].dtype)
    return out
```

```python
from contextlib import ExitStack

import concourse.bass as bass
from concourse import mybir

F32 = mybir.dt.float32
F32R = mybir.dt.float32r
I32 = mybir.dt.int32
U32 = mybir.dt.uint32
U8 = mybir.dt.uint8
ALU = mybir.AluOpType
ACT = mybir.ActivationFunctionType

B, S, D = 8, 224, 512
H, HD = 16, 32
NE, TOP = 8, 8
P = 128
KC = D // P
HC = P // HD
T = 112
NT = S // T
STEPS = 2 * B
TOKENS = B * S
MT = TOKENS // P
GT = MT // 2
ROOT = float(HD) ** 0.5
SCALE = 1.0 / ROOT
EPS = 1e-5
MASKED = -1.0e30
LOWEST = -3.0e38
RSQRT_MAGIC = float(0x5F3759DF)

LT, LC, LV = 3, 4, 5
END = H + LV
FILL_FROM = 2
PER_SLOT = 8
EVACUATE = {0: 5, 1: 8, 2: 14, 3: 15}
P_RING, W_RING = 4, 4
STACK_DMAS = 12
LN_OPS = 15

SELF_SLOT = {"k": 1, "q": 0, "v": 2, "o": 3}
CROSS_SLOT = {"k": 4, "q": 0, "v": 5, "o": 1}
EXPERT_SLOT = (2, 3)


def weight_jobs():
    jobs = []
    for m, slot, eng in (("self_k", 1, "dve"), ("self_q", 0, "dve"), ("self_v", 2, "dve"), ("self_o", 3, "dve"),
                         ("cross_k", 4, "pool"), ("cross_v", 5, "pool"), ("cross_q", 0, "dve"),
                         ("cross_o", 1, "pool"), ("e0", 2, "pool"), ("e1", 3, "pool")):
        jobs += [(m, c, slot, eng) for c in range(KC)]
    return jobs


JOBS = weight_jobs()
JOBS_AT = {}
for _c in range(8):
    JOBS_AT[(0, 2 + _c)] = [16 + _c]
for _c in range(4):
    JOBS_AT.setdefault((B - 1, _c // 2), []).append(24 + _c)
    JOBS_AT[(B - 1, 8 + _c)] = [28 + _c]
for _c in range(8):
    JOBS_AT[(STEPS - 1, _c)] = [32 + _c]


def lo_count(job, eng):
    return sum(JOBS[m][3] == eng for m in range(job + 1))


def decoder_layer(nc, a, out):
    with ExitStack() as ctx:
        def sb(name, shape, dt=F32, stack=ctx):
            return stack.enter_context(nc.sbuf_tensor(name, shape, dt))

        def sem(name):
            return ctx.enter_context(nc.semaphore(name))

        x1_dram = nc.dram_tensor("x1_rows", (B, S, D), F32).ap()
        x2_dram = nc.dram_tensor("x2_rows", (B, S, D), F32).ap()

        w_raw = sb("w_raw", [P, W_RING, D])
        weights = {s: sb(f"weights{s}", [P, 2, KC, D], F32R) for s in EXPERT_SLOT}
        ident = sb("ident", [P, P])
        qkv_bias = sb("qkv_bias", [P, 3, KC])
        prior = sb("prior", [T, NT, S])
        lam = sb("lam", [T, 1])
        mask_u8 = sb("mask_u8", [T, NT, S], U8)
        mask_bias = sb("mask_bias", [T, NT, S])
        out_bias = sb("out_bias", [T, 2, D])
        residual = sb("residual", [T, NT, D])
        rows = sb("rows", [T, NT, D])
        stats = sb("stats", [T, NT, 6])
        mean_var = sb("mean_var", [T, NT, 2])
        var_eps = sb("var_eps", [T, NT])
        rstd = sb("rstd", [T, NT])
        newton = sb("newton", [T, NT])
        neg_mean_rstd = sb("neg_mean_rstd", [T, NT])
        row_max = sb("row_max", [T, P_RING, NT])
        neg_max = sb("neg_max", [T, P_RING, NT])
        row_sum = sb("row_sum", [T, P_RING, NT])
        recip = sb("recip", [T, P_RING, NT])
        gate_raw = sb("gate_raw", [P, KC, NE])
        gate_w = sb("gate_w", [P, 2, KC, NE], F32R)
        gate_bias = sb("gate_bias", [P, NE])
        iota = sb("iota", [P, NE])

        attn = ExitStack()
        for s in (4, 5, 0, 1):
            weights[s] = sb(f"weights{s}", [P, 2, KC, D], F32R, attn)
        stacks = [sb(f"stack{w}", [3 * HD, HC, 2, 2 * S], F32R, attn) for w in range(2)]
        src_x = sb("src_x", [P, 2, KC, S], F32R, attn)
        src_c = sb("src_c", [P, 2, KC, S], F32R, attn)
        qk = sb("qk", [P, 4, 2 * S], F32R, attn)
        attended = sb("attended", [P, 2, KC, S], F32R, attn)
        values = sb("values", [T, NT, D], F32, attn)
        nat_x = sb("nat_x", [T, NT, D], F32, attn)
        nat_c = sb("nat_c", [T, NT, D], F32, attn)
        probs = sb("probs", [T, P_RING, NT, S], F32, attn)
        probs_t = sb("probs_t", [T, 2, NT * S], F32, attn)
        attn.close()

        moe = ctx.enter_context(ExitStack())
        acc = sb("acc", [P, MT, D], F32, moe)
        x2t = sb("x2t", [P, 2, KC, TOKENS], F32R, moe)
        be_raw = sb("be_raw", [3 * NE, D], F32, moe)
        be_lo = sb("be_lo", [3 * NE, D], F32R, moe)
        be_stack = sb("be_stack", [3 * NE, D], F32R, moe)
        gates_t = sb("gates_t", [3 * NE, TOKENS], F32R, moe)
        logits = sb("logits", [P, MT, NE], F32, moe)
        top = sb("top", [P, MT, TOP], F32, moe)
        top_at = sb("top_at", [P, MT, TOP], U32, moe)
        top_f = sb("top_f", [P, MT, 2], F32, moe)
        pair_w = sb("pair_w", [P, 4, MT], F32, moe)
        one_hot = sb("one_hot", [P, 2, MT, NE], F32, moe)
        gates = sb("gates", [P, MT, NE], F32, moe)
        gate_hl = sb("gate_hl", [P, MT, 3 * NE], F32R, moe)
        m_stats = sb("m_stats", [P, MT, 6], F32, moe)
        m_mean_var = sb("m_mean_var", [P, MT, 2], F32, moe)
        m_var = sb("m_var", [P, MT], F32, moe)
        m_rstd = sb("m_rstd", [P, MT], F32, moe)
        m_newton = sb("m_newton", [P, MT], F32, moe)
        m_shift = sb("m_shift", [P, MT], F32, moe)

        def bank(name):
            return ctx.enter_context(nc.psum_tensor(name, [P, 512], F32))

        score_bank = [bank(f"score_bank{n}") for n in range(2)]
        turn_bank = [bank(f"turn_bank{n}") for n in range(2)]
        value_bank = [bank(f"value_bank{n}") for n in range(2)]
        proj_bank = [bank(f"proj_bank{n}") for n in range(2)]
        product_bank = score_bank + value_bank

        ident_in = sem("ident_in")
        consts_in = sem("consts_in")
        gate_in = sem("gate_in")
        raw_in = [sem(f"raw_in{r}") for r in range(W_RING)]
        w_hi = sem("w_hi")
        w_lo = {"dve": sem("w_lo_dve"), "pool": sem("w_lo_pool")}
        x_in, c_in, mask_in, residual_in = sem("x_in"), sem("c_in"), sem("mask_in"), sem("residual_in")
        x_turned, x_hi, x_lo = sem("x_turned"), sem("x_hi"), sem("x_lo")
        c_turned, c_hi, c_lo = sem("c_turned"), sem("c_hi"), sem("c_lo")
        qk_full, qk_hi, qk_lo = sem("qk_full"), sem("qk_hi"), sem("qk_lo")
        stacked = [sem("stacked0"), sem("stacked1")]
        v_full, v_copied = sem("v_full"), sem("v_copied")
        prior_ready, bias_scaled, bias_ready = sem("prior_ready"), sem("bias_scaled"), sem("bias_ready")
        scored, biased, shift_ready, exp_done = sem("scored"), sem("biased"), sem("shift_ready"), sem("exp_done")
        sum_kept, recip_ready, normed = sem("sum_kept"), sem("recip_ready"), sem("normed")
        turned, copied_dve, copied_act, pv_done = sem("turned"), sem("copied_dve"), sem("copied_act"), sem("pv_done")
        att_hi, att_lo = sem("att_hi"), sem("att_lo")
        o_full, residual_ready, rows_added = sem("o_full"), sem("residual_ready"), sem("rows_added")
        ln_step, rows_normed, rows_stored = sem("ln_step"), sem("rows_normed"), sem("rows_stored")
        acc_in = [sem(f"acc_in{n}") for n in range(3)]
        be_in, be_step, be_stacked = sem("be_in"), sem("be_step"), sem("be_stacked")
        m_turned, m_hi, m_lo = sem("m_turned"), sem("m_hi"), sem("m_lo")
        gate_hi, gate_lo = sem("gate_hi"), sem("gate_lo")
        logits_full, gate_step, pair_diff, pair_exp = sem("logits_full"), sem("gate_step"), sem("pair_diff"), sem("pair_exp")
        gates_done, gates_turned, gates_copied = sem("gates_done"), sem("gates_turned"), sem("gates_copied")
        product_full, combined = sem("product_full"), sem("combined")
        bias_full, bias_added = sem("bias_full"), sem("bias_added")
        m_measured, m_ln, m_normed, out_stored = sem("m_measured"), sem("m_ln"), sem("m_normed"), sem("out_stored")

        def head(i, n):
            return i * H + n + 1

        def copies(i, n):
            if n < 0:
                i, n = i - 1, n + H
            if n % 4 == 3:
                return copied_act, i * (H // 4) + n // 4 + 1
            return copied_dve, i * (H - H // 4) + n - n // 4 + 1

        def wait_alone(eng, semaphore, value):
            if not isinstance(value, int):
                value = eng.snap(eng.to_reg(value))
            eng.wait_ge(ident_in, 16)
            eng.wait_ge(semaphore, value)

        def cross(kind):
            return kind == "cross"

        def key_tiles(kind, qt):
            return qt + 1 if cross(kind) else NT

        def turned_at(kind, qt, kt):
            if cross(kind) and kt == 1:
                return S
            return kt * S + qt * T

        def turned_cols(kind):
            return S + T if cross(kind) else NT * S

        def slots_of(kind):
            return CROSS_SLOT if cross(kind) else SELF_SLOT

        def sources(kind):
            return (src_x, src_c) if cross(kind) else (src_x, src_x)

        def projection_bias(kind, what, c):
            return qkv_bias[:, {"q": 0, "k": 1, "v": 2}[what], c:c + 1]

        FILLS = (("k", 0), ("q", 0), ("k", 1), ("q", 1))
        PLANE = {"q": 0, "k": 2}

        def three_passes(ps, stationary, moving):
            steps = [(sl, ml, c) for c in range(KC) for sl, ml in ((0, 0), (0, 1), (1, 0))]
            return [(ps, stationary(sl, c), moving(ml, c), n == 0, n == len(steps) - 1)
                    for n, (sl, ml, c) in enumerate(steps)]

        def run(matmuls):
            last = None
            for ps, lhs, rhs, first, end in matmuls:
                last = nc.tensor.matmul(ps, lhs, rhs, start=first, stop=end)
            return last

        def projection(kind, f):
            what, unit = FILLS[f]
            w = weights[slots_of(kind)[what]]
            src = sources(kind)[0 if what == "q" else 1]
            found = []
            for cc in range(2):
                o = P * (2 * unit + cc)
                found += three_passes(proj_bank[f % 2][:, cc * S:cc * S + S],
                                      lambda hl, c: w[:, hl, c, o:o + P], lambda hl, c: src[:, hl, c, :])
            return found

        def pe_turn_source(pe, s, kind, f, is_context):
            nat, done = (nat_c, c_turned) if is_context else (nat_x, x_turned)
            for cc in range(2):
                for t in range(NT):
                    last = nc.tensor.transpose(proj_bank[f % 2][:, cc * S + t * T:cc * S + t * T + T],
                                               nat[:, t, (2 * f + cc) * P:(2 * f + cc + 1) * P], ident[0:T, 0:T])
            last.then_inc(done, 1)

        def pe_turn_sources(pe, s, kind):
            if isinstance(s, int) and s == 1:
                pe.wait_ge(v_copied, 2)
            if cross(kind):
                pe.wait_ge(c_in, (s - B) * 16 + 16)
                for f in range(2):
                    pe.wait_ge(rows_added, (s - 2) * 2 + f + 1)
                    pe_turn_source(pe, s, kind, f, True)
            pe.wait_ge(x_in, s * 16 + 16)
            for f in range(2):
                if cross(kind):
                    pe.wait_ge(c_lo, (s - B) * 2 + f + 1)
                elif not isinstance(s, int) or s > 1:
                    pe.wait_ge(rows_added, (s - 2) * 2 + f + 1)
                pe_turn_source(pe, s, kind, f, False)

        def pe_projection_part(pe, s, kind, lo, hi):
            for m in range(lo, hi):
                f, at = divmod(m, 24)
                if at == 0:
                    what = FILLS[f][0]
                    if f < 2:
                        if what == "k" and cross(kind):
                            pe.wait_ge(c_lo, (s - B) * 2 + 2)
                        else:
                            pe.wait_ge(x_lo, s * 2 + 2)
                        pe_wait_weights(pe, kind, what, s)
                    if f < 2:
                        pe.wait_ge(x_lo, s * 2 + f + 1)
                    else:
                        pe.wait_ge(qk_lo, s * 4 + f - 1)
                last = run(projection(kind, f)[at:at + 1])
                if at == 23:
                    last.then_inc(qk_full, 1)

        def pe_wait_weights(pe, kind, what, s):
            first = {("self", "k"): 0, ("self", "q"): 0, ("self", "v"): 0, ("self", "o"): 0,
                     ("cross", "k"): B, ("cross", "q"): B, ("cross", "v"): B, ("cross", "o"): B}[(kind, what)]
            if isinstance(s, int) and s == first:
                job = max(m for m, j in enumerate(JOBS) if j[0] == f"{kind}_{what}")
                pe.wait_ge(w_lo[JOBS[job][3]], lo_count(job, JOBS[job][3]))

        def value_fill(kind, t):
            w = weights[slots_of(kind)["v"]]
            src = sources(kind)[1]
            return three_passes(proj_bank[t][0:T, :], lambda hl, c: src[:, hl, c, t * T:t * T + T],
                                lambda hl, c: w[:, hl, c, :])

        def pe_value_part(pe, s, kind, lo, hi):
            for m in range(lo, hi):
                t, at = divmod(m, 12)
                if at == 0:
                    if t == 0:
                        pe_wait_weights(pe, kind, "v", s)
                    pe.wait_ge(qk_lo, s * 4 + 3 + t)
                last = run(value_fill(kind, t)[at:at + 1])
                if at == 11:
                    last.then_inc(v_full, 1)

        def pe_scores(pe, i, kind, n):
            unit, slot = divmod(n, 8)
            c, j = divmod(slot, HC)
            st, o = stacks[unit], c * S
            if slot == 0:
                pe.wait_ge(stacked[unit], i * 16 * STACK_DMAS + 16 * STACK_DMAS)
            if not (isinstance(i, int) and i == 0 and n < 2):
                pe.wait_ge(biased, head(i, n - 2))
            for qt in range(NT):
                w = key_tiles(kind, qt) * T
                last = nc.tensor.matmul(score_bank[n % 2][0:T, qt * S:qt * S + w],
                                        st[:, j, 0, o + qt * T:o + qt * T + T], st[:, j, 1, o:o + w],
                                        start=True, stop=True)
            last.then_inc(scored, 1)

        def pe_turn_probs(pe, i, kind, n):
            pe.wait_ge(normed, head(i, n))
            if not (isinstance(i, int) and i == 0 and n < 2):
                pe.wait_ge(*copies(i, n - 2))
            for qt in range(NT):
                for kt in range(key_tiles(kind, qt)):
                    o = turned_at(kind, qt, kt)
                    last = nc.tensor.transpose(turn_bank[n % 2][0:T, o:o + T],
                                               probs[:, n % P_RING, qt, kt * T:kt * T + T], ident[0:T, 0:T])
            last.then_inc(turned, 1)

        def pe_values(pe, i, kind, n):
            unit, slot = divmod(n, 8)
            c, j = divmod(slot, HC)
            if slot == 0 and not (isinstance(i, int) and i == 0):
                pe.wait_ge(att_lo, i * 2 + unit - 1)
            if n == 0:
                pe.wait_ge(v_copied, i * 2 + 2)
            pe.wait_ge(*copies(i, n))
            for kt in range(NT):
                q0 = T if cross(kind) and kt == 1 else 0
                o = turned_at(kind, q0 // T, kt)
                last = nc.tensor.matmul(value_bank[unit][HD * j:HD * j + HD, c * S + q0:c * S + S],
                                        values[:, kt, n * HD:n * HD + HD], probs_t[:, n % 2, o:o + S - q0],
                                        start=kt == 0, stop=kt == NT - 1)
            last.then_inc(pv_done, 1)

        def pe_output(pe, i, kind):
            w = weights[slots_of(kind)["o"]]
            fills = [three_passes(proj_bank[t][0:T, :], lambda hl, c, t=t: attended[:, hl, c, t * T:t * T + T],
                                  lambda hl, c: w[:, hl, c, :]) for t in range(NT)]
            pe_wait_weights(pe, kind, "o", i)
            pe.wait_ge(att_lo, i * 2 + 1)
            for t in range(NT):
                if isinstance(i, int) and i == STEPS - 1:
                    pe.wait_ge(rows_added, i * 2)
                else:
                    pe.wait_ge(v_copied, i * 2 + 3 + t)
                run(fills[t][0:6])
            pe.wait_ge(att_lo, i * 2 + 2)
            for t in range(NT):
                run(fills[t][6:12]).then_inc(o_full, 1)

        def pe_step(pe, i, kind, nxt):
            for n in range(END):
                if n < H:
                    pe_scores(pe, i, kind, n)
                if nxt:
                    if n == 0:
                        pe_turn_sources(pe, i + 1, nxt)
                    lo = (n - FILL_FROM) * PER_SLOT
                    if 0 <= lo < 96:
                        pe_projection_part(pe, i + 1, nxt, lo, min(lo + PER_SLOT, 96))
                    if H <= n < H + 3:
                        pe_value_part(pe, i + 1, nxt, (n - H) * 8, (n - H) * 8 + 8)
                if LT <= n < H + LT:
                    pe_turn_probs(pe, i, kind, n - LT)
                if LV <= n:
                    pe_values(pe, i, kind, n - LV)
            pe_output(pe, i, kind)

        def act_split(act, dst_hi, ps, bias):
            if bias is None:
                return nc.scalar.activation(dst_hi, ps, ACT.Copy)
            return nc.scalar.activation(dst_hi, ps, ACT.Identity, bias=bias)

        def dve_split(dst_lo, ps, bias, src_hi):
            if bias is None:
                return nc.vector.tensor_tensor(dst_lo, ps, src_hi, ALU.subtract)
            return nc.vector.scalar_tensor_tensor(dst_lo, ps, bias, src_hi, ALU.add, ALU.subtract)

        def source_split(eng, s, kind, f, is_context, is_act):
            dst, hi_done, lo_done, full = ((src_c, c_hi, c_lo, c_turned) if is_context
                                           else (src_x, x_hi, x_lo, x_turned))
            j = s - B if is_context else s
            ps = proj_bank[f % 2][:, 0:2 * S].rearrange("p (c n) -> p c n", c=2)
            if is_act:
                eng.wait_ge(full, j * 2 + f + 1)
                act_split(eng, dst[:, 0, 2 * f:2 * f + 2, :], ps, None).then_inc(hi_done, 1)
            else:
                eng.wait_ge(hi_done, j * 2 + f + 1)
                dve_split(dst[:, 1, 2 * f:2 * f + 2, :], ps, None, dst[:, 0, 2 * f:2 * f + 2, :]).then_inc(lo_done, 1)

        def sources_split(eng, s, kind, is_act):
            if cross(kind):
                for f in range(2):
                    source_split(eng, s, kind, f, True, is_act)
            for f in range(2):
                source_split(eng, s, kind, f, False, is_act)

        def projection_split(eng, s, kind, f, is_act):
            what, unit = FILLS[f]
            plane = PLANE[what]
            ps = proj_bank[f % 2]
            if is_act:
                eng.wait_ge(qk_full, s * 4 + f + 1)
                if not (isinstance(s, int) and s == 0 and unit == 0):
                    eng.wait_ge(stacked[1 - unit], s * 16 * STACK_DMAS + (16 * STACK_DMAS if unit else 0))
            else:
                eng.wait_ge(qk_hi, s * 4 + f + 1)
            parts = [(slice(0, 2 * S), None)] if cross(kind) else [
                (slice(cc * S, cc * S + S), projection_bias(kind, what, 2 * unit + cc)) for cc in range(2)]
            for sl, bias in parts:
                if is_act:
                    last = act_split(eng, qk[:, plane, sl], ps[:, sl], bias)
                else:
                    last = dve_split(qk[:, plane + 1, sl], ps[:, sl], bias, qk[:, plane, sl])
            last.then_inc(qk_hi if is_act else qk_lo, 1)

        def attended_split(eng, i, kind, unit, is_act):
            ps = value_bank[unit][:, 0:2 * S].rearrange("p (c n) -> p c n", c=2)
            if is_act:
                eng.wait_ge(pv_done, head(i, 8 * unit + 7))
                if unit == 0 and not (isinstance(i, int) and i == 0):
                    eng.wait_ge(o_full, i * 2)
            else:
                eng.wait_ge(att_hi, i * 2 + unit + 1)
            parts = [(slice(0, 2), None)] if cross(kind) else [
                (slice(cc, cc + 1), projection_bias(kind, "v", 2 * unit + cc)) for cc in range(2)]
            for sl, bias in parts:
                at = slice(2 * unit + sl.start, 2 * unit + sl.stop)
                if is_act:
                    last = act_split(eng, attended[:, 0, at, :], ps[:, sl, :], bias)
                else:
                    last = dve_split(attended[:, 1, at, :], ps[:, sl, :], bias, attended[:, 0, at, :])
            last.then_inc(att_hi if is_act else att_lo, 1)

        def act_weight_hi(act, m):
            name, c, slot, _ = JOBS[m]
            act.wait_ge(raw_in[m % W_RING], 16 * (m // W_RING + 1))
            if c == 0:
                if name in ("cross_q", "cross_o"):
                    act.wait_ge(qk_full, 4 * B)
                if name == "e0":
                    act.wait_ge(v_full, 2 * B)
                if name == "e1":
                    act.wait_ge(o_full, 2 * B)
            nc.scalar.activation(weights[slot][:, 0, c, :], w_raw[:, m % W_RING, :], ACT.Copy).then_inc(w_hi, 1)

        def weight_lo(eng, m, which):
            _, c, slot, _ = JOBS[m]
            eng.wait_ge(w_hi, m + 1)
            e = nc.vector if which == "dve" else nc.gpsimd
            e.tensor_tensor(weights[slot][:, 1, c, :], w_raw[:, m % W_RING, :], weights[slot][:, 0, c, :],
                            ALU.subtract).then_inc(w_lo[which], 1)

        def act_exp(act, i, kind, n):
            r = n % P_RING
            act.wait_ge(shift_ready, head(i, n))
            for qt in range(NT):
                w = key_tiles(kind, qt) * T
                last = nc.scalar.activation(probs[:, r, qt, 0:w], probs[:, r, qt, 0:w], ACT.Exp,
                                            bias=neg_max[:, r, qt:qt + 1], scale=SCALE,
                                            accum_out=row_sum[:, r, qt:qt + 1])
            last.then_inc(exp_done, 1)

        def copy_turned(eng, i, kind, n, is_act):
            eng.wait_ge(turned, head(i, n))
            if not (isinstance(i, int) and i == 0 and n < 2):
                eng.wait_ge(pv_done, head(i, n - 2))
            w = turned_cols(kind)
            if is_act:
                nc.scalar.activation(probs_t[:, n % 2, 0:w], turn_bank[n % 2][0:T, 0:w], ACT.Copy).then_inc(copied_act, 1)
            else:
                nc.vector.tensor_copy(probs_t[:, n % 2, 0:w], turn_bank[n % 2][0:T, 0:w]).then_inc(copied_dve, 1)

        def act_values(act, s):
            for t in range(NT):
                act.wait_ge(v_full, s * 2 + t + 1)
                if t == 0 and not (isinstance(s, int) and s == 0):
                    act.wait_ge(pv_done, s * H)
                nc.scalar.activation(values[:, t, :], proj_bank[t][0:T, :], ACT.Copy).then_inc(v_copied, 1)

        def act_norm_rows(act, i):
            act.wait_ge(ln_step, i * LN_OPS + LN_OPS)
            for t in range(NT):
                last = nc.scalar.activation(rows[:, t, :], rows[:, t, :], ACT.Identity,
                                            bias=neg_mean_rstd[:, t:t + 1], scale=rstd[:, t:t + 1])
            last.then_inc(rows_normed, 1)

        def act_step(act, i, kind, nxt, finish):
            for n in range(END):
                for m in JOBS_AT.get((i, n), []) if isinstance(i, int) else []:
                    act_weight_hi(act, m)
                if n < H:
                    act_exp(act, i, kind, n)
                if nxt:
                    if n == 0:
                        sources_split(act, i + 1, nxt, True)
                    for f in range(4):
                        if EVACUATE[f] == n:
                            projection_split(act, i + 1, nxt, f, True)
                if LC <= n < H + LC and (n - LC) % 4 == 3:
                    copy_turned(act, i, kind, n - LC, True)
                if finish and n == 7:
                    act_norm_rows(act, i - 1)
                if n == 13:
                    attended_split(act, i, kind, 0, True)
            if nxt:
                act_values(act, i + 1)
            attended_split(act, i, kind, 1, True)

        def dve_bias_max(dve, i, kind, n):
            r = n % P_RING
            if n == 0 and cross(kind):
                dve.wait_ge(bias_ready, i - B + 1)
            if not (isinstance(i, int) and i == 0 and n < P_RING):
                dve.wait_ge(turned, head(i, n - P_RING))
            wait_alone(dve, scored, head(i, n))
            bias = mask_bias if cross(kind) else prior
            for qt in range(NT):
                w = key_tiles(kind, qt) * T
                last = nc.vector.tensor_tensor_reduce(probs[:, r, qt, 0:w], score_bank[n % 2][0:T, qt * S:qt * S + w],
                                                      bias[:, qt, 0:w], 1.0, LOWEST, ALU.add, ALU.max,
                                                      row_max[:, r, qt:qt + 1])
            last.then_inc(biased, 1)
            dve.wait_ge(biased, head(i, n))
            nc.vector.tensor_scalar(neg_max[:, r, :], row_max[:, r, :], -SCALE, -MASKED * SCALE * 1e-3,
                                    ALU.mult, ALU.min).then_inc(shift_ready, 1)

        def dve_keep_sum(dve, i, n):
            r = n % P_RING
            dve.wait_ge(exp_done, head(i, n))
            nc.vector.tensor_scalar(row_sum[:, r, :], row_sum[:, r, :], 0.5, None, ALU.max).then_inc(sum_kept, 1)

        def dve_recip(dve, i, n):
            r = n % P_RING
            dve.wait_ge(sum_kept, head(i, n))
            nc.vector.reciprocal(recip[:, r, :], row_sum[:, r, :]).then_inc(recip_ready, 1)

        def dve_add_rows(dve, i):
            dve.wait_ge(residual_ready, i + 1)
            if not (isinstance(i, int) and i == 0):
                dve.wait_ge(rows_stored, i * 16)
            for t in range(NT):
                dve.wait_ge(o_full, i * 2 + t + 1)
                nc.vector.tensor_tensor(rows[:, t, :], proj_bank[t][0:T, :], residual[:, t, :],
                                        ALU.add).then_inc(rows_added, 1)

        def rsqrt_ops(var, mean, r, tmp, shift):
            v = nc.vector
            ops = [lambda: v.tensor_scalar(r.bitcast(I32), var.bitcast(I32), 1, None, ALU.logical_shift_right),
                   lambda: v.tensor_scalar(r.bitcast(I32), r.bitcast(I32), -1.0, RSQRT_MAGIC, ALU.mult, ALU.add)]
            for _ in range(3):
                ops += [lambda: v.tensor_tensor(tmp, r, r, ALU.mult),
                        lambda: v.scalar_tensor_tensor(tmp, tmp, -0.5, var, ALU.mult, ALU.mult),
                        lambda: v.scalar_tensor_tensor(r, tmp, 1.5, r, ALU.add, ALU.mult)]
            return ops + [lambda: v.scalar_tensor_tensor(shift, mean, -1.0, r, ALU.mult, ALU.mult)]

        def dve_ln_op(dve, i, k):
            if k == 0:
                dve.wait_ge(rows_added, i * 2 + 2)
                nc.vector.bn_stats(stats[:, 0, :], rows[:, 0, :])
                last = nc.vector.bn_stats(stats[:, 1, :], rows[:, 1, :])
            elif k == 1:
                wait_alone(dve, ln_step, i * LN_OPS + k)
                nc.vector.bn_aggr(mean_var[:, 0, :], stats[:, 0, :])
                last = nc.vector.bn_aggr(mean_var[:, 1, :], stats[:, 1, :])
            elif k == 2:
                dve.wait_ge(ln_step, i * LN_OPS + k)
                last = nc.vector.tensor_scalar(var_eps[:, :], mean_var[:, :, 1], EPS, None, ALU.add)
            else:
                dve.wait_ge(ln_step, i * LN_OPS + k)
                last = rsqrt_ops(var_eps[:, :], mean_var[:, :, 0], rstd[:, :], newton[:, :],
                                 neg_mean_rstd[:, :])[k - 3]()
            last.then_inc(ln_step, 1)

        def dve_step(dve, i, kind, nxt, finish):
            for n in range(END):
                if n < H:
                    dve_bias_max(dve, i, kind, n)
                for m in JOBS_AT.get((i, n), []) if isinstance(i, int) else []:
                    if JOBS[m][3] == "dve":
                        weight_lo(dve, m, "dve")
                if 1 <= n <= H:
                    dve_keep_sum(dve, i, n - 1)
                if LC <= n < H + LC and (n - LC) % 4 != 3:
                    copy_turned(dve, i, kind, n - LC, False)
                if 1 <= n <= H:
                    dve_recip(dve, i, n - 1)
                if finish and n == 0:
                    dve_add_rows(dve, i - 1)
                if nxt:
                    if n == 0:
                        sources_split(dve, i + 1, nxt, False)
                    for f in range(4):
                        if EVACUATE[f] == n:
                            projection_split(dve, i + 1, nxt, f, False)
                if finish and 1 <= n <= 5:
                    for k in range((n - 1) * 3, n * 3):
                        dve_ln_op(dve, i - 1, k)
                if n == 13:
                    attended_split(dve, i, kind, 0, False)
            attended_split(dve, i, kind, 1, False)

        def pool_norm(pool, i, kind, n):
            r = n % P_RING
            pool.wait_ge(recip_ready, head(i, n))
            if cross(kind):
                for qt in range(NT):
                    w = key_tiles(kind, qt) * T
                    last = nc.gpsimd.tensor_tensor(probs[:, r, qt, 0:w], probs[:, r, qt, 0:w],
                                                   recip[:, r, qt:qt + 1].broadcast_to((T, w)), ALU.mult)
            else:
                last = nc.gpsimd.tensor_tensor(
                    probs[:, r], probs[:, r],
                    recip[:, r, :].rearrange("p (a b) -> p a b", b=1).broadcast_to((T, NT, S)), ALU.mult)
            last.then_inc(normed, 1)

        def pool_residual(pool, i, kind):
            pool.wait_ge(residual_in, i * 16 + 16)
            b = out_bias[:, 1 if cross(kind) else 0, :].rearrange("p (a b) -> p a b", a=1).broadcast_to((T, NT, D))
            nc.gpsimd.tensor_tensor(residual[:, :, :], residual[:, :, :], b, ALU.add).then_inc(residual_ready, 1)

        def pool_mask(pool, s):
            pool.wait_ge(mask_in, (s - B) * 16 + 16)
            wait_alone(pool, biased, s * H)
            nc.gpsimd.tensor_scalar(mask_bias[:, :, :], mask_u8[:, :, :], MASKED, None, ALU.mult).then_inc(bias_scaled, 1)
            wait_alone(pool, bias_scaled, s - B + 1)
            nc.gpsimd.affine_select(out=mask_bias[:, :, :], in_=mask_bias[:, :, :], compare_op=ALU.is_ge,
                                    fill=MASKED, base=0, pattern=[[T, NT], [-1, S]],
                                    channel_multiplier=1).then_inc(bias_ready, 1)

        def pool_step(pool, i, kind, nxt):
            for n in range(H):
                pool_norm(pool, i, kind, n)
                for m in JOBS_AT.get((i, n), []) if isinstance(i, int) else []:
                    if JOBS[m][3] == "pool":
                        weight_lo(pool, m, "pool")
                if n == 9:
                    pool_residual(pool, i, kind)
            if nxt and cross(nxt):
                pool_mask(pool, i + 1)

        def load_raw(sp, m, src, waited=True):
            if waited and m >= W_RING:
                eng = JOBS[m - W_RING][3]
                sp.wait_ge(w_lo[eng], lo_count(m - W_RING, eng))
            sp.dma_start(w_raw[:, m % W_RING, :], src).then_inc(raw_in[m % W_RING], 16)

        def load_job(sp, m):
            name, c, _, _ = JOBS[m]
            load_raw(sp, m, a["experts"][int(name[1:]), :, c, :] if name[0] == "e" else a[name][:, c, :])

        def batch_rows(dram, b):
            return dram[b].rearrange("(t p) d -> p t d", p=T)

        def load_sources(sp, s, kind, first):
            if not first:
                sp.wait_ge(x_turned, s * 2)
            if cross(kind):
                sp.wait_ge(rows_stored, (s - B) * 16 + 16)
                sp.dma_start(nat_x[:, :, :], batch_rows(x1_dram, s - B)).then_inc(x_in, 16)
                if not (isinstance(s, int) and s == B):
                    sp.wait_ge(c_turned, (s - B) * 2)
                sp.dma_start(nat_c[:, :, :], a["context"][s - B, 0:S, :].rearrange("(t p) d -> p t d", p=T)).then_inc(c_in, 16)
            else:
                sp.dma_start(nat_x[:, :, :], batch_rows(a["x"], s)).then_inc(x_in, 16)

        def load_residual(sp, i, kind):
            if not (isinstance(i, int) and i == 0):
                sp.wait_ge(rows_added, i * 2)
            src = batch_rows(x1_dram, i - B) if cross(kind) else batch_rows(a["x"], i)
            sp.dma_start(residual[:, :, :], src).then_inc(residual_in, 16)

        def load_mask(sp, s):
            if not (isinstance(s, int) and s == B):
                wait_alone(sp, bias_scaled, s - B)
            sp.dma_start(mask_u8[:, :, :], a["mask"][s - B, 0:S, 0:S].rearrange("(t p) k -> p t k", p=T)).then_inc(mask_in, 16)

        def stack_unit(sp, s, unit):
            wait_alone(sp, qk_lo, s * 4 + 2 * unit + 2)
            if unit == 1 or not (isinstance(s, int) and s == 0):
                if not (isinstance(s, int) and s == 0):
                    sp.wait_ge(scored, s * H - (0 if unit else 8))
            for j in range(HC):
                for role, planes in enumerate((slice(0, 3, 2), slice(1, 3), slice(0, 4, 3))):
                    sp.dma_start(stacks[unit][HD * role:HD * role + HD, j, :, :].bitcast(F32),
                                 qk[HD * j:HD * j + HD, planes, :].bitcast(F32)).then_inc(stacked[unit], 16)

        def store_rows(sp, i, kind):
            sp.wait_ge(rows_normed, i + 1)
            dst = batch_rows(x2_dram, i - B) if cross(kind) else batch_rows(x1_dram, i)
            sp.dma_start(dst, rows[:, :, :]).then_inc(rows_stored, 16)

        def sp_step(sp, i, kind, prev, nxt, nxt2):
            stack_unit(sp, i, 1)
            if isinstance(i, int) and i == 0:
                for m in range(16, 20):
                    load_job(sp, m)
            if nxt2:
                load_sources(sp, i + 2, nxt2, False)
            load_residual(sp, i, kind)
            if nxt and cross(nxt):
                load_mask(sp, i + 1)
            if isinstance(i, int) and i == STEPS - 1:
                for m in range(36, 40):
                    load_job(sp, m)
            if prev:
                store_rows(sp, i - 1, prev)
            if isinstance(i, int) and i == 0:
                for m in range(20, 24):
                    load_job(sp, m)
            if isinstance(i, int) and i == B - 1:
                for m in range(28, 32):
                    load_job(sp, m)
            if nxt:
                stack_unit(sp, i + 1, 0)
            if isinstance(i, int) and i == 0:
                for m in range(24, 28):
                    load_job(sp, m)
            if isinstance(i, int) and i == B - 1:
                for m in range(32, 36):
                    load_job(sp, m)

        M_JOB = 40

        def m_batches(n):
            lo, hi = ((0, 7), (7, 12), (12, 14))[n]
            return lo, hi, (hi * P + S - 1) // S

        def sp_experts(sp):
            sp.wait_ge(v_full, 2 * STEPS)
            sp.wait_ge(qk_full, 4 * STEPS)
            x2_flat = x2_dram.rearrange("b s d -> (b s) d")
            for n in range(2):
                lo, hi, nb = m_batches(n)
                sp.wait_ge(rows_stored, 16 * (B + nb))
                sp.dma_start(acc[:, lo:hi, :], x2_flat[lo * P:hi * P, :].rearrange("(t p) d -> p t d", p=P)).then_inc(acc_in[n], 16)
            store_rows(sp, STEPS - 1, "cross")
            lo, hi, nb = m_batches(2)
            sp.wait_ge(rows_stored, 16 * (B + nb))
            sp.dma_start(acc[:, lo:hi, :], x2_flat[lo * P:hi * P, :].rearrange("(t p) d -> p t d", p=P)).then_inc(acc_in[2], 16)
            for r in range(3):
                sp.dma_start(be_raw[r * NE:(r + 1) * NE, :], a["expert_bias"]).then_inc(be_in, 16)
            sp.wait_ge(be_step, 3)
            sp.dma_start(be_stack[2 * NE:3 * NE, :].bitcast(F32), be_lo[0:NE, :].bitcast(F32)).then_inc(be_stacked, 16)
            with sp.Fori(0, NE // 2 - 1) as it:
                for m in range(2 * KC):
                    sp.wait_ge(w_lo["pool"], it * 2 * KC + lo_count(M_JOB - 1, "pool") - W_RING + m + 1)
                    sp.dma_start(w_raw[:, m % W_RING, :], a["experts"][it * 2 + 2 + m // KC, :, m % KC, :]).then_inc(raw_in[m % W_RING], 16)
            for g, tiles in enumerate(M_GROUPS):
                sp.wait_ge(m_normed, g + 1)
                lo, hi = tiles
                sp.dma_start(out.rearrange("b s d -> (b s) d")[lo * P:hi * P, :].rearrange("(t p) d -> p t d", p=P),
                             acc[:, lo:hi, :]).then_inc(out_stored, 16)
            sp.wait_ge(out_stored, 16 * len(M_GROUPS))

        M_GROUPS = ((0, 4), (4, 8), (8, 12), (12, 14))
        M_LN = LN_OPS - 1

        def pe_experts(pe):
            pe.wait_ge(biased, head(STEPS - 1, H - 1))
            pe.wait_ge(*copies(STEPS - 1, H - 2))
            pe.wait_ge(*copies(STEPS - 1, H - 1))
            pe.wait_ge(att_lo, 2 * STEPS)
            pe.wait_ge(rows_added, 2 * STEPS)

            def turn(t):
                if t in (0, 7, 12):
                    pe.wait_ge(acc_in[(0, 7, 12).index(t)], 16)
                if t >= 2:
                    pe.wait_ge(m_lo, t - 1)
                for c in range(KC):
                    last = nc.tensor.transpose(proj_bank[t % 2][:, c * P:c * P + P], acc[:, t, c * P:c * P + P], ident[:, :])
                last.then_inc(m_turned, 1)

            def gate(t):
                pe.wait_ge(m_lo, t + 1)
                if t == 0:
                    pe.wait_ge(gate_lo, 1)
                g = t % GT
                last = run(three_passes(turn_bank[t // GT][:, g * NE:g * NE + NE],
                                        lambda hl, c: x2t[:, hl, c, t * P:t * P + P],
                                        lambda hl, c: gate_w[:, hl, c, :]))
                if g == GT - 1:
                    last.then_inc(logits_full, 1)

            turn(0)
            for t in range(MT):
                if t + 1 < MT:
                    turn(t + 1)
                gate(t)

            def expert(q0, e, slot, weights_split):
                pe.wait_ge(w_lo["pool"], weights_split)
                for t in range(MT):
                    q = q0 + t
                    pe.wait_ge(combined, q + 1)
                    run(three_passes(product_bank[(slot * MT + t) % 4][:, :], lambda hl, c: x2t[:, hl, c, t * P:t * P + P],
                                     lambda hl, c: weights[EXPERT_SLOT[slot]][:, hl, c, :])).then_inc(product_full, 1)

            base = lo_count(M_JOB - 1, "pool") - 2 * KC
            with pe.Fori(0, NE // 2 - 1) as it:
                for s in range(2):
                    expert(it * 2 * MT + s * MT, None, s, it * 2 * KC + base + (s + 1) * KC)
            for f in range(4):
                lo, hi = 4 * f, min(4 * f + 4, MT)
                pe.wait_ge(gates_done, 2 if hi > GT else 1)
                if f >= 2:
                    pe.wait_ge(gates_copied, f - 1)
                for t in range(lo, hi):
                    last = nc.tensor.transpose(turn_bank[f % 2][0:3 * NE, (t - lo) * P:(t - lo) * P + P],
                                               gate_hl[:, t, :].bitcast(F32), ident[:, :])
                last.then_inc(gates_turned, 1)
            pe.wait_ge(gates_copied, 4)
            pe.wait_ge(be_stacked, 16)
            for t in range(MT):
                if t >= 2:
                    pe.wait_ge(bias_added, t - 1)
                nc.tensor.matmul(proj_bank[t % 2][:, :], gates_t[:, t * P:t * P + P], be_stack[:, :],
                                 start=True, stop=True).then_inc(bias_full, 1)
            for s in range(2):
                expert((NE - 2 + s) * MT, None, s, (NE // 2 - 1) * 2 * KC + base + (s + 1) * KC)

        def act_experts(act):
            act.wait_ge(o_full, 2 * STEPS)
            for t in range(MT):
                act.wait_ge(m_turned, t + 1)
                nc.scalar.activation(x2t[:, 0, :, t * P:t * P + P], proj_bank[t % 2][:, :].rearrange("p (c n) -> p c n", c=KC),
                                     ACT.Copy).then_inc(m_hi, 1)
                if t in (9, MT - 1):
                    g = 0 if t == 9 else 1
                    act.wait_ge(pair_diff, g + 1)
                    nc.scalar.activation(pair_w[:, 1, g * GT:g * GT + GT], pair_w[:, 0, g * GT:g * GT + GT],
                                         ACT.Exp).then_inc(pair_exp, 1)
            with act.Fori(0, NE // 2 - 1) as it:
                for m in range(2 * KC):
                    c, s = m % KC, m // KC
                    act.wait_ge(raw_in[m % W_RING], it * 32 + 16 * (M_JOB // W_RING + m // W_RING + 1))
                    if c == 0:
                        act.wait_ge(product_full, it * 2 * MT + (s + 1) * MT)
                    nc.scalar.activation(weights[EXPERT_SLOT[s]][:, 0, c, :], w_raw[:, m % W_RING, :], ACT.Copy).then_inc(w_hi, 1)
            for f in range(4):
                lo, hi = 4 * f, min(4 * f + 4, MT)
                act.wait_ge(gates_turned, f + 1)
                nc.scalar.activation(gates_t[:, lo * P:hi * P], turn_bank[f % 2][0:3 * NE, 0:(hi - lo) * P],
                                     ACT.Copy).then_inc(gates_copied, 1)
            for g, (lo, hi) in enumerate(M_GROUPS):
                act.wait_ge(m_ln, (g + 1) * M_LN)
                for t in range(lo, hi):
                    last = nc.scalar.activation(acc[:, t, :], acc[:, t, :], ACT.Identity,
                                                bias=m_shift[:, t:t + 1], scale=m_rstd[:, t:t + 1])
                last.then_inc(m_normed, 1)

        def pool_experts(pool):
            with pool.Fori(0, NE // 2 - 1) as it:
                for m in range(2 * KC):
                    c, s = m % KC, m // KC
                    pool.wait_ge(w_hi, it * 2 * KC + M_JOB + m + 1)
                    w = weights[EXPERT_SLOT[s]]
                    nc.gpsimd.tensor_tensor(w[:, 1, c, :], w_raw[:, m % W_RING, :], w[:, 0, c, :],
                                            ALU.subtract).then_inc(w_lo["pool"], 1)

        def dve_experts(dve):
            def split(t):
                dve.wait_ge(m_hi, t + 1)
                nc.vector.tensor_tensor(x2t[:, 1, :, t * P:t * P + P], proj_bank[t % 2][:, :].rearrange("p (c n) -> p c n", c=KC),
                                        x2t[:, 0, :, t * P:t * P + P], ALU.subtract).then_inc(m_lo, 1)

            links = [0]

            def link(instruction):
                links[0] += 1
                instruction.then_inc(gate_step, 1)
                dve.wait_ge(gate_step, links[0])

            def spread(x, n):
                return x.rearrange("p (a b) -> p a b", b=1).broadcast_to((P, GT, n))

            def gate_first(g):
                tiles = slice(g * GT, g * GT + GT)
                dve.wait_ge(logits_full, g + 1)
                link(nc.vector.tensor_tensor(
                    logits[:, tiles, :], turn_bank[g][:, 0:GT * NE].rearrange("p (t e) -> p t e", t=GT),
                    gate_bias[:, :].rearrange("p (a e) -> p a e", a=1).broadcast_to((P, GT, NE)), ALU.add))
                for t in range(g * GT, g * GT + GT):
                    last = nc.vector.max(top[:, t, :], logits[:, t, :])
                link(last)
                nc.vector.tensor_tensor(pair_w[:, 0, tiles], top[:, tiles, 1], top[:, tiles, 0],
                                        ALU.subtract).then_inc(pair_diff, 1)
                for t in range(g * GT, g * GT + GT):
                    last = nc.vector.max_index(top_at[:, t, :], top[:, t, :], logits[:, t, :])
                link(last)
                link(nc.vector.tensor_copy(top_f[:, tiles, :], top_at[:, tiles, 0:2]))

            def gate_second(g):
                tiles = slice(g * GT, g * GT + GT)
                dve.wait_ge(pair_exp, g + 1)
                link(nc.vector.tensor_scalar(pair_w[:, 3, tiles], pair_w[:, 1, tiles], 1.0, None, ALU.add))
                link(nc.vector.reciprocal(pair_w[:, 2, tiles], pair_w[:, 3, tiles]))
                link(nc.vector.tensor_tensor(pair_w[:, 3, tiles], pair_w[:, 1, tiles], pair_w[:, 2, tiles], ALU.mult))
                every = iota[:, :].rearrange("p (a e) -> p a e", a=1).broadcast_to((P, GT, NE))
                for k in range(2):
                    link(nc.vector.tensor_tensor(one_hot[:, k, tiles, :], every, spread(top_f[:, tiles, k], NE), ALU.is_equal))
                    link(nc.vector.tensor_tensor(one_hot[:, k, tiles, :], one_hot[:, k, tiles, :],
                                                 spread(pair_w[:, 2 + k, tiles], NE), ALU.mult))
                link(nc.vector.tensor_tensor(gates[:, tiles, :], one_hot[:, 0, tiles, :], one_hot[:, 1, tiles, :], ALU.add))
                nc.vector.tensor_copy(gate_hl[:, tiles, 0:NE], gates[:, tiles, :])
                link(nc.vector.tensor_copy(gate_hl[:, tiles, 2 * NE:3 * NE], gates[:, tiles, :]))
                nc.vector.tensor_tensor(gate_hl[:, tiles, NE:2 * NE], gates[:, tiles, :], gate_hl[:, tiles, 0:NE],
                                        ALU.subtract).then_inc(gates_done, 1)

            for t in range(MT):
                split(t)
                if t == 8:
                    gate_first(0)
                if t == 10:
                    gate_second(0)
            dve.wait_ge(be_in, 48)
            nc.vector.tensor_copy(be_lo[:, :], be_raw[:, :]).then_inc(be_step, 1)
            dve.wait_ge(be_step, 1)
            nc.vector.tensor_copy(be_stack[:, :], be_lo[:, :]).then_inc(be_step, 1)
            dve.wait_ge(be_step, 2)
            nc.vector.tensor_tensor(be_lo[:, :], be_raw[:, :], be_stack[:, :], ALU.subtract).then_inc(be_step, 1)
            gate_first(1)
            gate_second(1)
            dve.wait_ge(gates_done, 2)
            nc.vector.memset(pair_w[:, 0, 0:1], 0.0).then_inc(combined, 4)

            def combine(q, t, bank_at, gate_at):
                dve.wait_ge(product_full, q + 1)
                dve.wait_ge(combined, q + 4)
                return nc.vector.scalar_tensor_tensor(acc[:, t, :], product_bank[bank_at][:, :], gate_at, acc[:, t, :],
                                                      ALU.mult, ALU.add)

            with dve.Fori(0, NE // 2 - 1) as it:
                for s in range(2):
                    for t in range(MT):
                        combine(it * 2 * MT + s * MT + t, t, (s * MT + t) % 4,
                                gates[:, t, bass.ds(it * 2 + s, 1)]).then_inc(combined, 1)
            for t in range(MT):
                dve.wait_ge(bias_full, t + 1)
                nc.vector.tensor_tensor(acc[:, t, :], proj_bank[t % 2][:, :], acc[:, t, :], ALU.add).then_inc(bias_added, 1)
            dve.wait_ge(bias_added, MT)
            steps = [0]

            def ln_link(instruction):
                steps[0] += 1
                instruction.then_inc(m_ln, 1)
                dve.wait_ge(m_ln, steps[0])

            for s in range(2):
                e = NE - 2 + s
                for t in range(MT):
                    combine(e * MT + t, t, (s * MT + t) % 4, gates[:, t, e:e + 1]).then_inc(combined, 1)
                    if s == 1:
                        dve.wait_ge(combined, e * MT + t + 5)
                        nc.vector.bn_stats(m_stats[:, t, :], acc[:, t, :]).then_inc(m_measured, 1)
                        for g, (lo, hi) in enumerate(M_GROUPS):
                            if t == hi - 1:
                                dve.wait_ge(m_measured, hi)
                                for u in range(lo, hi):
                                    last = nc.vector.bn_aggr(m_mean_var[:, u, :], m_stats[:, u, :])
                                ln_link(last)
                                ln_link(nc.vector.tensor_scalar(m_var[:, lo:hi], m_mean_var[:, lo:hi, 1], EPS, None, ALU.add))
                                for op in rsqrt_ops(m_var[:, lo:hi], m_mean_var[:, lo:hi, 0], m_rstd[:, lo:hi],
                                                    m_newton[:, lo:hi], m_shift[:, lo:hi]):
                                    ln_link(op())

        block = ctx.enter_context(nc.Block())

        def steps(engine, step):
            step(0, "self", None, "self", "self")
            with engine.Fori(1, B - 2) as i:
                step(i, "self", "self", "self", "self")
            step(B - 2, "self", "self", "self", "cross")
            step(B - 1, "self", "self", "cross", "cross")
            step(B, "cross", "self", "cross", "cross")
            with engine.Fori(B + 1, STEPS - 2) as i:
                step(i, "cross", "cross", "cross", "cross")
            step(STEPS - 2, "cross", "cross", "cross", None)
            step(STEPS - 1, "cross", "cross", None, None)

        @block.sync
        def _(sp):
            load_sources(sp, 0, "self", True)
            sp.dma_start(ident[:, :], a["ident"]).then_inc(ident_in, 16)
            for m in range(4):
                load_job(sp, m)
            for dst, src in ((qkv_bias[:, 0, :], a["bq"]), (qkv_bias[:, 1, :], a["bk"]), (qkv_bias[:, 2, :], a["bv"])):
                sp.dma_start(dst, src).then_inc(consts_in, 16)
            for m in range(4, 8):
                load_job(sp, m)
            sp.dma_start(prior[:, :, :], a["prior"].rearrange("(t p) k -> p t k", p=T)).then_inc(consts_in, 16)
            sp.dma_start(lam[:, :], a["lam"].broadcast_to((T, 1))).then_inc(consts_in, 16)
            for n, name in enumerate(("bo", "b_out")):
                sp.dma_start(out_bias[:, n, :], a[name].rearrange("(a d) -> a d", a=1).broadcast_to((T, D))).then_inc(consts_in, 16)
            sp.dma_start(gate_raw[:, :, :], a["gate"]).then_inc(gate_in, 16)
            sp.dma_start(gate_bias[:, :], a["gate_bias"].rearrange("(a d) -> a d", a=1).broadcast_to((P, NE))).then_inc(gate_in, 16)
            sp.dma_start(iota[:, :], a["iota"].rearrange("(a d) -> a d", a=1).broadcast_to((P, NE))).then_inc(gate_in, 16)
            load_sources(sp, 1, "self", False)
            for m in range(8, 12):
                load_job(sp, m)
            stack_unit(sp, 0, 0)
            for m in range(12, 16):
                load_job(sp, m)
            steps(sp, lambda i, kind, prev, nxt, nxt2: sp_step(sp, i, kind, prev, nxt, nxt2))
            sp_experts(sp)

        @block.gpsimd
        def _(pool):
            pool.wait_ge(consts_in, 16 * 7)
            nc.gpsimd.tensor_scalar(prior[:, :, :], prior[:, :, :], lam[:, 0:1], ROOT, ALU.mult, ALU.mult).then_inc(prior_ready, 1)
            steps(pool, lambda i, kind, prev, nxt, nxt2: pool_step(pool, i, kind, nxt))
            pool_experts(pool)

        @block.scalar
        def _(act):
            sources_split(act, 0, "self", True)
            for m in range(0, 8):
                act_weight_hi(act, m)
            act.wait_ge(consts_in, 16 * 7)
            projection_split(act, 0, "self", 0, True)
            projection_split(act, 0, "self", 1, True)
            for m in range(8, 12):
                act_weight_hi(act, m)
            act.wait_ge(gate_in, 48)
            nc.scalar.activation(gate_w[:, 0, :, :], gate_raw[:, :, :], ACT.Copy).then_inc(gate_hi, 1)
            projection_split(act, 0, "self", 2, True)
            projection_split(act, 0, "self", 3, True)
            act_values(act, 0)
            for m in range(12, 16):
                act_weight_hi(act, m)
            steps(act, lambda i, kind, prev, nxt, nxt2: act_step(act, i, kind, nxt, prev is not None))
            act_norm_rows(act, STEPS - 1)
            act_experts(act)

        @block.vector
        def _(dve):
            sources_split(dve, 0, "self", False)
            for m in range(0, 8):
                weight_lo(dve, m, "dve")
            dve.wait_ge(consts_in, 16 * 7)
            projection_split(dve, 0, "self", 0, False)
            projection_split(dve, 0, "self", 1, False)
            for m in range(8, 12):
                weight_lo(dve, m, "dve")
            dve.wait_ge(gate_hi, 1)
            nc.vector.tensor_tensor(gate_w[:, 1, :, :], gate_raw[:, :, :], gate_w[:, 0, :, :], ALU.subtract).then_inc(gate_lo, 1)
            projection_split(dve, 0, "self", 2, False)
            projection_split(dve, 0, "self", 3, False)
            for m in range(12, 16):
                weight_lo(dve, m, "dve")
            dve.wait_ge(prior_ready, 1)
            steps(dve, lambda i, kind, prev, nxt, nxt2: dve_step(dve, i, kind, nxt, prev is not None))
            dve_add_rows(dve, STEPS - 1)
            for k in range(LN_OPS):
                dve_ln_op(dve, STEPS - 1, k)
            dve_experts(dve)

        @block.tensor
        def _(pe):
            pe.wait_ge(ident_in, 16)
            pe_turn_sources(pe, 0, "self")
            pe_projection_part(pe, 0, "self", 0, 96)
            pe_value_part(pe, 0, "self", 0, 24)
            steps(pe, lambda i, kind, prev, nxt, nxt2: pe_step(pe, i, kind, nxt))
            pe_experts(pe)


def _prior(np):
    at = np.arange(S, dtype=np.float32)
    delta = np.abs(at[:, None] - at[None, :])
    total = np.zeros_like(delta)
    for p, w, sigma in zip((1.0, 30.0), (0.8, 0.4), (0.5, 2.0)):
        total = total + np.float32(w) * np.exp(-(delta - np.float32(p)) ** 2 / np.float32(2.0 * sigma ** 2))
    return total.astype(np.float32)


def kernel(**inputs):
    import numpy as np
    import concourse.bacc as bacc
    from concourse.bass_utils import run_bass_kernel_spmd

    def chunks(w):
        return np.ascontiguousarray(np.asarray(w).T.reshape(KC, P, -1).transpose(1, 0, 2))

    def columns(b):
        return np.ascontiguousarray(np.asarray(b).reshape(KC, P).T)

    arrays = {
        "x": inputs["x"], "context": inputs["ctx_1024"],
        "mask": inputs["mask_BxSxS2_bf0"],
        "self_q": chunks(inputs["L0_attn_Wq"]), "self_k": chunks(inputs["L0_attn_Wk"]),
        "self_v": chunks(inputs["L0_attn_Wv"]), "self_o": chunks(inputs["L0_attn_Wo"]),
        "cross_q": chunks(inputs["L0_xattn_Wq"]), "cross_k": chunks(inputs["L0_xattn_Wk"]),
        "cross_v": chunks(inputs["L0_xattn_Wv"]), "cross_o": chunks(inputs["L0_xattn_Wout"]),
        "bq": columns(inputs["L0_attn_bq"]), "bk": columns(inputs["L0_attn_bk"]), "bv": columns(inputs["L0_attn_bv"]),
        "bo": inputs["L0_attn_bo"], "b_out": inputs["L0_xattn_b_out"],
        "lam": np.asarray(inputs["L0_attn_prior_lambda"]).reshape(1, 1),
        "experts": np.stack([chunks(w) for w in np.asarray(inputs["L0_ffn_We"])]),
        "expert_bias": inputs["L0_ffn_be"], "gate": chunks(inputs["L0_ffn_Wg"]), "gate_bias": inputs["L0_ffn_bg"],
        "ident": np.eye(P, dtype=np.float32), "iota": np.arange(NE, dtype=np.float32), "prior": _prior(np),
    }
    nc = bacc.Bacc("TRN2", target_bir_lowering=False, num_devices=1)
    named, aps = {}, {}
    for name, value in arrays.items():
        value = np.ascontiguousarray(value)
        named[f"in_{name}"] = value
        aps[name] = nc.dram_tensor(f"in_{name}", value.shape, mybir.dt.from_np(value.dtype), kind="ExternalInput").ap()
    out = nc.dram_tensor("out_rows", (B, S, D), F32, kind="ExternalOutput").ap()
    decoder_layer(nc, aps, out)
    result = run_bass_kernel_spmd(nc, [named], core_ids=[0])
    return result.results[0]["out_rows"]
```

```python
from contextlib import ExitStack

import concourse.bass as bass
from concourse import mybir

F32 = mybir.dt.float32
F32R = mybir.dt.float32r
I32 = mybir.dt.int32
U32 = mybir.dt.uint32
U8 = mybir.dt.uint8
ALU = mybir.AluOpType
ACT = mybir.ActivationFunctionType

B, S, D = 8, 224, 512
H, HD = 16, 32
NE, TOP = 8, 8
P = 128
KC = D // P
HC = P // HD
T = 112
NT = S // T
STEPS = 2 * B
TOKENS = B * S
MT = TOKENS // P
GT = MT // 2
ROOT = float(HD) ** 0.5
SCALE = 1.0 / ROOT
EPS = 1e-5
MASKED = -1.0e30
LOWEST = -3.0e38
RSQRT_MAGIC = float(0x5F3759DF)

LT, LC, LV = 3, 4, 5
DRAIN = H + LV
P_RING, W_RING = 4, 4
TURN_SLOTS = {"self": {("x", 0): 0, ("x", 1): 1},
              "cross": {("c", 0): 0, ("c", 1): 1, ("x", 0): 1, ("x", 1): 2}}
ATT_SLOT = (3, 6)
STACK_DMAS = 12
LN_OPS = 15

SELF_SLOT = {"k": 1, "q": 0, "v": 2, "o": 3}
CROSS_SLOT = {"k": 4, "q": 0, "v": 5, "o": 1}
EXPERT_SLOT = (2, 3)


def weight_jobs():
    jobs = []
    for m, slot, eng in (("self_k", 1, "dve"), ("self_q", 0, "dve"), ("self_v", 2, "dve"), ("self_o", 3, "dve"),
                         ("cross_k", 4, "pool"), ("cross_v", 5, "pool"), ("cross_q", 0, "dve"),
                         ("cross_o", 1, "pool"), ("e0", 2, "pool"), ("e1", 3, "pool")):
        jobs += [(m, c, slot, eng) for c in range(KC)]
    return jobs


JOBS = weight_jobs()
JOBS_AT = {}
for _c in range(8):
    JOBS_AT[(0, 2 + _c)] = [16 + _c]
for _c in range(4):
    JOBS_AT.setdefault((B - 1, _c // 2), []).append(24 + _c)
    JOBS_AT[(B - 1, 8 + _c)] = [28 + _c]
for _c in range(8):
    JOBS_AT[(STEPS - 1, _c)] = [32 + _c]


def fill_pieces(nxt, with_output):
    pieces = []
    if nxt:
        for what in ("c", "x") if nxt == "cross" else ("x",):
            pieces += [(what, f, 0, 4 * T) for f in range(2)]
    if with_output:
        pieces += [("o", h, m, D) for h in range(4) for m in range(6)]
    if nxt:
        pieces += [("p", f, m, S) for f in range(2) for m in range(24)]
        pieces += [("v", t, m, D) for t in range(NT) for m in range(12)]
        pieces += [("p", f, m, S) for f in range(2, 4) for m in range(24)]
    return pieces


def fill_slots(nxt, with_output):
    pieces = fill_pieces(nxt, with_output)
    slots, end, done = [[] for _ in range(H)], {}, 0
    total = sum(p[3] for p in pieces if (p[0], p[1]) not in TURN_SLOTS[nxt])
    first = max(TURN_SLOTS[nxt].values()) + 1
    for what, f, m, cost in pieces:
        if (what, f) in TURN_SLOTS[nxt]:
            n = TURN_SLOTS[nxt][(what, f)]
        else:
            n = first + done * (H - first) // total
            done += cost
        slots[n].append((what, f, m))
        end[(what, f)] = n
    return slots, end


def last_fill_slots():
    slots, end = [[] for _ in range(H)], {}
    for what, first in (("o", 0), ("O", 9)):
        for h in range(4):
            for m in range(6):
                slots[first + h].append((what, h, m))
            end[(what, h)] = first + h
    return slots, end


def schedule(nxt, with_output):
    slots, end = fill_slots(nxt, with_output) if nxt else last_fill_slots()
    assert not nxt or end[("p", 3)] == H - 1
    return slots, end


def lo_count(job, eng):
    return sum(JOBS[m][3] == eng for m in range(job + 1))


def decoder_layer(nc, a, out):
    with ExitStack() as ctx:
        def sb(name, shape, dt=F32, stack=ctx):
            return stack.enter_context(nc.sbuf_tensor(name, shape, dt))

        def sem(name):
            return ctx.enter_context(nc.semaphore(name))

        x1_dram = nc.dram_tensor("x1_rows", (B, S, D), F32).ap()
        x2_dram = nc.dram_tensor("x2_rows", (B, S, D), F32).ap()

        w_raw = sb("w_raw", [P, W_RING, D])
        weights = {s: sb(f"weights{s}", [P, 2, KC, D], F32R) for s in EXPERT_SLOT}
        ident = sb("ident", [P, P])
        qkv_bias = sb("qkv_bias", [P, 3, KC])
        late_bias = sb("late_bias", [T, NT, S])
        lam = sb("lam", [T, 1])
        mask_u8 = sb("mask_u8", [T, NT, S], U8)
        mask_bias = sb("mask_bias", [T, NT, S])
        out_bias = sb("out_bias", [T, 2, D])
        residual = sb("residual", [T, NT, D])
        rows = sb("rows", [T, NT, D])
        stats = sb("stats", [T, NT, 6])
        mean_var = sb("mean_var", [T, NT, 2])
        var_eps = sb("var_eps", [T, NT])
        rstd = sb("rstd", [T, NT])
        newton = sb("newton", [T, NT])
        neg_mean_rstd = sb("neg_mean_rstd", [T, NT])
        neg_max = sb("neg_max", [T, P_RING, NT])
        row_sum = sb("row_sum", [T, P_RING, NT])
        recip = sb("recip", [T, P_RING, NT])
        gate_raw = sb("gate_raw", [P, KC, NE])
        gate_w = sb("gate_w", [P, 2, KC, NE], F32R)
        gate_bias = sb("gate_bias", [P, NE])
        iota = sb("iota", [P, NE])

        attn = ExitStack()
        for s in (4, 5, 0, 1):
            weights[s] = sb(f"weights{s}", [P, 2, KC, D], F32R, attn)
        stacks = [sb(f"stack{w}", [3 * HD, HC, 2, 2 * S], F32R, attn) for w in range(2)]
        src_x = sb("src_x", [P, 2, KC, S], F32R, attn)
        src_c = sb("src_c", [P, 2, KC, S], F32R, attn)
        qk = sb("qk", [P, 4, 2 * S], F32R, attn)
        attended = sb("attended", [P, 2, KC, S], F32R, attn)
        values = sb("values", [T, NT, D], F32, attn)
        values_next = sb("values_next", [T, NT, D], F32, attn)
        nat_x = sb("nat_x", [T, NT, D], F32, attn)
        nat_c = sb("nat_c", [T, NT, D], F32, attn)
        probs = sb("probs", [T, P_RING, NT, S], F32, attn)
        probs_t = sb("probs_t", [T, 2, NT * S], F32, attn)
        attn.close()

        moe = ctx.enter_context(ExitStack())
        acc = sb("acc", [P, MT, D], F32, moe)
        x2t = sb("x2t", [P, 2, KC, TOKENS], F32R, moe)
        be_raw = sb("be_raw", [3 * NE, D], F32, moe)
        be_lo = sb("be_lo", [3 * NE, D], F32R, moe)
        be_stack = sb("be_stack", [3 * NE, D], F32R, moe)
        gates_t = sb("gates_t", [3 * NE, TOKENS], F32R, moe)
        logits = sb("logits", [P, MT, NE], F32, moe)
        top = sb("top", [P, MT, TOP], F32, moe)
        top_at = sb("top_at", [P, MT, TOP], U32, moe)
        top_f = sb("top_f", [P, MT, 2], F32, moe)
        pair_w = sb("pair_w", [P, 4, MT], F32, moe)
        one_hot = sb("one_hot", [P, 2, MT, NE], F32, moe)
        gates = sb("gates", [P, MT, NE], F32, moe)
        gate_hl = sb("gate_hl", [P, MT, 3 * NE], F32R, moe)
        m_stats = sb("m_stats", [P, MT, 6], F32, moe)
        m_mean_var = sb("m_mean_var", [P, MT, 2], F32, moe)
        m_var = sb("m_var", [P, MT], F32, moe)
        m_rstd = sb("m_rstd", [P, MT], F32, moe)
        m_newton = sb("m_newton", [P, MT], F32, moe)
        m_shift = sb("m_shift", [P, MT], F32, moe)

        def bank(name):
            return ctx.enter_context(nc.psum_tensor(name, [P, 512], F32))

        score_bank = [bank(f"score_bank{n}") for n in range(2)]
        turn_bank = [bank(f"turn_bank{n}") for n in range(2)]
        value_bank = [bank(f"value_bank{n}") for n in range(2)]
        proj_bank = [bank(f"proj_bank{n}") for n in range(2)]
        product_bank = score_bank + value_bank

        ident_in = sem("ident_in")
        consts_in = sem("consts_in")
        gate_in = sem("gate_in")
        raw_in = [sem(f"raw_in{r}") for r in range(W_RING)]
        w_hi = sem("w_hi")
        w_lo = {"dve": sem("w_lo_dve"), "pool": sem("w_lo_pool")}
        x_in, c_in, mask_in, residual_in = sem("x_in"), sem("c_in"), sem("mask_in"), sem("residual_in")
        x_turned, x_hi, x_lo = sem("x_turned"), sem("x_hi"), sem("x_lo")
        c_turned, c_hi, c_lo = sem("c_turned"), sem("c_hi"), sem("c_lo")
        qk_full, qk_hi, qk_lo = sem("qk_full"), sem("qk_hi"), sem("qk_lo")
        stacked = [sem("stacked0"), sem("stacked1")]
        v_full, v_copied = sem("v_full"), sem("v_copied")
        v_placed = [sem("v_placed0"), sem("v_placed1")]
        prior_ready, bias_scaled, bias_ready = sem("prior_ready"), sem("bias_scaled"), sem("bias_ready")
        bias_doubled = sem("bias_doubled")
        scored, biased, exp_done = sem("scored"), sem("biased"), sem("exp_done")
        sum_kept, recip_ready, normed = sem("sum_kept"), sem("recip_ready"), sem("normed")
        turned, copied_dve, copied_act, pv_done = sem("turned"), sem("copied_dve"), sem("copied_act"), sem("pv_done")
        att_hi, att_lo, att_half_read = sem("att_hi"), sem("att_lo"), sem("att_half_read")
        o_full, residual_ready, rows_added = sem("o_full"), sem("residual_ready"), sem("rows_added")
        ln_step, rows_normed, rows_stored = sem("ln_step"), sem("rows_normed"), sem("rows_stored")
        acc_in = [sem(f"acc_in{n}") for n in range(3)]
        be_in, be_step, be_stacked = sem("be_in"), sem("be_step"), sem("be_stacked")
        m_turned, m_hi, m_lo = sem("m_turned"), sem("m_hi"), sem("m_lo")
        gate_hi, gate_lo = sem("gate_hi"), sem("gate_lo")
        logits_full, gate_step, pair_diff, pair_exp = sem("logits_full"), sem("gate_step"), sem("pair_diff"), sem("pair_exp")
        gates_done, gates_turned, gates_copied = sem("gates_done"), sem("gates_turned"), sem("gates_copied")
        product_full, combined = sem("product_full"), sem("combined")
        bias_full, bias_added = sem("bias_full"), sem("bias_added")
        m_measured, m_ln, m_normed, out_stored = sem("m_measured"), sem("m_ln"), sem("m_normed"), sem("out_stored")

        def head(i, n):
            return i * H + n + 1

        def copies(i, n):
            if n < 0:
                i, n = i - 1, n + H
            if n % 4 == 3:
                return copied_act, i * (H // 4) + n // 4 + 1
            return copied_dve, i * (H - H // 4) + n - n // 4 + 1

        def wait_alone(eng, *waits):
            waits = [(semaphore, value if isinstance(value, int) else eng.snap(eng.to_reg(value)))
                     for semaphore, value in waits]
            eng.wait_ge(ident_in, 16)
            for semaphore, value in waits:
                eng.wait_ge(semaphore, value)

        def cross(kind):
            return kind == "cross"

        def key_tiles(kind, qt):
            return qt + 1 if cross(kind) else NT

        def turned_at(kind, qt, kt):
            if cross(kind) and kt == 1:
                return S
            return kt * S + qt * T

        def turned_cols(kind):
            return S + T if cross(kind) else NT * S

        def slots_of(kind):
            return CROSS_SLOT if cross(kind) else SELF_SLOT

        def sources(kind):
            return (src_x, src_c) if cross(kind) else (src_x, src_x)

        def projection_bias(kind, what, c):
            return qkv_bias[:, {"q": 0, "k": 1, "v": 2}[what], c:c + 1]

        FILLS = (("k", 0), ("q", 0), ("k", 1), ("q", 1))
        PLANE = {"q": 0, "k": 2}

        def three_passes(ps, stationary, moving):
            steps = [(sl, ml, c) for c in range(KC) for sl, ml in ((0, 0), (0, 1), (1, 0))]
            return [(ps, stationary(sl, c), moving(ml, c), n == 0, n == len(steps) - 1)
                    for n, (sl, ml, c) in enumerate(steps)]

        def run(matmuls):
            last = None
            for ps, lhs, rhs, first, end in matmuls:
                last = nc.tensor.matmul(ps, lhs, rhs, start=first, stop=end)
            return last

        def projection(kind, f):
            what, unit = FILLS[f]
            w = weights[slots_of(kind)[what]]
            src = sources(kind)[0 if what == "q" else 1]
            found = []
            for cc in range(2):
                o = P * (2 * unit + cc)
                found += three_passes(proj_bank[f % 2][:, cc * S:cc * S + S],
                                      lambda hl, c: w[:, hl, c, o:o + P], lambda hl, c: src[:, hl, c, :])
            return found

        def pe_turn_source(pe, s, kind, what, f):
            if what == "c":
                nat, done = nat_c, c_turned
                if f == 0:
                    pe.wait_ge(c_in, (s - B) * 16 + 16)
            else:
                nat, done = nat_x, x_turned
                if f == 0:
                    pe.wait_ge(x_in, s * 16 + 16)
            if what == "x" and cross(kind):
                pe.wait_ge(c_lo, (s - B) * 2 + f + 1)
            elif not (isinstance(s, int) and s == 0):
                pe.wait_ge(qk_lo, s * 4 - 1 + f)
            for cc in range(2):
                for t in range(NT):
                    last = nc.tensor.transpose(proj_bank[f % 2][:, cc * S + t * T:cc * S + t * T + T],
                                               nat[:, t, (2 * f + cc) * P:(2 * f + cc + 1) * P], ident[0:T, 0:T])
            last.then_inc(done, 1)

        def pe_projection_piece(pe, s, kind, f, at):
            if at == 0:
                if f < 2:
                    if FILLS[f][0] == "k" and cross(kind):
                        pe.wait_ge(c_lo, (s - B) * 2 + 2)
                    pe.wait_ge(x_lo, s * 2 + 2)
                    pe_wait_weights(pe, kind, FILLS[f][0], s)
                    if not isinstance(s, int) or s >= 3:
                        pe.wait_ge(rows_added, (s - 3) * 2 + f + 1)
                else:
                    pe.wait_ge(v_copied, s * 2 + f - 1)
            last = run(projection(kind, f)[at:at + 1])
            if at == 23:
                last.then_inc(qk_full, 1)

        def pe_wait_weights(pe, kind, what, s):
            first = {("self", "k"): 0, ("self", "q"): 0, ("self", "v"): 0, ("self", "o"): 0,
                     ("cross", "k"): B, ("cross", "q"): B, ("cross", "v"): B, ("cross", "o"): B}[(kind, what)]
            if isinstance(s, int) and s == first:
                job = max(m for m, j in enumerate(JOBS) if j[0] == f"{kind}_{what}")
                pe.wait_ge(w_lo[JOBS[job][3]], lo_count(job, JOBS[job][3]))

        def value_fill(kind, t):
            w = weights[slots_of(kind)["v"]]
            src = sources(kind)[1]
            return three_passes(proj_bank[t][0:T, :], lambda hl, c: src[:, hl, c, t * T:t * T + T],
                                lambda hl, c: w[:, hl, c, :])

        def pe_value_piece(pe, s, kind, t, at):
            if at == 0:
                if t == 0:
                    pe_wait_weights(pe, kind, "v", s)
                pe.wait_ge(qk_lo, s * 4 + t + 1)
            last = run(value_fill(kind, t)[at:at + 1])
            if at == 11:
                last.then_inc(v_full, 1)

        def pe_scores(pe, i, kind, n):
            unit, slot = divmod(n, 8)
            c, j = divmod(slot, HC)
            st, o = stacks[unit], c * S
            if slot == 0:
                pe.wait_ge(stacked[unit], i * 16 * STACK_DMAS + 16 * STACK_DMAS)
            if not (isinstance(i, int) and i == 0 and n < 2):
                pe.wait_ge(biased, head(i, n - 2))
            for qt in range(NT):
                w = key_tiles(kind, qt) * T
                last = nc.tensor.matmul(score_bank[n % 2][0:T, qt * S:qt * S + w],
                                        st[:, j, 0, o + qt * T:o + qt * T + T], st[:, j, 1, o:o + w],
                                        start=True, stop=True)
            last.then_inc(scored, 1)

        def pe_turn_probs(pe, i, kind, n):
            pe.wait_ge(normed, head(i, n))
            if not (isinstance(i, int) and i == 0 and n < 2):
                pe.wait_ge(*copies(i, n - 2))
            for qt in range(NT):
                for kt in range(key_tiles(kind, qt)):
                    o = turned_at(kind, qt, kt)
                    last = nc.tensor.transpose(turn_bank[n % 2][0:T, o:o + T],
                                               probs[:, n % P_RING, qt, kt * T:kt * T + T], ident[0:T, 0:T])
            last.then_inc(turned, 1)

        def pe_values(pe, i, kind, n):
            unit, slot = divmod(n, 8)
            c, j = divmod(slot, HC)
            if slot == 0 and not (isinstance(i, int) and i == 0):
                pe.wait_ge(att_lo, i * 2 + unit - 1)
            if slot == 0:
                pe.wait_ge(v_placed[unit], i * 16 + 16)
            pe.wait_ge(*copies(i, n))
            for kt in range(NT):
                q0 = T if cross(kind) and kt == 1 else 0
                o = turned_at(kind, q0 // T, kt)
                last = nc.tensor.matmul(value_bank[unit][HD * j:HD * j + HD, c * S + q0:c * S + S],
                                        values[:, kt, n * HD:n * HD + HD], probs_t[:, n % 2, o:o + S - q0],
                                        start=kt == 0, stop=kt == NT - 1)
            last.then_inc(pv_done, 1)

        def pe_output_piece(pe, k, kind, h, m, banks_read):
            half, t = divmod(h, 2)
            if m == 0:
                if h == 0:
                    pe_wait_weights(pe, kind, "o", k)
                if t == 0:
                    pe.wait_ge(att_lo, k * 2 + half + 1)
                if half == 0:
                    semaphore, value = banks_read
                    pe.wait_ge(semaphore, value + t)
            w = weights[slots_of(kind)["o"]]
            fill = three_passes(proj_bank[t][0:T, :], lambda hl, c: attended[:, hl, c, t * T:t * T + T],
                                lambda hl, c: w[:, hl, c, :])
            last = run(fill[6 * half + m:6 * half + m + 1])
            if m == 5 and half == 1:
                last.then_inc(o_full, 1)
            elif m == 5 and t == 1:
                last.then_inc(att_half_read, 1)

        def pe_piece(pe, i, kinds, piece):
            before2, before, _, nxt = kinds
            what, f, m = piece
            if what in ("c", "x"):
                pe_turn_source(pe, i + 1, nxt, what, f)
            elif what == "p":
                pe_projection_piece(pe, i + 1, nxt, f, m)
            elif what == "v":
                pe_value_piece(pe, i + 1, nxt, f, m)
            elif what == "o":
                pe_output_piece(pe, i - 2, before2, f, m, (x_lo, i * 2 + 3) if nxt else (qk_lo, i * 4 + 3))
            else:
                pe_output_piece(pe, i - 1, before, f, m, (rows_added, i * 2 - 3))

        def pe_step(pe, i, kinds):
            before2, before, kind, nxt = kinds
            pieces, _ = schedule(nxt, before2)
            for n in range(H if nxt else DRAIN):
                if n < H - 1:
                    pe_scores(pe, i, kind, n + 1)
                elif nxt:
                    pe_scores(pe, i + 1, nxt, 0)
                if n - LT < 0:
                    if before:
                        pe_turn_probs(pe, i - 1, before, n - LT + H)
                elif n - LT < H:
                    pe_turn_probs(pe, i, kind, n - LT)
                if n < H:
                    for piece in pieces[n]:
                        pe_piece(pe, i, kinds, piece)
                if n - LV >= 0:
                    pe_values(pe, i, kind, n - LV)
                elif before:
                    pe_values(pe, i - 1, before, n - LV + H)

        def act_split(act, dst_hi, ps, bias):
            if bias is None:
                return nc.scalar.activation(dst_hi, ps, ACT.Copy)
            return nc.scalar.activation(dst_hi, ps, ACT.Identity, bias=bias)

        def dve_split(dst_lo, ps, bias, src_hi):
            if bias is None:
                return nc.vector.tensor_tensor(dst_lo, ps, src_hi, ALU.subtract)
            return nc.vector.scalar_tensor_tensor(dst_lo, ps, bias, src_hi, ALU.add, ALU.subtract)

        def source_split(eng, s, kind, f, is_context, is_act):
            dst, hi_done, lo_done, full = ((src_c, c_hi, c_lo, c_turned) if is_context
                                           else (src_x, x_hi, x_lo, x_turned))
            j = s - B if is_context else s
            ps = proj_bank[f % 2][:, 0:2 * S].rearrange("p (c n) -> p c n", c=2)
            if is_act:
                eng.wait_ge(full, j * 2 + f + 1)
                act_split(eng, dst[:, 0, 2 * f:2 * f + 2, :], ps, None).then_inc(hi_done, 1)
            else:
                eng.wait_ge(hi_done, j * 2 + f + 1)
                dve_split(dst[:, 1, 2 * f:2 * f + 2, :], ps, None, dst[:, 0, 2 * f:2 * f + 2, :]).then_inc(lo_done, 1)

        def projection_split(eng, s, kind, f, is_act):
            what, unit = FILLS[f]
            plane = PLANE[what]
            ps = proj_bank[f % 2]
            if is_act:
                eng.wait_ge(qk_full, s * 4 + f + 1)
                if not (isinstance(s, int) and s == 0 and unit == 0):
                    eng.wait_ge(stacked[1 - unit], s * 16 * STACK_DMAS + (16 * STACK_DMAS if unit else 0))
            else:
                eng.wait_ge(qk_hi, s * 4 + f + 1)
            parts = [(slice(0, 2 * S), None)] if cross(kind) else [
                (slice(cc * S, cc * S + S), projection_bias(kind, what, 2 * unit + cc)) for cc in range(2)]
            for sl, bias in parts:
                if is_act:
                    last = act_split(eng, qk[:, plane, sl], ps[:, sl], bias)
                else:
                    last = dve_split(qk[:, plane + 1, sl], ps[:, sl], bias, qk[:, plane, sl])
            last.then_inc(qk_hi if is_act else qk_lo, 1)

        def attended_split(eng, i, kind, unit, is_act):
            ps = value_bank[unit][:, 0:2 * S].rearrange("p (c n) -> p c n", c=2)
            if is_act:
                eng.wait_ge(pv_done, head(i, 8 * unit + 7))
                if not (isinstance(i, int) and i == 0):
                    if unit == 0:
                        eng.wait_ge(att_half_read, i)
                    else:
                        eng.wait_ge(o_full, i * 2)
            else:
                eng.wait_ge(att_hi, i * 2 + unit + 1)
            parts = [(slice(0, 2), None)] if cross(kind) else [
                (slice(cc, cc + 1), projection_bias(kind, "v", 2 * unit + cc)) for cc in range(2)]
            for sl, bias in parts:
                at = slice(2 * unit + sl.start, 2 * unit + sl.stop)
                if is_act:
                    last = act_split(eng, attended[:, 0, at, :], ps[:, sl, :], bias)
                else:
                    last = dve_split(attended[:, 1, at, :], ps[:, sl, :], bias, attended[:, 0, at, :])
            last.then_inc(att_hi if is_act else att_lo, 1)

        def act_weight_hi(act, m):
            name, c, slot, _ = JOBS[m]
            act.wait_ge(raw_in[m % W_RING], 16 * (m // W_RING + 1))
            if c == 0:
                if name in ("cross_q", "cross_o"):
                    act.wait_ge(qk_full, 4 * B)
                if name == "e0":
                    act.wait_ge(v_full, 2 * B)
                if name == "e1":
                    act.wait_ge(o_full, 2 * B)
            nc.scalar.activation(weights[slot][:, 0, c, :], w_raw[:, m % W_RING, :], ACT.Copy).then_inc(w_hi, 1)

        def weight_lo(eng, m, which):
            _, c, slot, _ = JOBS[m]
            eng.wait_ge(w_hi, m + 1)
            e = nc.vector if which == "dve" else nc.gpsimd
            e.tensor_tensor(weights[slot][:, 1, c, :], w_raw[:, m % W_RING, :], weights[slot][:, 0, c, :],
                            ALU.subtract).then_inc(w_lo[which], 1)

        def act_exp(act, i, kind, n):
            r = n % P_RING
            act.wait_ge(biased, head(i, n))
            for qt in range(NT):
                w = key_tiles(kind, qt) * T
                last = nc.scalar.activation(probs[:, r, qt, 0:w], probs[:, r, qt, 0:w], ACT.Exp,
                                            bias=neg_max[:, r, qt:qt + 1], scale=-1.0,
                                            accum_out=row_sum[:, r, qt:qt + 1])
            last.then_inc(exp_done, 1)

        def copy_turned(eng, i, kind, n, is_act):
            eng.wait_ge(turned, head(i, n))
            if not (isinstance(i, int) and i == 0 and n < 2):
                eng.wait_ge(pv_done, head(i, n - 2))
            w = turned_cols(kind)
            if is_act:
                nc.scalar.activation(probs_t[:, n % 2, 0:w], turn_bank[n % 2][0:T, 0:w], ACT.Copy).then_inc(copied_act, 1)
            else:
                nc.vector.tensor_copy(probs_t[:, n % 2, 0:w], turn_bank[n % 2][0:T, 0:w]).then_inc(copied_dve, 1)

        def act_values(act, s, t):
            act.wait_ge(v_full, s * 2 + t + 1)
            if t == 0 and not (isinstance(s, int) and s == 0):
                for unit in range(2):
                    act.wait_ge(v_placed[unit], s * 16)
            nc.scalar.activation(values_next[:, t, :], proj_bank[t][0:T, :], ACT.Copy).then_inc(v_copied, 1)

        def fill_done(eng, i, nxt, what, f, is_act):
            if what in ("c", "x"):
                source_split(eng, i + 1, nxt, f, what == "c", is_act)
            elif what == "p":
                projection_split(eng, i + 1, nxt, f, is_act)
            elif what == "v" and is_act:
                act_values(eng, i + 1, f)

        def act_norm_rows(act, i):
            act.wait_ge(ln_step, i * LN_OPS + LN_OPS)
            for t in range(NT):
                last = nc.scalar.activation(rows[:, t, :], rows[:, t, :], ACT.Identity,
                                            bias=neg_mean_rstd[:, t:t + 1], scale=rstd[:, t:t + 1])
            last.then_inc(rows_normed, 1)

        def act_step(act, i, kinds):
            before2, before, kind, nxt = kinds
            _, end = schedule(nxt, before2)
            for n in range(H if nxt else DRAIN):
                for m in JOBS_AT.get((i, n), []) if isinstance(i, int) else []:
                    act_weight_hi(act, m)
                if n < H:
                    act_exp(act, i, kind, n)
                m = n - LC
                if m % 4 == 3 and m < H:
                    if m >= 0:
                        copy_turned(act, i, kind, m, True)
                    elif before:
                        copy_turned(act, i - 1, before, m + H, True)
                for (what, f), slot in end.items():
                    if slot == n:
                        fill_done(act, i, nxt, what, f, True)
                if before and n == ATT_SLOT[0]:
                    attended_split(act, i - 1, before, 0, True)
                if before and n == ATT_SLOT[1]:
                    attended_split(act, i - 1, before, 1, True)
                if before2 and n == end[("o", 3)] + 8:
                    act_norm_rows(act, i - 2)
                if not nxt and n == end[("O", 3)] + 8:
                    act_norm_rows(act, i - 1)
            if not nxt:
                attended_split(act, i, kind, 0, True)
                attended_split(act, i, kind, 1, True)

        def dve_bias_max(dve, i, kind, n):
            r = n % P_RING
            if n == 0 and cross(kind):
                dve.wait_ge(bias_ready, i - B + 1)
            if n == 8 and cross(kind):
                dve.wait_ge(bias_doubled, (i - B) * 16 + 16)
            if not (isinstance(i, int) and i == 0 and n < P_RING):
                dve.wait_ge(turned, head(i, n - P_RING))
            wait_alone(dve, (scored, head(i, n)))
            bias = mask_bias if cross(kind) and n < 8 else late_bias
            for qt in range(NT):
                w = key_tiles(kind, qt) * T
                last = nc.vector.tensor_tensor_reduce(probs[:, r, qt, 0:w], score_bank[n % 2][0:T, qt * S:qt * S + w],
                                                      bias[:, qt, 0:w], -SCALE, -MASKED * SCALE * 1e-3, ALU.add, ALU.min,
                                                      neg_max[:, r, qt:qt + 1])
            last.then_inc(biased, 1)

        def dve_keep_sum(dve, i, n):
            r = n % P_RING
            dve.wait_ge(exp_done, head(i, n))
            nc.vector.tensor_scalar(row_sum[:, r, :], row_sum[:, r, :], 0.5, None, ALU.max).then_inc(sum_kept, 1)

        def dve_recip(dve, i, kind, n):
            r = n % P_RING
            if cross(kind):
                dve.wait_ge(sum_kept, head(i - B, n))
            else:
                dve.wait_ge(exp_done, head(i, n))
            nc.vector.reciprocal(recip[:, r, :], row_sum[:, r, :]).then_inc(recip_ready, 1)

        def dve_add_rows(dve, i, t):
            if t == 0:
                dve.wait_ge(residual_ready, i + 1)
                if not (isinstance(i, int) and i == 0):
                    dve.wait_ge(rows_stored, i * 16)
            dve.wait_ge(o_full, i * 2 + t + 1)
            nc.vector.tensor_tensor(rows[:, t, :], proj_bank[t][0:T, :], residual[:, t, :],
                                    ALU.add).then_inc(rows_added, 1)

        def rsqrt_ops(var, mean, r, tmp, shift):
            v = nc.vector
            ops = [lambda: v.tensor_scalar(r.bitcast(I32), var.bitcast(I32), 1, None, ALU.logical_shift_right),
                   lambda: v.tensor_scalar(r.bitcast(I32), r.bitcast(I32), -1.0, RSQRT_MAGIC, ALU.mult, ALU.add)]
            for _ in range(3):
                ops += [lambda: v.tensor_tensor(tmp, r, r, ALU.mult),
                        lambda: v.scalar_tensor_tensor(tmp, tmp, -0.5, var, ALU.mult, ALU.mult),
                        lambda: v.scalar_tensor_tensor(r, tmp, 1.5, r, ALU.add, ALU.mult)]
            return ops + [lambda: v.scalar_tensor_tensor(shift, mean, -1.0, r, ALU.mult, ALU.mult)]

        def dve_ln_op(dve, i, k):
            if k == 0:
                dve.wait_ge(rows_added, i * 2 + 2)
                nc.vector.bn_stats(stats[:, 0, :], rows[:, 0, :])
                last = nc.vector.bn_stats(stats[:, 1, :], rows[:, 1, :])
            elif k == 1:
                wait_alone(dve, (ln_step, i * LN_OPS + k))
                nc.vector.bn_aggr(mean_var[:, 0, :], stats[:, 0, :])
                last = nc.vector.bn_aggr(mean_var[:, 1, :], stats[:, 1, :])
            elif k == 2:
                dve.wait_ge(ln_step, i * LN_OPS + k)
                last = nc.vector.tensor_scalar(var_eps[:, :], mean_var[:, :, 1], EPS, None, ALU.add)
            else:
                dve.wait_ge(ln_step, i * LN_OPS + k)
                last = rsqrt_ops(var_eps[:, :], mean_var[:, :, 0], rstd[:, :], newton[:, :],
                                 neg_mean_rstd[:, :])[k - 3]()
            last.then_inc(ln_step, 1)

        def dve_step(dve, i, kinds):
            before2, before, kind, nxt = kinds
            _, end = schedule(nxt, before2)
            for n in range(H if nxt else DRAIN):
                if n < H:
                    dve_bias_max(dve, i, kind, n)
                if n == 0:
                    fill_done(dve, i - 1, kind, "p", 3, False)
                for (what, f), slot in end.items():
                    if slot == n - 1 and (what, f) != ("p", 3):
                        fill_done(dve, i, nxt, what, f, False)
                if before and n == ATT_SLOT[0] + 1:
                    attended_split(dve, i - 1, before, 0, False)
                if before and n == ATT_SLOT[1] + 1:
                    attended_split(dve, i - 1, before, 1, False)
                for m in JOBS_AT.get((i, n), []) if isinstance(i, int) else []:
                    if JOBS[m][3] == "dve":
                        weight_lo(dve, m, "dve")
                summed = (i, kind, n - 1) if n >= 1 else (i - 1, before, H - 1)
                if summed[1] and n <= H and cross(summed[1]):
                    dve_keep_sum(dve, summed[0], summed[2])
                m = n - LC
                if m % 4 != 3 and m < H:
                    if m >= 0:
                        copy_turned(dve, i, kind, m, False)
                    elif before:
                        copy_turned(dve, i - 1, before, m + H, False)
                if summed[1] and n <= H:
                    dve_recip(dve, *summed)
                for (what, f), slot in end.items():
                    if slot == n - 1 and what in ("o", "O") and f >= 2:
                        dve_add_rows(dve, i - 2 if what == "o" else i - 1, f - 2)
                for what, step in (("o", i - 2), ("O", i - 1)):
                    if (what, 3) in end and (what == "O" or before2) and 2 <= n - end[(what, 3)] <= 6:
                        at = n - end[(what, 3)] - 1
                        for k in range((at - 1) * 3, at * 3):
                            dve_ln_op(dve, step, k)
            if not nxt:
                attended_split(dve, i, kind, 0, False)
                attended_split(dve, i, kind, 1, False)

        def pool_norm(pool, i, kind, n):
            r = n % P_RING
            pool.wait_ge(recip_ready, head(i, n))
            if cross(kind):
                for qt in range(NT):
                    w = key_tiles(kind, qt) * T
                    last = nc.gpsimd.tensor_tensor(probs[:, r, qt, 0:w], probs[:, r, qt, 0:w],
                                                   recip[:, r, qt:qt + 1].broadcast_to((T, w)), ALU.mult)
            else:
                last = nc.gpsimd.tensor_tensor(
                    probs[:, r], probs[:, r],
                    recip[:, r, :].rearrange("p (a b) -> p a b", b=1).broadcast_to((T, NT, S)), ALU.mult)
            last.then_inc(normed, 1)

        def pool_residual(pool, i, kind):
            pool.wait_ge(residual_in, i * 16 + 16)
            b = out_bias[:, 1 if cross(kind) else 0, :].rearrange("p (a b) -> p a b", a=1).broadcast_to((T, NT, D))
            nc.gpsimd.tensor_tensor(residual[:, :, :], residual[:, :, :], b, ALU.add).then_inc(residual_ready, 1)

        def pool_mask(pool, s):
            wait_alone(pool, (mask_in, (s - B) * 16 + 16), (biased, head(s - 1, 7)))
            nc.gpsimd.tensor_scalar(mask_bias[:, :, :], mask_u8[:, :, :], MASKED, None, ALU.mult).then_inc(bias_scaled, 1)
            wait_alone(pool, (bias_scaled, s - B + 1))
            nc.gpsimd.affine_select(out=mask_bias[:, :, :], in_=mask_bias[:, :, :], compare_op=ALU.is_ge,
                                    fill=MASKED, base=0, pattern=[[T, NT], [-1, S]],
                                    channel_multiplier=1).then_inc(bias_ready, 1)

        def pool_step(pool, i, kinds):
            before2, before, kind, nxt = kinds
            for n in range(H):
                pool_norm(pool, i, kind, n)
                for m in JOBS_AT.get((i, n), []) if isinstance(i, int) else []:
                    if JOBS[m][3] == "pool":
                        weight_lo(pool, m, "pool")
                if before and n == 8:
                    pool_residual(pool, i - 1, before)
                if nxt and cross(nxt) and n == 10:
                    pool_mask(pool, i + 1)

        def load_raw(sp, m, src):
            if m >= W_RING:
                eng = JOBS[m - W_RING][3]
                sp.wait_ge(w_lo[eng], lo_count(m - W_RING, eng))
            sp.dma_start(w_raw[:, m % W_RING, :], src).then_inc(raw_in[m % W_RING], 16)

        def load_job(sp, m):
            name, c, _, _ = JOBS[m]
            load_raw(sp, m, a["experts"][int(name[1:]), :, c, :] if name[0] == "e" else a[name][:, c, :])

        def batch_rows(dram, b):
            return dram[b].rearrange("(t p) d -> p t d", p=T)

        def load_sources(sp, s, kind, first):
            if not first:
                sp.wait_ge(x_turned, s * 2)
            if cross(kind):
                sp.wait_ge(rows_stored, (s - B) * 16 + 16)
                sp.dma_start(nat_x[:, :, :], batch_rows(x1_dram, s - B)).then_inc(x_in, 16)
                if not (isinstance(s, int) and s == B):
                    sp.wait_ge(c_turned, (s - B) * 2)
                sp.dma_start(nat_c[:, :, :], a["context"][s - B, 0:S, :].rearrange("(t p) d -> p t d", p=T)).then_inc(c_in, 16)
            else:
                sp.dma_start(nat_x[:, :, :], batch_rows(a["x"], s)).then_inc(x_in, 16)

        def load_residual(sp, i, kind):
            if not (isinstance(i, int) and i == 0):
                sp.wait_ge(rows_added, i * 2)
            src = batch_rows(x1_dram, i - B) if cross(kind) else batch_rows(a["x"], i)
            sp.dma_start(residual[:, :, :], src).then_inc(residual_in, 16)

        def load_mask(sp, s):
            if not (isinstance(s, int) and s == B):
                wait_alone(sp, (bias_scaled, s - B))
            sp.dma_start(mask_u8[:, :, :], a["mask"][s - B, 0:S, 0:S].rearrange("(t p) k -> p t k", p=T)).then_inc(mask_in, 16)

        def stack_unit(sp, s, unit):
            wait_alone(sp, (qk_lo, s * 4 + 2 * unit + 2))
            if unit == 1 or not (isinstance(s, int) and s == 0):
                if not (isinstance(s, int) and s == 0):
                    sp.wait_ge(scored, s * H - (0 if unit else 8))
            for j in range(HC):
                for role, planes in enumerate((slice(0, 3, 2), slice(1, 3), slice(0, 4, 3))):
                    sp.dma_start(stacks[unit][HD * role:HD * role + HD, j, :, :].bitcast(F32),
                                 qk[HD * j:HD * j + HD, planes, :].bitcast(F32)).then_inc(stacked[unit], 16)

        def store_rows(sp, i, kind):
            sp.wait_ge(rows_normed, i + 1)
            dst = batch_rows(x2_dram, i - B) if cross(kind) else batch_rows(x1_dram, i)
            sp.dma_start(dst, rows[:, :, :]).then_inc(rows_stored, 16)

        def place_values(sp, s, unit):
            used = [] if isinstance(s, int) and s == 0 else [(pv_done, head(s - 1, 8 * unit + 7))]
            wait_alone(sp, (v_copied, s * 2 + 2), *used)
            at = slice(unit * D // 2, (unit + 1) * D // 2)
            sp.dma_start(values[:, :, at], values_next[:, :, at]).then_inc(v_placed[unit], 16)

        def double_bias(sp, i):
            wait_alone(sp, (bias_ready, i - B + 1), (biased, i * H))
            sp.dma_start(late_bias[:, :, :], mask_bias[:, :, :]).then_inc(bias_doubled, 16)

        def load_jobs(sp, i, step, lo):
            if isinstance(i, int) and i == step:
                for m in range(lo, lo + W_RING):
                    load_job(sp, m)

        def sp_step(sp, i, kinds, nxt2):
            before2, before, kind, nxt = kinds
            stack_unit(sp, i, 1)
            if cross(kind):
                double_bias(sp, i)
            load_jobs(sp, i, 0, 16)
            load_jobs(sp, i, B - 1, 28)
            if nxt2:
                load_sources(sp, i + 2, nxt2, False)
            place_values(sp, i, 1)
            if nxt and cross(nxt):
                load_mask(sp, i + 1)
            load_jobs(sp, i, STEPS - 1, 36)
            if before:
                load_residual(sp, i - 1, before)
            load_jobs(sp, i, 0, 20)
            if nxt:
                stack_unit(sp, i + 1, 0)
            if before2:
                store_rows(sp, i - 2, before2)
            if nxt:
                place_values(sp, i + 1, 0)
            load_jobs(sp, i, 0, 24)
            load_jobs(sp, i, B - 1, 32)

        M_JOB = 40

        def m_batches(n):
            lo, hi = ((0, 7), (7, 12), (12, 14))[n]
            return lo, hi, (hi * P + S - 1) // S

        def sp_experts(sp):
            load_residual(sp, STEPS - 1, "cross")
            store_rows(sp, STEPS - 2, "cross")
            sp.wait_ge(v_full, 2 * STEPS)
            sp.wait_ge(qk_full, 4 * STEPS)
            x2_flat = x2_dram.rearrange("b s d -> (b s) d")
            for n in range(2):
                lo, hi, nb = m_batches(n)
                sp.wait_ge(rows_stored, 16 * (B + nb))
                sp.dma_start(acc[:, lo:hi, :], x2_flat[lo * P:hi * P, :].rearrange("(t p) d -> p t d", p=P)).then_inc(acc_in[n], 16)
            store_rows(sp, STEPS - 1, "cross")
            lo, hi, nb = m_batches(2)
            sp.wait_ge(rows_stored, 16 * (B + nb))
            sp.dma_start(acc[:, lo:hi, :], x2_flat[lo * P:hi * P, :].rearrange("(t p) d -> p t d", p=P)).then_inc(acc_in[2], 16)
            for r in range(3):
                sp.dma_start(be_raw[r * NE:(r + 1) * NE, :], a["expert_bias"]).then_inc(be_in, 16)
            sp.wait_ge(be_step, 3)
            sp.dma_start(be_stack[2 * NE:3 * NE, :].bitcast(F32), be_lo[0:NE, :].bitcast(F32)).then_inc(be_stacked, 16)
            with sp.Fori(0, NE // 2 - 1) as it:
                for m in range(2 * KC):
                    sp.wait_ge(w_lo["pool"], it * 2 * KC + lo_count(M_JOB - 1, "pool") - W_RING + m + 1)
                    sp.dma_start(w_raw[:, m % W_RING, :], a["experts"][it * 2 + 2 + m // KC, :, m % KC, :]).then_inc(raw_in[m % W_RING], 16)
            for g, tiles in enumerate(M_GROUPS):
                sp.wait_ge(m_normed, g + 1)
                lo, hi = tiles
                sp.dma_start(out.rearrange("b s d -> (b s) d")[lo * P:hi * P, :].rearrange("(t p) d -> p t d", p=P),
                             acc[:, lo:hi, :]).then_inc(out_stored, 16)
            sp.wait_ge(out_stored, 16 * len(M_GROUPS))

        M_GROUPS = ((0, 4), (4, 8), (8, 12), (12, 14))
        M_LN = LN_OPS - 1

        def pe_experts(pe):
            pe.wait_ge(biased, head(STEPS - 1, H - 1))
            pe.wait_ge(*copies(STEPS - 1, H - 2))
            pe.wait_ge(*copies(STEPS - 1, H - 1))
            pe.wait_ge(att_lo, 2 * STEPS)
            pe.wait_ge(rows_added, 2 * STEPS)

            def turn(t):
                if t in (0, 7, 12):
                    pe.wait_ge(acc_in[(0, 7, 12).index(t)], 16)
                if t >= 2:
                    pe.wait_ge(m_lo, t - 1)
                for c in range(KC):
                    last = nc.tensor.transpose(proj_bank[t % 2][:, c * P:c * P + P], acc[:, t, c * P:c * P + P], ident[:, :])
                last.then_inc(m_turned, 1)

            def gate(t):
                pe.wait_ge(m_lo, t + 1)
                if t == 0:
                    pe.wait_ge(gate_lo, 1)
                g = t % GT
                last = run(three_passes(turn_bank[t // GT][:, g * NE:g * NE + NE],
                                        lambda hl, c: x2t[:, hl, c, t * P:t * P + P],
                                        lambda hl, c: gate_w[:, hl, c, :]))
                if g == GT - 1:
                    last.then_inc(logits_full, 1)

            turn(0)
            for t in range(MT):
                if t + 1 < MT:
                    turn(t + 1)
                gate(t)

            def expert(q0, slot, weights_split):
                pe.wait_ge(w_lo["pool"], weights_split)
                for t in range(MT):
                    q = q0 + t
                    pe.wait_ge(combined, q + 1)
                    run(three_passes(product_bank[(slot * MT + t) % 4][:, :], lambda hl, c: x2t[:, hl, c, t * P:t * P + P],
                                     lambda hl, c: weights[EXPERT_SLOT[slot]][:, hl, c, :])).then_inc(product_full, 1)

            base = lo_count(M_JOB - 1, "pool") - 2 * KC
            with pe.Fori(0, NE // 2 - 1) as it:
                for s in range(2):
                    expert(it * 2 * MT + s * MT, s, it * 2 * KC + base + (s + 1) * KC)
            for f in range(4):
                lo, hi = 4 * f, min(4 * f + 4, MT)
                pe.wait_ge(gates_done, 2 if hi > GT else 1)
                if f >= 2:
                    pe.wait_ge(gates_copied, f - 1)
                for t in range(lo, hi):
                    last = nc.tensor.transpose(turn_bank[f % 2][0:3 * NE, (t - lo) * P:(t - lo) * P + P],
                                               gate_hl[:, t, :].bitcast(F32), ident[:, :])
                last.then_inc(gates_turned, 1)
            pe.wait_ge(gates_copied, 4)
            pe.wait_ge(be_stacked, 16)
            for t in range(MT):
                if t >= 2:
                    pe.wait_ge(bias_added, t - 1)
                nc.tensor.matmul(proj_bank[t % 2][:, :], gates_t[:, t * P:t * P + P], be_stack[:, :],
                                 start=True, stop=True).then_inc(bias_full, 1)
            for s in range(2):
                expert((NE - 2 + s) * MT, s, (NE // 2 - 1) * 2 * KC + base + (s + 1) * KC)

        def act_experts(act):
            act.wait_ge(o_full, 2 * STEPS)
            for t in range(MT):
                act.wait_ge(m_turned, t + 1)
                nc.scalar.activation(x2t[:, 0, :, t * P:t * P + P], proj_bank[t % 2][:, :].rearrange("p (c n) -> p c n", c=KC),
                                     ACT.Copy).then_inc(m_hi, 1)
                if t in (9, MT - 1):
                    g = 0 if t == 9 else 1
                    act.wait_ge(pair_diff, g + 1)
                    nc.scalar.activation(pair_w[:, 1, g * GT:g * GT + GT], pair_w[:, 0, g * GT:g * GT + GT],
                                         ACT.Exp).then_inc(pair_exp, 1)
            with act.Fori(0, NE // 2 - 1) as it:
                for m in range(2 * KC):
                    c, s = m % KC, m // KC
                    act.wait_ge(raw_in[m % W_RING], it * 32 + 16 * (M_JOB // W_RING + m // W_RING + 1))
                    if c == 0:
                        act.wait_ge(product_full, it * 2 * MT + (s + 1) * MT)
                    nc.scalar.activation(weights[EXPERT_SLOT[s]][:, 0, c, :], w_raw[:, m % W_RING, :], ACT.Copy).then_inc(w_hi, 1)
            for f in range(4):
                lo, hi = 4 * f, min(4 * f + 4, MT)
                act.wait_ge(gates_turned, f + 1)
                nc.scalar.activation(gates_t[:, lo * P:hi * P], turn_bank[f % 2][0:3 * NE, 0:(hi - lo) * P],
                                     ACT.Copy).then_inc(gates_copied, 1)
            for g, (lo, hi) in enumerate(M_GROUPS):
                act.wait_ge(m_ln, (g + 1) * M_LN)
                for t in range(lo, hi):
                    last = nc.scalar.activation(acc[:, t, :], acc[:, t, :], ACT.Identity,
                                                bias=m_shift[:, t:t + 1], scale=m_rstd[:, t:t + 1])
                last.then_inc(m_normed, 1)

        def pool_experts(pool):
            with pool.Fori(0, NE // 2 - 1) as it:
                for m in range(2 * KC):
                    c, s = m % KC, m // KC
                    pool.wait_ge(w_hi, it * 2 * KC + M_JOB + m + 1)
                    w = weights[EXPERT_SLOT[s]]
                    nc.gpsimd.tensor_tensor(w[:, 1, c, :], w_raw[:, m % W_RING, :], w[:, 0, c, :],
                                            ALU.subtract).then_inc(w_lo["pool"], 1)

        def dve_experts(dve):
            def split(t):
                dve.wait_ge(m_hi, t + 1)
                nc.vector.tensor_tensor(x2t[:, 1, :, t * P:t * P + P], proj_bank[t % 2][:, :].rearrange("p (c n) -> p c n", c=KC),
                                        x2t[:, 0, :, t * P:t * P + P], ALU.subtract).then_inc(m_lo, 1)

            links = [0]

            def link(instruction):
                links[0] += 1
                instruction.then_inc(gate_step, 1)
                dve.wait_ge(gate_step, links[0])

            def spread(x, n):
                return x.rearrange("p (a b) -> p a b", b=1).broadcast_to((P, GT, n))

            def gate_first(g):
                tiles = slice(g * GT, g * GT + GT)
                dve.wait_ge(logits_full, g + 1)
                link(nc.vector.tensor_tensor(
                    logits[:, tiles, :], turn_bank[g][:, 0:GT * NE].rearrange("p (t e) -> p t e", t=GT),
                    gate_bias[:, :].rearrange("p (a e) -> p a e", a=1).broadcast_to((P, GT, NE)), ALU.add))
                for t in range(g * GT, g * GT + GT):
                    last = nc.vector.max(top[:, t, :], logits[:, t, :])
                link(last)
                nc.vector.tensor_tensor(pair_w[:, 0, tiles], top[:, tiles, 1], top[:, tiles, 0],
                                        ALU.subtract).then_inc(pair_diff, 1)
                for t in range(g * GT, g * GT + GT):
                    last = nc.vector.max_index(top_at[:, t, :], top[:, t, :], logits[:, t, :])
                link(last)
                link(nc.vector.tensor_copy(top_f[:, tiles, :], top_at[:, tiles, 0:2]))

            def gate_second(g):
                tiles = slice(g * GT, g * GT + GT)
                dve.wait_ge(pair_exp, g + 1)
                link(nc.vector.tensor_scalar(pair_w[:, 3, tiles], pair_w[:, 1, tiles], 1.0, None, ALU.add))
                link(nc.vector.reciprocal(pair_w[:, 2, tiles], pair_w[:, 3, tiles]))
                link(nc.vector.tensor_tensor(pair_w[:, 3, tiles], pair_w[:, 1, tiles], pair_w[:, 2, tiles], ALU.mult))
                every = iota[:, :].rearrange("p (a e) -> p a e", a=1).broadcast_to((P, GT, NE))
                for k in range(2):
                    link(nc.vector.tensor_tensor(one_hot[:, k, tiles, :], every, spread(top_f[:, tiles, k], NE), ALU.is_equal))
                    link(nc.vector.tensor_tensor(one_hot[:, k, tiles, :], one_hot[:, k, tiles, :],
                                                 spread(pair_w[:, 2 + k, tiles], NE), ALU.mult))
                link(nc.vector.tensor_tensor(gates[:, tiles, :], one_hot[:, 0, tiles, :], one_hot[:, 1, tiles, :], ALU.add))
                nc.vector.tensor_copy(gate_hl[:, tiles, 0:NE], gates[:, tiles, :])
                link(nc.vector.tensor_copy(gate_hl[:, tiles, 2 * NE:3 * NE], gates[:, tiles, :]))
                nc.vector.tensor_tensor(gate_hl[:, tiles, NE:2 * NE], gates[:, tiles, :], gate_hl[:, tiles, 0:NE],
                                        ALU.subtract).then_inc(gates_done, 1)

            for t in range(MT):
                split(t)
                if t == 8:
                    gate_first(0)
                if t == 10:
                    gate_second(0)
            dve.wait_ge(be_in, 48)
            nc.vector.tensor_copy(be_lo[:, :], be_raw[:, :]).then_inc(be_step, 1)
            dve.wait_ge(be_step, 1)
            nc.vector.tensor_copy(be_stack[:, :], be_lo[:, :]).then_inc(be_step, 1)
            dve.wait_ge(be_step, 2)
            nc.vector.tensor_tensor(be_lo[:, :], be_raw[:, :], be_stack[:, :], ALU.subtract).then_inc(be_step, 1)
            gate_first(1)
            gate_second(1)
            dve.wait_ge(gates_done, 2)
            nc.vector.memset(pair_w[:, 0, 0:1], 0.0).then_inc(combined, 4)

            def combine(q, t, bank_at, gate_at):
                dve.wait_ge(product_full, q + 1)
                dve.wait_ge(combined, q + 4)
                return nc.vector.scalar_tensor_tensor(acc[:, t, :], product_bank[bank_at][:, :], gate_at, acc[:, t, :],
                                                      ALU.mult, ALU.add)

            with dve.Fori(0, NE // 2 - 1) as it:
                for s in range(2):
                    for t in range(MT):
                        combine(it * 2 * MT + s * MT + t, t, (s * MT + t) % 4,
                                gates[:, t, bass.ds(it * 2 + s, 1)]).then_inc(combined, 1)
            for t in range(MT):
                dve.wait_ge(bias_full, t + 1)
                nc.vector.tensor_tensor(acc[:, t, :], proj_bank[t % 2][:, :], acc[:, t, :], ALU.add).then_inc(bias_added, 1)
            dve.wait_ge(bias_added, MT)
            steps = [0]

            def ln_link(instruction):
                steps[0] += 1
                instruction.then_inc(m_ln, 1)
                dve.wait_ge(m_ln, steps[0])

            for s in range(2):
                e = NE - 2 + s
                for t in range(MT):
                    combine(e * MT + t, t, (s * MT + t) % 4, gates[:, t, e:e + 1]).then_inc(combined, 1)
                    if s == 1:
                        dve.wait_ge(combined, e * MT + t + 5)
                        nc.vector.bn_stats(m_stats[:, t, :], acc[:, t, :]).then_inc(m_measured, 1)
                        for g, (lo, hi) in enumerate(M_GROUPS):
                            if t == hi - 1:
                                dve.wait_ge(m_measured, hi)
                                for u in range(lo, hi):
                                    last = nc.vector.bn_aggr(m_mean_var[:, u, :], m_stats[:, u, :])
                                ln_link(last)
                                ln_link(nc.vector.tensor_scalar(m_var[:, lo:hi], m_mean_var[:, lo:hi, 1], EPS, None, ALU.add))
                                for op in rsqrt_ops(m_var[:, lo:hi], m_mean_var[:, lo:hi, 0], m_rstd[:, lo:hi],
                                                    m_newton[:, lo:hi], m_shift[:, lo:hi]):
                                    ln_link(op())

        block = ctx.enter_context(nc.Block())

        def steps(engine, step):
            s, c = "self", "cross"
            step(0, (None, None, s, s), s)
            step(1, (None, s, s, s), s)
            step(2, (s, s, s, s), s)
            with engine.Fori(3, B - 2) as i:
                step(i, (s, s, s, s), s)
            step(B - 2, (s, s, s, s), c)
            step(B - 1, (s, s, s, c), c)
            step(B, (s, s, c, c), c)
            step(B + 1, (s, c, c, c), c)
            with engine.Fori(B + 2, STEPS - 2) as i:
                step(i, (c, c, c, c), c)
            step(STEPS - 2, (c, c, c, c), None)
            step(STEPS - 1, (c, c, c, None), None)

        @block.sync
        def _(sp):
            load_sources(sp, 0, "self", True)
            sp.dma_start(ident[:, :], a["ident"]).then_inc(ident_in, 16)
            for m in range(4):
                load_job(sp, m)
            for dst, src in ((qkv_bias[:, 0, :], a["bq"]), (qkv_bias[:, 1, :], a["bk"]), (qkv_bias[:, 2, :], a["bv"])):
                sp.dma_start(dst, src).then_inc(consts_in, 16)
            for m in range(4, 8):
                load_job(sp, m)
            sp.dma_start(late_bias[:, :, :], a["prior"].rearrange("(t p) k -> p t k", p=T)).then_inc(consts_in, 16)
            sp.dma_start(lam[:, :], a["lam"].broadcast_to((T, 1))).then_inc(consts_in, 16)
            for n, name in enumerate(("bo", "b_out")):
                sp.dma_start(out_bias[:, n, :], a[name].rearrange("(a d) -> a d", a=1).broadcast_to((T, D))).then_inc(consts_in, 16)
            sp.dma_start(gate_raw[:, :, :], a["gate"]).then_inc(gate_in, 16)
            sp.dma_start(gate_bias[:, :], a["gate_bias"].rearrange("(a d) -> a d", a=1).broadcast_to((P, NE))).then_inc(gate_in, 16)
            sp.dma_start(iota[:, :], a["iota"].rearrange("(a d) -> a d", a=1).broadcast_to((P, NE))).then_inc(gate_in, 16)
            load_sources(sp, 1, "self", False)
            for m in range(8, 12):
                load_job(sp, m)
            stack_unit(sp, 0, 0)
            for m in range(12, 16):
                load_job(sp, m)
            place_values(sp, 0, 0)
            steps(sp, lambda i, kinds, nxt2: sp_step(sp, i, kinds, nxt2))
            sp_experts(sp)

        @block.gpsimd
        def _(pool):
            pool.wait_ge(consts_in, 16 * 7)
            nc.gpsimd.tensor_scalar(late_bias[:, :, :], late_bias[:, :, :], lam[:, 0:1], ROOT, ALU.mult, ALU.mult).then_inc(prior_ready, 1)
            steps(pool, lambda i, kinds, nxt2: pool_step(pool, i, kinds))
            pool_residual(pool, STEPS - 1, "cross")
            pool_experts(pool)

        @block.scalar
        def _(act):
            for f in range(2):
                fill_done(act, -1, "self", "x", f, True)
            for m in range(0, 8):
                act_weight_hi(act, m)
            act.wait_ge(consts_in, 16 * 7)
            fill_done(act, -1, "self", "p", 0, True)
            fill_done(act, -1, "self", "p", 1, True)
            for m in range(8, 12):
                act_weight_hi(act, m)
            act.wait_ge(gate_in, 48)
            nc.scalar.activation(gate_w[:, 0, :, :], gate_raw[:, :, :], ACT.Copy).then_inc(gate_hi, 1)
            for t in range(NT):
                fill_done(act, -1, "self", "v", t, True)
            fill_done(act, -1, "self", "p", 2, True)
            fill_done(act, -1, "self", "p", 3, True)
            for m in range(12, 16):
                act_weight_hi(act, m)
            steps(act, lambda i, kinds, nxt2: act_step(act, i, kinds))
            act_norm_rows(act, STEPS - 1)
            act_experts(act)

        @block.vector
        def _(dve):
            for f in range(2):
                fill_done(dve, -1, "self", "x", f, False)
            for m in range(0, 8):
                weight_lo(dve, m, "dve")
            dve.wait_ge(consts_in, 16 * 7)
            fill_done(dve, -1, "self", "p", 0, False)
            fill_done(dve, -1, "self", "p", 1, False)
            for m in range(8, 12):
                weight_lo(dve, m, "dve")
            dve.wait_ge(gate_hi, 1)
            nc.vector.tensor_tensor(gate_w[:, 1, :, :], gate_raw[:, :, :], gate_w[:, 0, :, :], ALU.subtract).then_inc(gate_lo, 1)
            fill_done(dve, -1, "self", "p", 2, False)
            for m in range(12, 16):
                weight_lo(dve, m, "dve")
            dve.wait_ge(prior_ready, 1)
            steps(dve, lambda i, kinds, nxt2: dve_step(dve, i, kinds))
            for t in range(NT):
                dve_add_rows(dve, STEPS - 1, t)
            for k in range(LN_OPS):
                dve_ln_op(dve, STEPS - 1, k)
            dve_experts(dve)

        @block.tensor
        def _(pe):
            pe.wait_ge(ident_in, 16)
            for what, f, m, _ in fill_pieces("self", False):
                pe_piece(pe, -1, (None, None, None, "self"), (what, f, m))
            pe_scores(pe, 0, "self", 0)
            steps(pe, lambda i, kinds, nxt2: pe_step(pe, i, kinds))
            for h in range(4):
                for m in range(6):
                    pe_output_piece(pe, STEPS - 1, "cross", h, m, (rows_added, 2 * STEPS - 3))
            pe_experts(pe)


def _prior(np):
    at = np.arange(S, dtype=np.float32)
    delta = np.abs(at[:, None] - at[None, :])
    total = np.zeros_like(delta)
    for p, w, sigma in zip((1.0, 30.0), (0.8, 0.4), (0.5, 2.0)):
        total = total + np.float32(w) * np.exp(-(delta - np.float32(p)) ** 2 / np.float32(2.0 * sigma ** 2))
    return total.astype(np.float32)


def kernel(**inputs):
    import numpy as np
    import concourse.bacc as bacc
    from concourse.bass_utils import run_bass_kernel_spmd

    def chunks(w):
        return np.ascontiguousarray(np.asarray(w).T.reshape(KC, P, -1).transpose(1, 0, 2))

    def columns(b):
        return np.ascontiguousarray(np.asarray(b).reshape(KC, P).T)

    arrays = {
        "x": inputs["x"], "context": inputs["ctx_1024"],
        "mask": inputs["mask_BxSxS2_bf0"],
        "self_q": chunks(inputs["L0_attn_Wq"]), "self_k": chunks(inputs["L0_attn_Wk"]),
        "self_v": chunks(inputs["L0_attn_Wv"]), "self_o": chunks(inputs["L0_attn_Wo"]),
        "cross_q": chunks(inputs["L0_xattn_Wq"]), "cross_k": chunks(inputs["L0_xattn_Wk"]),
        "cross_v": chunks(inputs["L0_xattn_Wv"]), "cross_o": chunks(inputs["L0_xattn_Wout"]),
        "bq": columns(inputs["L0_attn_bq"]), "bk": columns(inputs["L0_attn_bk"]), "bv": columns(inputs["L0_attn_bv"]),
        "bo": inputs["L0_attn_bo"], "b_out": inputs["L0_xattn_b_out"],
        "lam": np.asarray(inputs["L0_attn_prior_lambda"]).reshape(1, 1),
        "experts": np.stack([chunks(w) for w in np.asarray(inputs["L0_ffn_We"])]),
        "expert_bias": inputs["L0_ffn_be"], "gate": chunks(inputs["L0_ffn_Wg"]), "gate_bias": inputs["L0_ffn_bg"],
        "ident": np.eye(P, dtype=np.float32), "iota": np.arange(NE, dtype=np.float32), "prior": _prior(np),
    }
    nc = bacc.Bacc("TRN2", target_bir_lowering=False, num_devices=1)
    named, aps = {}, {}
    for name, value in arrays.items():
        value = np.ascontiguousarray(value)
        named[f"in_{name}"] = value
        aps[name] = nc.dram_tensor(f"in_{name}", value.shape, mybir.dt.from_np(value.dtype), kind="ExternalInput").ap()
    out = nc.dram_tensor("out_rows", (B, S, D), F32, kind="ExternalOutput").ap()
    decoder_layer(nc, aps, out)
    result = run_bass_kernel_spmd(nc, [named], core_ids=[0])
    return result.results[0]["out_rows"]
```

```python
from contextlib import ExitStack

import concourse.bass as bass
from concourse import mybir

F32 = mybir.dt.float32
F32R = mybir.dt.float32r
I32 = mybir.dt.int32
U32 = mybir.dt.uint32
U8 = mybir.dt.uint8
BF16 = mybir.dt.bfloat16
ALU = mybir.AluOpType
ACT = mybir.ActivationFunctionType

B, S, D = 8, 224, 512
H, HD = 16, 32
NE, TOP = 8, 8
P = 128
KC = D // P
HC = P // HD
T = 112
NT = S // T
STEPS = 2 * B
TOKENS = B * S
MT = TOKENS // P
ST = 2 * TOKENS // P + NE - 1
EARLY = 8
GROUPS = ((0, EARLY), (EARLY, MT))
FOURS = ((0, 4), (4, 8), (8, 12), (12, 14))
LOADS = ((0, 4), (4, 8), (8, 10), (10, 12), (12, 14))
ROOT = float(HD) ** 0.5
SCALE = 1.0 / ROOT
EPS = 1e-5
MASKED = -1.0e30
HIGHEST_SHIFT = -MASKED * SCALE * 1e-3
RSQRT_MAGIC = float(0x5F3759DF)

LT, LC, LV = 3, 4, 5
DRAIN = H + LV
P_RING = 4
TURN_SLOTS = {"self": {("x", 0): 0, ("x", 1): 1},
              "cross": {("c", 0): 0, ("c", 1): 1, ("x", 0): 1, ("x", 1): 2}}
OUT_SLOTS = (2, 5)
ATT_SLOT = (3, 5)
STACK_DMAS = 12
LN_OPS = 15

SELF_SLOT = {"k": 1, "q": 0, "v": 2, "o": 3}
CROSS_SLOT = {"k": 4, "q": 0, "v": 5, "o": 1}
EXPERT = 6


def weight_jobs():
    jobs = []
    for m, slot, eng in (("self_k", 1, "dve"), ("self_q", 0, "dve"), ("self_v", 2, "dve"), ("self_o", 3, "dve"),
                         ("cross_k", 4, "pool"), ("cross_v", 5, "pool"), ("cross_q", 0, "dve"),
                         ("cross_o", 1, "pool"), ("e0", EXPERT, "pool"), ("e1", EXPERT + 1, "pool")):
        jobs += [(m, c, slot, eng) for c in range(KC)]
    return jobs + [(f"e{e}", c, EXPERT + e, "dve") for e in range(2, NE) for c in range(KC)]


JOBS = weight_jobs()
JOBS_AT = {}
for _c in range(8):
    JOBS_AT[(0, 6 + _c)] = [16 + _c]
for _c in range(4):
    JOBS_AT.setdefault((B - 1, 4 + _c // 2), []).append(24 + _c)
    JOBS_AT[(B - 1, 8 + _c)] = [28 + _c]
for _c in range(8):
    JOBS_AT[(STEPS - 2, 5 + _c)] = [32 + _c]


def fill_pieces(nxt, with_output):
    pieces = []
    if nxt:
        for what in ("c", "x") if nxt == "cross" else ("x",):
            pieces += [(what, f, 0, 4 * T) for f in range(2)]
    if with_output:
        pieces += [("o", h, m, D) for h in range(4) for m in range(6)]
    if nxt:
        pieces += [("p", f, m, S) for f in range(2) for m in range(24)]
        pieces += [("v", t, m, D) for t in range(NT) for m in range(12)]
        pieces += [("p", f, m, S) for f in range(2, 4) for m in range(24)]
    return pieces


def fill_slots(nxt, with_output):
    pieces = fill_pieces(nxt, with_output)
    slots, end = [[] for _ in range(H)], {}
    rest = [p for p in pieces if p[0] in ("p", "v")]
    total, done = sum(p[3] for p in rest), 0
    first = OUT_SLOTS[1] if with_output else OUT_SLOTS[0]
    for what, f, m, cost in pieces:
        if what in ("c", "x"):
            n = TURN_SLOTS[nxt][(what, f)]
        elif what == "o":
            n = OUT_SLOTS[0] + (f * 6 + m) * (OUT_SLOTS[1] - OUT_SLOTS[0]) // 24
        else:
            n = first + done * (H - first) // total
            done += cost
        slots[n].append((what, f, m))
        end[(what, f)] = n
    return slots, end


def last_fill_slots():
    slots, end = [[] for _ in range(H)], {}
    for what, first in (("o", 0), ("O", 10)):
        for h in range(4):
            for m in range(6):
                slots[first + h].append((what, h, m))
            end[(what, h)] = first + h
    for t in range(EARLY):
        end[("t", t)] = 5 + t // 2
    for g in range(2):
        end[("l", g)] = 14 + g
    for (what, f), n in end.items():
        if what in ("t", "l"):
            slots[n].append((what, f, 0))
    return slots, end


def schedule(nxt, with_output):
    slots, end = fill_slots(nxt, with_output) if nxt else last_fill_slots()
    assert not nxt or end[("p", 3)] == H - 1
    return slots, end


def leaves_at(end, n):
    return [fill for fill, slot in end.items() if slot == n]


def load_count(job):
    return sum(j[1:3] == JOBS[job][1:3] for j in JOBS[:job + 1])


def lo_count(job, eng):
    return sum(JOBS[m][3] == eng for m in range(job + 1))


def decoder_layer(nc, a, out):
    with ExitStack() as ctx:
        def sb(name, shape, dt=F32, stack=ctx):
            return stack.enter_context(nc.sbuf_tensor(name, shape, dt))

        def sem(name):
            return ctx.enter_context(nc.semaphore(name))

        x1_dram = nc.dram_tensor("x1_rows", (B, S, D), F32).ap()
        x2_dram = nc.dram_tensor("x2_rows", (B, S, D), F32).ap()
        sorted_dram = nc.dram_tensor("sorted_rows", (ST * P, D), F32).ap()
        products_dram = nc.dram_tensor("product_rows", (ST * P, D), F32).ap()

        raw_weights = {}

        def weight_slot(s, stack):
            with ExitStack() as raw:
                raw_weights[s] = sb(f"raw_weights{s}", [P, 2, KC, D], F32, raw)
            return sb(f"weights{s}", [P, 2, KC, D], F32R, stack)

        ident = sb("ident", [P, P])
        qkv_bias = sb("qkv_bias", [P, 3, KC])
        late_bias = sb("late_bias", [T, NT, S])
        lam = sb("lam", [T, 1])
        mask_u8 = sb("mask_u8", [T, NT, S], U8)
        mask_bias = sb("mask_bias", [T, NT, S])
        out_bias = sb("out_bias", [T, 2, D])
        residual = sb("residual", [T, NT, D])
        rows = sb("rows", [T, NT, D])
        stats = sb("stats", [T, NT, 6])
        mean_var = sb("mean_var", [T, NT, 2])
        var_eps = sb("var_eps", [T, NT])
        rstd = sb("rstd", [T, NT])
        newton = sb("newton", [T, NT])
        neg_mean_rstd = sb("neg_mean_rstd", [T, NT])
        neg_max = sb("neg_max", [T, P_RING, NT])
        row_sum = sb("row_sum", [T, P_RING, NT])
        recip = sb("recip", [T, P_RING, NT])
        gate_raw = sb("gate_raw", [P, KC, NE])
        gate_w = sb("gate_w", [P, 2, KC, NE], F32R)
        gate_bias = sb("gate_bias", [P, NE])
        iota = sb("iota", [P, NE])

        attn = ExitStack()
        weights = {s: weight_slot(s, attn) for s in (2, 3)}
        weights[1] = weight_slot(1, attn)
        attended = sb("attended", [P, 2, KC, S], F32R, attn)
        stacks = [sb(f"stack{w}", [3 * HD, HC, 2, 2 * S], F32R, attn) for w in range(2)]
        probs = sb("probs", [T, P_RING, NT, S], F32, attn)
        probs_t = sb("probs_t", [T, 2, NT * S], F32, attn)
        values = sb("values", [T, NT, D], F32, attn)
        values_next = sb("values_next", [T, NT, D], F32, attn)
        qk = sb("qk", [P, 4, 2 * S], F32R, attn)
        nat_x = sb("nat_x", [T, NT, D], F32, attn)
        nat_c = sb("nat_c", [T, NT, D], F32, attn)
        src_x = sb("src_x", [P, 2, KC, S], F32R, attn)
        src_c = sb("src_c", [P, 2, KC, S], F32R, attn)
        for s in (4, 5, 0):
            weights[s] = weight_slot(s, attn)
        attn.close()

        turning = ExitStack()
        slot_size = 2 * KC * D
        used_late = (3 * slot_size + 2 * KC * S + 2 * HC * 2 * 2 * S
                     + P_RING * NT * S + 2 * NT * S + 2 * NT * D)
        sb("before_ring", [P, used_late], F32, turning)
        x2t = sb("x2t", [P, EARLY, 2, KC, P], F32R, turning)
        turning.close()
        with ExitStack() as raw:
            raw_experts = [sb(f"raw_expert{e}", [P, 2, KC, D], F32, raw) for e in range(NE)]
        with ExitStack() as gathered_tiles:
            gathered = sb("gathered", [P, MT, 2, D], F32, gathered_tiles)
        moe = ctx.enter_context(ExitStack())
        experts = sb("experts", [P, NE, 2, KC, D], F32R, moe)
        y_out = sb("y_out", [P, 2, D], F32, moe)
        sb("behind_ring", [P, used_late + EARLY * 2 * D - NE * slot_size - 2 * D], F32, moe)
        acc = sb("acc", [P, MT, D], F32, moe)
        with ExitStack() as biases:
            be_raw = sb("be_raw", [3 * NE, D], F32, biases)
            be_lo = sb("be_lo", [3 * NE, D], F32R, biases)
            be_stack = sb("be_stack", [3 * NE, D], F32R, biases)
            with ExitStack() as first:
                logits_t = sb("logits_t", [NE, TOKENS], F32, first)
            gates_t = sb("gates_t", [3 * NE, TOKENS], F32R, biases)
        rows_x = sb("rows_x", [P, 2, D], F32, moe)
        xt = sb("xt", [P, 2, 2, KC, P], F32R, moe)
        sb("behind_biases", [P, 3 * D + TOKENS - 6 * D], F32, moe)
        logits = sb("logits", [P, MT, NE], F32, moe)
        top = sb("top", [P, MT, TOP], F32, moe)
        top_at = sb("top_at", [P, MT, TOP], U32, moe)
        top_f = sb("top_f", [P, MT, 2], F32, moe)
        pair_w = sb("pair_w", [P, 4, MT], F32, moe)
        hot = sb("hot", [P, 2, MT, NE], F32, moe)
        weighted = sb("weighted", [P, 2, MT, NE], F32, moe)
        chosen = sb("chosen", [P, MT * NE], BF16, moe)
        place_of = sb("place_of", [P, MT * NE], F32, moe)
        place_f = sb("place_f", [P, 2 * MT], F32, moe)
        place = sb("place", [P, 2 * MT], I32, moe)
        whole = sb("whole", [P, NE], I32, moe)
        ends = [sb(f"ends{n}", [P, 2 * NE], F32, moe) for n in range(2)]
        ended = sb("ended", [1, ST, NE], F32, moe)
        expert_f = sb("expert_f", [1, ST], F32, moe)
        expert_of = sb("expert_of", [1, ST], I32, moe)
        tile_iota = sb("tile_iota", [1, ST], F32, moe)
        tables_f = sb("tables_f", [P, 2, P], F32, moe)
        before = sb("before", [P, P], BF16, moe)
        ones = sb("ones", [P, P], BF16, moe)
        gates = sb("gates", [P, MT, NE], F32, moe)
        gate_hl = sb("gate_hl", [P, MT, 3 * NE], F32R, moe)
        m_stats = sb("m_stats", [P, MT, 6], F32, moe)
        m_mean_var = sb("m_mean_var", [P, MT, 2], F32, moe)
        m_var = sb("m_var", [P, MT], F32, moe)
        m_rstd = sb("m_rstd", [P, MT], F32, moe)
        m_newton = sb("m_newton", [P, MT], F32, moe)
        m_shift = sb("m_shift", [P, MT], F32, moe)

        def bank(name):
            return ctx.enter_context(nc.psum_tensor(name, [P, 512], F32))

        score_bank = [bank(f"score_bank{n}") for n in range(2)]
        turn_bank = [bank(f"turn_bank{n}") for n in range(2)]
        value_bank = [bank(f"value_bank{n}") for n in range(2)]
        proj_bank = [bank(f"proj_bank{n}") for n in range(2)]

        ident_in = sem("ident_in")
        consts_in = sem("consts_in")
        gate_in = sem("gate_in")
        raw_in = [[sem(f"raw_in{slot}_{c}") for c in range(KC)] for slot in range(EXPERT)]
        expert_in = [sem(f"expert_in{e}") for e in range(NE)]
        w_hi = sem("w_hi")
        w_lo = {"dve": sem("w_lo_dve"), "pool": sem("w_lo_pool")}
        x_in, c_in, mask_in, residual_in = sem("x_in"), sem("c_in"), sem("mask_in"), sem("residual_in")
        x_turned, x_hi, x_lo = sem("x_turned"), sem("x_hi"), sem("x_lo")
        c_turned, c_hi, c_lo = sem("c_turned"), sem("c_hi"), sem("c_lo")
        qk_full, qk_hi, qk_lo = sem("qk_full"), sem("qk_hi"), sem("qk_lo")
        stacked = [sem("stacked0"), sem("stacked1")]
        v_full, v_copied = sem("v_full"), sem("v_copied")
        v_placed = [sem("v_placed0"), sem("v_placed1")]
        prior_ready, bias_scaled, bias_ready = sem("prior_ready"), sem("bias_scaled"), sem("bias_ready")
        bias_doubled = sem("bias_doubled")
        scored, biased, exp_done = sem("scored"), sem("biased"), sem("exp_done")
        sum_kept, recip_ready, normed = sem("sum_kept"), sem("recip_ready"), sem("normed")
        turned, copied_dve, copied_act, pv_done = sem("turned"), sem("copied_dve"), sem("copied_act"), sem("pv_done")
        att_hi, att_lo, att_half_read = sem("att_hi"), sem("att_lo"), sem("att_half_read")
        o_full, residual_ready, rows_added = sem("o_full"), sem("residual_ready"), sem("rows_added")
        ln_step, rows_normed, rows_stored = sem("ln_step"), sem("rows_normed"), sem("rows_stored")
        acc_in = [sem(f"acc_in{n}") for n in range(len(LOADS))]
        be_in, be_step, be_stacked = sem("be_in"), sem("be_step"), sem("be_stacked")
        m_turned, m_hi, m_lo = sem("m_turned"), sem("m_hi"), sem("m_lo")
        gate_hi, gate_lo = sem("gate_hi"), sem("gate_lo")
        logits_full, logits_copied, logits_turned, logits_added = (
            sem("logits_full"), sem("logits_copied"), sem("logits_turned"), sem("logits_added"))
        gate_step, pair_diff, pair_exp = sem("gate_step"), sem("pair_diff"), sem("pair_exp")
        gates_done, gates_turned, gates_copied = sem("gates_done"), sem("gates_turned"), sem("gates_copied")
        product_full = sem("product_full")
        filler_in, chosen_ready, ranked, ends_ready = sem("filler_in"), sem("chosen_ready"), sem("ranked"), sem("ends_ready")
        placed, tables_in = sem("placed"), sem("tables_in")
        scattered = [sem(f"scattered{t}") for t in range(MT)]
        rows_in = [sem("rows_in0"), sem("rows_in1")]
        y_copied, y_stored = sem("y_copied"), [sem("y_stored0"), sem("y_stored1")]
        gathered_in, added = [sem(f"gathered_in{t}") for t in range(MT)], sem("added")
        bias_full, bias_added = sem("bias_full"), sem("bias_added")
        m_measured, m_ln, m_normed, out_stored = sem("m_measured"), sem("m_ln"), sem("m_normed"), sem("out_stored")

        def head(i, n):
            return i * H + n + 1

        def copies(i, n):
            if n < 0:
                i, n = i - 1, n + H
            if n % 4 == 3:
                return copied_act, i * (H // 4) + n // 4 + 1
            return copied_dve, i * (H - H // 4) + n - n // 4 + 1

        def wait_alone(eng, *waits):
            waits = [(semaphore, value if isinstance(value, int) else eng.snap(eng.to_reg(value)))
                     for semaphore, value in waits]
            eng.wait_ge(ident_in, 16)
            for semaphore, value in waits:
                eng.wait_ge(semaphore, value)

        def cross(kind):
            return kind == "cross"

        def key_tiles(kind, qt):
            return qt + 1 if cross(kind) else NT

        def turned_at(kind, qt, kt):
            if cross(kind) and kt == 1:
                return S
            return kt * S + qt * T

        def turned_cols(kind):
            return S + T if cross(kind) else NT * S

        def slots_of(kind):
            return CROSS_SLOT if cross(kind) else SELF_SLOT

        def sources(kind):
            return (src_x, src_c) if cross(kind) else (src_x, src_x)

        def projection_bias(kind, what, c):
            return qkv_bias[:, {"q": 0, "k": 1, "v": 2}[what], c:c + 1]

        FILLS = (("k", 0), ("q", 0), ("k", 1), ("q", 1))
        PLANE = {"q": 0, "k": 2}

        def three_passes(ps, stationary, moving):
            steps = [(sl, ml, c) for c in range(KC) for sl, ml in ((0, 0), (0, 1), (1, 0))]
            return [(ps, stationary(sl, c), moving(ml, c), n == 0, n == len(steps) - 1)
                    for n, (sl, ml, c) in enumerate(steps)]

        def run(matmuls):
            last = None
            for ps, lhs, rhs, first, end in matmuls:
                last = nc.tensor.matmul(ps, lhs, rhs, start=first, stop=end)
            return last

        def projection(kind, f):
            what, unit = FILLS[f]
            w = weights[slots_of(kind)[what]]
            src = sources(kind)[0 if what == "q" else 1]
            found = []
            for cc in range(2):
                o = P * (2 * unit + cc)
                found += three_passes(proj_bank[f % 2][:, cc * S:cc * S + S],
                                      lambda hl, c: w[:, hl, c, o:o + P], lambda hl, c: src[:, hl, c, :])
            return found

        def pe_turn_source(pe, s, kind, what, f):
            if what == "c":
                nat, done = nat_c, c_turned
                if f == 0:
                    pe.wait_ge(c_in, (s - B) * 16 + 16)
            else:
                nat, done = nat_x, x_turned
                if f == 0:
                    pe.wait_ge(x_in, s * 16 + 16)
            if what == "x" and cross(kind):
                pe.wait_ge(c_lo, (s - B) * 2 + f + 1)
            elif not (isinstance(s, int) and s == 0):
                pe.wait_ge(qk_lo, s * 4 - 1 + f)
            for cc in range(2):
                for t in range(NT):
                    last = nc.tensor.transpose(proj_bank[f % 2][:, cc * S + t * T:cc * S + t * T + T],
                                               nat[:, t, (2 * f + cc) * P:(2 * f + cc + 1) * P], ident[0:T, 0:T])
            last.then_inc(done, 1)

        def pe_projection_piece(pe, s, kind, f, at):
            if at == 0:
                if f < 2:
                    if FILLS[f][0] == "k" and cross(kind):
                        pe.wait_ge(c_lo, (s - B) * 2 + 2)
                    pe.wait_ge(x_lo, s * 2 + 2)
                    pe_wait_weights(pe, kind, FILLS[f][0], s)
                    if not isinstance(s, int) or s >= 3:
                        pe.wait_ge(rows_added, (s - 3) * 2 + f + 1)
                else:
                    pe.wait_ge(v_copied, s * 2 + f - 1)
            last = run(projection(kind, f)[at:at + 1])
            if at == 23:
                last.then_inc(qk_full, 1)

        def pe_wait_weights(pe, kind, what, s):
            first = {("self", "k"): 0, ("self", "q"): 0, ("self", "v"): 0, ("self", "o"): 0,
                     ("cross", "k"): B, ("cross", "q"): B, ("cross", "v"): B, ("cross", "o"): B}[(kind, what)]
            if isinstance(s, int) and s == first:
                job = max(m for m, j in enumerate(JOBS) if j[0] == f"{kind}_{what}")
                pe.wait_ge(w_lo[JOBS[job][3]], lo_count(job, JOBS[job][3]))

        def value_fill(kind, t):
            w = weights[slots_of(kind)["v"]]
            src = sources(kind)[1]
            return three_passes(proj_bank[t][0:T, :], lambda hl, c: src[:, hl, c, t * T:t * T + T],
                                lambda hl, c: w[:, hl, c, :])

        def pe_value_piece(pe, s, kind, t, at):
            if at == 0:
                if t == 0:
                    pe_wait_weights(pe, kind, "v", s)
                pe.wait_ge(qk_lo, s * 4 + t + 1)
            last = run(value_fill(kind, t)[at:at + 1])
            if at == 11:
                last.then_inc(v_full, 1)

        def pe_scores(pe, i, kind, n):
            unit, slot = divmod(n, 8)
            c, j = divmod(slot, HC)
            st, o = stacks[unit], c * S
            if slot == 0:
                pe.wait_ge(stacked[unit], i * 16 * STACK_DMAS + 16 * STACK_DMAS)
            if not (isinstance(i, int) and i == 0 and n < 2):
                pe.wait_ge(biased, head(i, n - 2))
            for qt in range(NT):
                w = key_tiles(kind, qt) * T
                last = nc.tensor.matmul(score_bank[n % 2][0:T, qt * S:qt * S + w],
                                        st[:, j, 0, o + qt * T:o + qt * T + T], st[:, j, 1, o:o + w],
                                        start=True, stop=True)
            last.then_inc(scored, 1)

        def pe_turn_probs(pe, i, kind, n):
            pe.wait_ge(normed, head(i, n))
            if not (isinstance(i, int) and i == 0 and n < 2):
                pe.wait_ge(*copies(i, n - 2))
            for qt in range(NT):
                for kt in range(key_tiles(kind, qt)):
                    o = turned_at(kind, qt, kt)
                    last = nc.tensor.transpose(turn_bank[n % 2][0:T, o:o + T],
                                               probs[:, n % P_RING, qt, kt * T:kt * T + T], ident[0:T, 0:T])
            last.then_inc(turned, 1)

        def pe_values(pe, i, kind, n):
            unit, slot = divmod(n, 8)
            c, j = divmod(slot, HC)
            if slot == 0 and not (isinstance(i, int) and i == 0):
                pe.wait_ge(att_lo, i * 2 + unit - 1)
            if slot == 0:
                pe.wait_ge(v_placed[unit], i * 16 + 16)
            pe.wait_ge(*copies(i, n))
            for kt in range(NT):
                q0 = T if cross(kind) and kt == 1 else 0
                o = turned_at(kind, q0 // T, kt)
                last = nc.tensor.matmul(value_bank[unit][HD * j:HD * j + HD, c * S + q0:c * S + S],
                                        values[:, kt, n * HD:n * HD + HD], probs_t[:, n % 2, o:o + S - q0],
                                        start=kt == 0, stop=kt == NT - 1)
            last.then_inc(pv_done, 1)

        def pe_output_piece(pe, k, kind, h, m, banks_read):
            half, t = divmod(h, 2)
            if m == 0:
                if h == 0:
                    pe_wait_weights(pe, kind, "o", k)
                if t == 0:
                    pe.wait_ge(att_lo, k * 2 + half + 1)
                if half == 0:
                    semaphore, value = banks_read
                    pe.wait_ge(semaphore, value + t)
            w = weights[slots_of(kind)["o"]]
            fill = three_passes(proj_bank[t][0:T, :], lambda hl, c: attended[:, hl, c, t * T:t * T + T],
                                lambda hl, c: w[:, hl, c, :])
            last = run(fill[6 * half + m:6 * half + m + 1])
            if m == 5 and half == 1:
                last.then_inc(o_full, 1)
            elif m == 5 and t == 1:
                last.then_inc(att_half_read, 1)

        def pe_piece(pe, i, kinds, piece):
            before2, before, _, nxt = kinds
            what, f, m = piece
            if what in ("c", "x"):
                pe_turn_source(pe, i + 1, nxt, what, f)
            elif what == "p":
                pe_projection_piece(pe, i + 1, nxt, f, m)
            elif what == "v":
                pe_value_piece(pe, i + 1, nxt, f, m)
            elif what == "o":
                pe_output_piece(pe, i - 2, before2, f, m, (x_lo, i * 2 + 3) if nxt else (qk_lo, i * 4 + 3))
            elif what == "O":
                pe_output_piece(pe, i - 1, before, f, m, (m_lo, EARLY - 1))
            elif what == "t":
                pe_turn_tile(pe, f)
            elif what == "l":
                pe_logits(pe, f)

        def pe_step(pe, i, kinds):
            before2, before, kind, nxt = kinds
            pieces, _ = schedule(nxt, before2)
            for n in range(H if nxt else DRAIN):
                if n < H - 1:
                    pe_scores(pe, i, kind, n + 1)
                elif nxt:
                    pe_scores(pe, i + 1, nxt, 0)
                if n - LT < 0:
                    if before:
                        pe_turn_probs(pe, i - 1, before, n - LT + H)
                elif n - LT < H:
                    pe_turn_probs(pe, i, kind, n - LT)
                if n - LV >= 0:
                    pe_values(pe, i, kind, n - LV)
                elif before:
                    pe_values(pe, i - 1, before, n - LV + H)
                if n < H:
                    for piece in pieces[n]:
                        pe_piece(pe, i, kinds, piece)
                if n == H + 1:
                    pe_turn_logits(pe, 0)

        def act_split(act, dst_hi, ps, bias):
            if bias is None:
                return nc.scalar.activation(dst_hi, ps, ACT.Copy)
            return nc.scalar.activation(dst_hi, ps, ACT.Identity, bias=bias)

        def dve_split(dst_lo, ps, bias, src_hi):
            if bias is None:
                return nc.vector.tensor_tensor(dst_lo, ps, src_hi, ALU.subtract)
            return nc.vector.scalar_tensor_tensor(dst_lo, ps, bias, src_hi, ALU.add, ALU.subtract)

        def source_split(eng, s, kind, f, is_context, is_act):
            dst, hi_done, lo_done, full = ((src_c, c_hi, c_lo, c_turned) if is_context
                                           else (src_x, x_hi, x_lo, x_turned))
            j = s - B if is_context else s
            ps = proj_bank[f % 2][:, 0:2 * S].rearrange("p (c n) -> p c n", c=2)
            if is_act:
                eng.wait_ge(full, j * 2 + f + 1)
                act_split(eng, dst[:, 0, 2 * f:2 * f + 2, :], ps, None).then_inc(hi_done, 1)
            else:
                eng.wait_ge(hi_done, j * 2 + f + 1)
                dve_split(dst[:, 1, 2 * f:2 * f + 2, :], ps, None, dst[:, 0, 2 * f:2 * f + 2, :]).then_inc(lo_done, 1)

        def projection_split(eng, s, kind, f, is_act):
            what, unit = FILLS[f]
            plane = PLANE[what]
            ps = proj_bank[f % 2]
            if is_act:
                eng.wait_ge(qk_full, s * 4 + f + 1)
                if not (isinstance(s, int) and s == 0 and unit == 0):
                    eng.wait_ge(stacked[1 - unit], s * 16 * STACK_DMAS + (16 * STACK_DMAS if unit else 0))
            else:
                eng.wait_ge(qk_hi, s * 4 + f + 1)
            parts = [(slice(0, 2 * S), None)] if cross(kind) else [
                (slice(cc * S, cc * S + S), projection_bias(kind, what, 2 * unit + cc)) for cc in range(2)]
            for sl, bias in parts:
                if is_act:
                    last = act_split(eng, qk[:, plane, sl], ps[:, sl], bias)
                else:
                    last = dve_split(qk[:, plane + 1, sl], ps[:, sl], bias, qk[:, plane, sl])
            last.then_inc(qk_hi if is_act else qk_lo, 1)

        def attended_split(eng, i, kind, unit, is_act):
            ps = value_bank[unit][:, 0:2 * S].rearrange("p (c n) -> p c n", c=2)
            if is_act:
                eng.wait_ge(pv_done, head(i, 8 * unit + 7))
                if not (isinstance(i, int) and i == 0):
                    if unit == 0:
                        eng.wait_ge(att_half_read, i)
                    else:
                        eng.wait_ge(o_full, i * 2)
            else:
                eng.wait_ge(att_hi, i * 2 + unit + 1)
            parts = [(slice(0, 2), None)] if cross(kind) else [
                (slice(cc, cc + 1), projection_bias(kind, "v", 2 * unit + cc)) for cc in range(2)]
            for sl, bias in parts:
                at = slice(2 * unit + sl.start, 2 * unit + sl.stop)
                if is_act:
                    last = act_split(eng, attended[:, 0, at, :], ps[:, sl, :], bias)
                else:
                    last = dve_split(attended[:, 1, at, :], ps[:, sl, :], bias, attended[:, 0, at, :])
            last.then_inc(att_hi if is_act else att_lo, 1)

        def chunk_planes(slot, c):
            if slot >= EXPERT:
                e = slot - EXPERT
                return experts[:, e, 0, c, :], experts[:, e, 1, c, :], raw_experts[e][:, 1, c, :]
            return weights[slot][:, 0, c, :], weights[slot][:, 1, c, :], raw_weights[slot][:, 1, c, :]

        def chunk_hi(slot, c):
            hi, _, raw = chunk_planes(slot, c)
            nc.scalar.activation(hi, raw, ACT.Copy).then_inc(w_hi, 1)

        def chunk_lo(slot, c, which):
            hi, lo, raw = chunk_planes(slot, c)
            e = nc.vector if which == "dve" else nc.gpsimd
            e.tensor_tensor(lo, raw, hi, ALU.subtract).then_inc(w_lo[which], 1)

        def act_weight_hi(act, m):
            _, c, slot, _ = JOBS[m]
            if slot >= EXPERT:
                act.wait_ge(expert_in[slot - EXPERT], 16)
            else:
                act.wait_ge(raw_in[slot][c], 16 * load_count(m))
            chunk_hi(slot, c)

        def weight_lo(eng, m, which):
            _, c, slot, _ = JOBS[m]
            eng.wait_ge(w_hi, m + 1)
            chunk_lo(slot, c, which)

        def act_exp(act, i, kind, n):
            r = n % P_RING
            act.wait_ge(biased, head(i, n))
            for qt in range(NT):
                w = key_tiles(kind, qt) * T
                last = nc.scalar.activation(probs[:, r, qt, 0:w], probs[:, r, qt, 0:w], ACT.Exp,
                                            bias=neg_max[:, r, qt:qt + 1], scale=-1.0,
                                            accum_out=row_sum[:, r, qt:qt + 1])
            last.then_inc(exp_done, 1)

        def copy_turned(eng, i, kind, n, is_act):
            eng.wait_ge(turned, head(i, n))
            if not (isinstance(i, int) and i == 0 and n < 2):
                eng.wait_ge(pv_done, head(i, n - 2))
            w = turned_cols(kind)
            if is_act:
                nc.scalar.activation(probs_t[:, n % 2, 0:w], turn_bank[n % 2][0:T, 0:w], ACT.Copy).then_inc(copied_act, 1)
            else:
                nc.vector.tensor_copy(probs_t[:, n % 2, 0:w], turn_bank[n % 2][0:T, 0:w]).then_inc(copied_dve, 1)

        def act_values(act, s, t):
            act.wait_ge(v_full, s * 2 + t + 1)
            if t == 0 and not (isinstance(s, int) and s == 0):
                for unit in range(2):
                    act.wait_ge(v_placed[unit], s * 16)
            nc.scalar.activation(values_next[:, t, :], proj_bank[t][0:T, :], ACT.Copy).then_inc(v_copied, 1)

        def fill_done(eng, i, nxt, what, f, is_act):
            if what in ("c", "x"):
                source_split(eng, i + 1, nxt, f, what == "c", is_act)
            elif what == "p":
                projection_split(eng, i + 1, nxt, f, is_act)
            elif what == "v" and is_act:
                act_values(eng, i + 1, f)
            elif what == "t":
                tile_split(eng, f, is_act)
            elif what == "l" and is_act:
                act_logits(eng, f)

        def act_norm_rows(act, i):
            act.wait_ge(ln_step, i * LN_OPS + LN_OPS)
            for t in range(NT):
                last = nc.scalar.activation(rows[:, t, :], rows[:, t, :], ACT.Identity,
                                            bias=neg_mean_rstd[:, t:t + 1], scale=rstd[:, t:t + 1])
            last.then_inc(rows_normed, 1)

        def act_step(act, i, kinds):
            before2, before, kind, nxt = kinds
            _, end = schedule(nxt, before2)
            for n in range(H if nxt else DRAIN):
                for m in JOBS_AT.get((i, n), []) if isinstance(i, int) else []:
                    act_weight_hi(act, m)
                if n < H:
                    act_exp(act, i, kind, n)
                m = n - LC
                if m % 4 == 3 and m < H:
                    if m >= 0:
                        copy_turned(act, i, kind, m, True)
                    elif before:
                        copy_turned(act, i - 1, before, m + H, True)
                for what, f in leaves_at(end, n):
                    fill_done(act, i, nxt, what, f, True)
                if before and n == ATT_SLOT[0]:
                    attended_split(act, i - 1, before, 0, True)
                if before and n == ATT_SLOT[1]:
                    attended_split(act, i - 1, before, 1, True)
                if before2 and n == end[("o", 3)] + 7:
                    act_norm_rows(act, i - 2)
                if not nxt and n == H - 2:
                    attended_split(act, i, kind, 0, True)
                if not nxt and n == end[("O", 3)] + 7:
                    act_norm_rows(act, i - 1)
            if not nxt:
                attended_split(act, i, kind, 1, True)

        def dve_bias_max(dve, i, kind, n):
            r = n % P_RING
            if n == 0 and cross(kind):
                dve.wait_ge(bias_ready, i - B + 1)
            if n == 8 and cross(kind):
                dve.wait_ge(bias_doubled, (i - B) * 16 + 16)
            if not (isinstance(i, int) and i == 0 and n < P_RING):
                dve.wait_ge(turned, head(i, n - P_RING))
            wait_alone(dve, (scored, head(i, n)))
            bias = mask_bias if cross(kind) and n < 8 else late_bias
            for qt in range(NT):
                w = key_tiles(kind, qt) * T
                last = nc.vector.tensor_tensor_reduce(probs[:, r, qt, 0:w], score_bank[n % 2][0:T, qt * S:qt * S + w],
                                                      bias[:, qt, 0:w], -SCALE, HIGHEST_SHIFT, ALU.add, ALU.min,
                                                      neg_max[:, r, qt:qt + 1])
            last.then_inc(biased, 1)

        def dve_keep_sum(dve, i, n):
            r = n % P_RING
            dve.wait_ge(exp_done, head(i, n))
            nc.vector.tensor_scalar(row_sum[:, r, :], row_sum[:, r, :], 0.5, None, ALU.max).then_inc(sum_kept, 1)

        def dve_recip(dve, i, kind, n):
            r = n % P_RING
            if cross(kind):
                dve.wait_ge(sum_kept, head(i - B, n))
            else:
                dve.wait_ge(exp_done, head(i, n))
            nc.vector.reciprocal(recip[:, r, :], row_sum[:, r, :]).then_inc(recip_ready, 1)

        def dve_add_rows(dve, i, t):
            if t == 0:
                dve.wait_ge(residual_ready, i + 1)
                if not (isinstance(i, int) and i == 0):
                    dve.wait_ge(rows_stored, i * 16)
            dve.wait_ge(o_full, i * 2 + t + 1)
            nc.vector.tensor_tensor(rows[:, t, :], proj_bank[t][0:T, :], residual[:, t, :],
                                    ALU.add).then_inc(rows_added, 1)

        def rsqrt_ops(var, mean, r, tmp, shift):
            v = nc.vector
            ops = [lambda: v.tensor_scalar(r.bitcast(I32), var.bitcast(I32), 1, None, ALU.logical_shift_right),
                   lambda: v.tensor_scalar(r.bitcast(I32), r.bitcast(I32), -1.0, RSQRT_MAGIC, ALU.mult, ALU.add)]
            for _ in range(3):
                ops += [lambda: v.tensor_tensor(tmp, r, r, ALU.mult),
                        lambda: v.scalar_tensor_tensor(tmp, tmp, -0.5, var, ALU.mult, ALU.mult),
                        lambda: v.scalar_tensor_tensor(r, tmp, 1.5, r, ALU.add, ALU.mult)]
            return ops + [lambda: v.scalar_tensor_tensor(shift, mean, -1.0, r, ALU.mult, ALU.mult)]

        def dve_ln_op(dve, i, k):
            if k == 0:
                dve.wait_ge(rows_added, i * 2 + 2)
                nc.vector.bn_stats(stats[:, 0, :], rows[:, 0, :])
                last = nc.vector.bn_stats(stats[:, 1, :], rows[:, 1, :])
            elif k == 1:
                wait_alone(dve, (ln_step, i * LN_OPS + k))
                nc.vector.bn_aggr(mean_var[:, 0, :], stats[:, 0, :])
                last = nc.vector.bn_aggr(mean_var[:, 1, :], stats[:, 1, :])
            elif k == 2:
                dve.wait_ge(ln_step, i * LN_OPS + k)
                last = nc.vector.tensor_scalar(var_eps[:, :], mean_var[:, :, 1], EPS, None, ALU.add)
            else:
                dve.wait_ge(ln_step, i * LN_OPS + k)
                last = rsqrt_ops(var_eps[:, :], mean_var[:, :, 0], rstd[:, :], newton[:, :],
                                 neg_mean_rstd[:, :])[k - 3]()
            last.then_inc(ln_step, 1)

        def dve_step(dve, i, kinds):
            before2, before, kind, nxt = kinds
            _, end = schedule(nxt, before2)
            for n in range(H if nxt else DRAIN):
                if n < H:
                    dve_bias_max(dve, i, kind, n)
                for m in JOBS_AT.get((i, n), []) if isinstance(i, int) else []:
                    if JOBS[m][3] == "dve":
                        weight_lo(dve, m, "dve")
                summed = (i, kind, n - 1) if n >= 1 else (i - 1, before, H - 1)
                if summed[1] and n <= H and cross(summed[1]):
                    dve_keep_sum(dve, summed[0], summed[2])
                m = n - LC
                if m % 4 != 3 and m < H:
                    if m >= 0:
                        copy_turned(dve, i, kind, m, False)
                    elif before:
                        copy_turned(dve, i - 1, before, m + H, False)
                if summed[1] and n <= H:
                    dve_recip(dve, *summed)
                if n == 0:
                    fill_done(dve, i - 1, kind, "p", 3, False)
                for what, f in leaves_at(end, n - 1):
                    if (what, f) != ("p", 3):
                        fill_done(dve, i, nxt, what, f, False)
                if before and n == ATT_SLOT[0] + 1:
                    attended_split(dve, i - 1, before, 0, False)
                if before and n == ATT_SLOT[1] + 1:
                    attended_split(dve, i - 1, before, 1, False)
                for (what, f), slot in end.items():
                    if slot == n - 1 and what in ("o", "O") and f >= 2:
                        dve_add_rows(dve, i - 2 if what == "o" else i - 1, f - 2)
                for what, step in (("o", i - 2), ("O", i - 1)):
                    if (what, 3) in end and (what == "O" or before2) and 2 <= n - end[(what, 3)] <= 6:
                        at = n - end[(what, 3)] - 1
                        for k in range((at - 1) * 3, at * 3):
                            dve_ln_op(dve, step, k)
                if not nxt and n == H - 1:
                    attended_split(dve, i, kind, 0, False)
                if not nxt and n == H + 2:
                    gate_logits(dve, 0)
            if not nxt:
                attended_split(dve, i, kind, 1, False)

        def pool_norm(pool, i, kind, n):
            r = n % P_RING
            pool.wait_ge(recip_ready, head(i, n))
            if cross(kind):
                for qt in range(NT):
                    w = key_tiles(kind, qt) * T
                    last = nc.gpsimd.tensor_tensor(probs[:, r, qt, 0:w], probs[:, r, qt, 0:w],
                                                   recip[:, r, qt:qt + 1].broadcast_to((T, w)), ALU.mult)
            else:
                last = nc.gpsimd.tensor_tensor(
                    probs[:, r], probs[:, r],
                    recip[:, r, :].rearrange("p (a b) -> p a b", b=1).broadcast_to((T, NT, S)), ALU.mult)
            last.then_inc(normed, 1)

        def pool_residual(pool, i, kind):
            pool.wait_ge(residual_in, i * 16 + 16)
            b = out_bias[:, 1 if cross(kind) else 0, :].rearrange("p (a b) -> p a b", a=1).broadcast_to((T, NT, D))
            nc.gpsimd.tensor_tensor(residual[:, :, :], residual[:, :, :], b, ALU.add).then_inc(residual_ready, 1)

        def pool_mask(pool, s):
            wait_alone(pool, (mask_in, (s - B) * 16 + 16), (biased, head(s - 1, 7)))
            nc.gpsimd.tensor_scalar(mask_bias[:, :, :], mask_u8[:, :, :], MASKED, None, ALU.mult).then_inc(bias_scaled, 1)
            wait_alone(pool, (bias_scaled, s - B + 1))
            nc.gpsimd.affine_select(out=mask_bias[:, :, :], in_=mask_bias[:, :, :], compare_op=ALU.is_ge,
                                    fill=MASKED, base=0, pattern=[[T, NT], [-1, S]],
                                    channel_multiplier=1).then_inc(bias_ready, 1)

        def pool_step(pool, i, kinds):
            before2, before, kind, nxt = kinds
            for n in range(H):
                pool_norm(pool, i, kind, n)
                for m in JOBS_AT.get((i, n), []) if isinstance(i, int) else []:
                    if JOBS[m][3] == "pool":
                        weight_lo(pool, m, "pool")
                if before and n == 8:
                    pool_residual(pool, i - 1, before)
                if nxt and cross(nxt) and n == 10:
                    pool_mask(pool, i + 1)

        def load_matrix(sp, name):
            for matrix, c, slot, _ in JOBS:
                if matrix == name:
                    sp.dma_start(raw_weights[slot][:, 1, c, :], a[name][:, c, :]).then_inc(raw_in[slot][c], 16)

        def load_expert(sp, e):
            sp.dma_start(raw_experts[e][:, 1, :, :], a["experts"][e]).then_inc(expert_in[e], 16)

        def batch_rows(dram, b):
            return dram[b].rearrange("(t p) d -> p t d", p=T)

        def load_sources(sp, s, kind, first):
            if not first:
                sp.wait_ge(x_turned, s * 2)
            if cross(kind):
                sp.wait_ge(rows_stored, (s - B) * 16 + 16)
                sp.dma_start(nat_x[:, :, :], batch_rows(x1_dram, s - B)).then_inc(x_in, 16)
                if not (isinstance(s, int) and s == B):
                    sp.wait_ge(c_turned, (s - B) * 2)
                sp.dma_start(nat_c[:, :, :], a["context"][s - B, 0:S, :].rearrange("(t p) d -> p t d", p=T)).then_inc(c_in, 16)
            else:
                sp.dma_start(nat_x[:, :, :], batch_rows(a["x"], s)).then_inc(x_in, 16)

        def load_residual(sp, i, kind):
            if not (isinstance(i, int) and i == 0):
                sp.wait_ge(rows_added, i * 2)
            src = batch_rows(x1_dram, i - B) if cross(kind) else batch_rows(a["x"], i)
            sp.dma_start(residual[:, :, :], src).then_inc(residual_in, 16)

        def load_mask(sp, s):
            if not (isinstance(s, int) and s == B):
                wait_alone(sp, (bias_scaled, s - B))
            sp.dma_start(mask_u8[:, :, :], a["mask"][s - B, 0:S, 0:S].rearrange("(t p) k -> p t k", p=T)).then_inc(mask_in, 16)

        def stack_unit(sp, s, unit):
            wait_alone(sp, (qk_lo, s * 4 + 2 * unit + 2))
            if unit == 1 or not (isinstance(s, int) and s == 0):
                if not (isinstance(s, int) and s == 0):
                    sp.wait_ge(scored, s * H - (0 if unit else 8))
            for j in range(HC):
                for role, planes in enumerate((slice(0, 3, 2), slice(1, 3), slice(0, 4, 3))):
                    sp.dma_start(stacks[unit][HD * role:HD * role + HD, j, :, :].bitcast(F32),
                                 qk[HD * j:HD * j + HD, planes, :].bitcast(F32)).then_inc(stacked[unit], 16)

        def store_rows(sp, i, kind):
            sp.wait_ge(rows_normed, i + 1)
            dst = batch_rows(x2_dram, i - B) if cross(kind) else batch_rows(x1_dram, i)
            sp.dma_start(dst, rows[:, :, :]).then_inc(rows_stored, 16)

        def place_values(sp, s, unit):
            used = [] if isinstance(s, int) and s == 0 else [(pv_done, head(s - 1, 8 * unit + 7))]
            wait_alone(sp, (v_copied, s * 2 + 2), *used)
            at = slice(unit * D // 2, (unit + 1) * D // 2)
            sp.dma_start(values[:, :, at], values_next[:, :, at]).then_inc(v_placed[unit], 16)

        def double_bias(sp, i):
            wait_alone(sp, (bias_ready, i - B + 1), (biased, i * H))
            sp.dma_start(late_bias[:, :, :], mask_bias[:, :, :]).then_inc(bias_doubled, 16)

        def load_weights(sp, i):
            if i == 0:
                load_matrix(sp, "cross_k")
                load_matrix(sp, "cross_v")
            if i == B - 1:
                sp.wait_ge(qk_full, 4 * B)
                load_matrix(sp, "cross_q")
                load_matrix(sp, "cross_o")
            if i == STEPS - 2:
                sp.wait_ge(v_full, 2 * B)
                load_expert(sp, 0)
                sp.wait_ge(o_full, 2 * B)
                load_expert(sp, 1)

        def sp_step(sp, i, kinds, nxt2):
            before2, before, kind, nxt = kinds
            if isinstance(i, int) and i == B - 1:
                load_weights(sp, i)
            stack_unit(sp, i, 1)
            if cross(kind):
                double_bias(sp, i)
            if isinstance(i, int) and i != B - 1:
                load_weights(sp, i)
            if nxt2:
                load_sources(sp, i + 2, nxt2, False)
            place_values(sp, i, 1)
            if kind == "self" and before:
                rows = ST * P // (B - 1)
                sp.dma_start(sorted_dram[bass.ds((i - 1) * rows, rows), :], a["x"].rearrange("b s d -> (b s) d")[0:rows, :]
                             ).then_inc(filler_in, 16)
            if nxt and cross(nxt):
                load_mask(sp, i + 1)
            if before:
                load_residual(sp, i - 1, before)
            if nxt:
                stack_unit(sp, i + 1, 0)
            if before2:
                store_rows(sp, i - 2, before2)
            if nxt:
                place_values(sp, i + 1, 0)
            else:
                load_tiles(sp, 2)
            if isinstance(i, int) and i == STEPS - 2:
                sp.wait_ge(v_full, 2 * STEPS)
                sp.wait_ge(qk_full, 4 * STEPS - 1)
                load_tiles(sp, 0)
                load_tiles(sp, 1)

        def load_tiles(sp, n):
            lo, hi = LOADS[n]
            sp.wait_ge(rows_stored, 16 * (B + (hi * P + S - 1) // S))
            sp.dma_start(acc[:, lo:hi, :], x2_dram.rearrange("b s d -> (b s) d")[lo * P:hi * P, :].rearrange(
                "(t p) d -> p t d", p=P)).then_inc(acc_in[n], 16)

        def sp_experts(sp):
            load_residual(sp, STEPS - 1, "cross")
            store_rows(sp, STEPS - 2, "cross")
            load_tiles(sp, 3)
            first = TOKENS - S - 12 * P
            sp.dma_start(acc[0:first, 12, :], x2_dram[B - 2, S - first:S, :]).then_inc(acc_in[4], 16)
            sp.wait_ge(rows_normed, STEPS)
            for dst, src in ((acc[first:P, 12, :], rows[0:P - first, 0, :]), (acc[0:T - P + first, 13, :], rows[P - first:T, 0, :]),
                             (acc[T - P + first:P, 13, :], rows[:, 1, :])):
                sp.dma_start(dst, src).then_inc(acc_in[4], 16)
            sp.dma_start(tables_f[:, 0, :], a["before"]).then_inc(tables_in, 16)
            sp.dma_start(tables_f[:, 1, :], a["ones"]).then_inc(tables_in, 16)
            sp.dma_start(tile_iota[:, :], a["tile_iota"]).then_inc(tables_in, 16)
            for r in range(3):
                sp.dma_start(be_raw[r * NE:(r + 1) * NE, :], a["expert_bias"]).then_inc(be_in, 16)
            sp.wait_ge(o_full, 2 * STEPS)
            for e in range(2, 6):
                load_expert(sp, e)
            sp.wait_ge(logits_full, 4)
            for e in range(6, NE):
                load_expert(sp, e)
            sp.wait_ge(be_step, 3)
            sp.dma_start(be_stack[2 * NE:3 * NE, :].bitcast(F32), be_lo[0:NE, :].bitcast(F32)).then_inc(be_stacked, 16)
            for t in range(MT):
                sp.wait_ge(scattered[t], 32)
            sp.wait_ge(bias_full, MT)

            def load(j, s, wait=True):
                if wait:
                    sp.wait_ge(m_turned, MT + j - 1)
                sp.dma_start(rows_x[:, s, :], sorted_dram[bass.ds(j * P, P), :]).then_inc(rows_in[s], 16)

            load(0, 0, False)
            load(1, 1, False)
            with sp.Fori(1, ST // 2) as it:
                for s in range(2):
                    load(it * 2 + s, s)
            load(ST - 1, 0)
            for g, tiles in enumerate(M_GROUPS):
                sp.wait_ge(m_normed, g + 1)
                lo, hi = tiles
                sp.dma_start(out.rearrange("b s d -> (b s) d")[lo * P:hi * P, :].rearrange("(t p) d -> p t d", p=P),
                             acc[:, lo:hi, :]).then_inc(out_stored, 16)
            sp.wait_ge(out_stored, 16 * len(M_GROUPS))

        M_GROUPS = ((0, 4), (4, 8), (8, 12), (12, 14))
        M_LN = LN_OPS - 1

        LATE_JOBS = min(m for m, j in enumerate(JOBS) if j[0] == "e2")

        def tile_bank(t):
            return (proj_bank if t < EARLY else turn_bank)[t % 2]

        def pe_turn_tile(pe, t):
            for n, (lo, _) in enumerate(LOADS):
                if t == lo:
                    pe.wait_ge(acc_in[n], 64 if n == 4 else 16)
            if t < 2:
                pe.wait_ge(rows_added, 2 * (STEPS - 3) + t + 1)
            elif t in (EARLY, EARLY + 1):
                pe.wait_ge(*copies(STEPS - 1, H - 2 + t - EARLY))
            else:
                pe.wait_ge(m_lo, t - 1)
            for c in range(KC):
                last = nc.tensor.transpose(tile_bank(t)[:, c * P:c * P + P], acc[:, t, c * P:c * P + P], ident[:, :])
            last.then_inc(m_turned, 1)

        def pe_logits(pe, g):
            lo, hi = FOURS[g]
            pe.wait_ge(m_lo, hi)
            if g == 0:
                pe.wait_ge(gate_lo, 1)
            pe.wait_ge(rows_added, 2 * (STEPS - 2 if g < 2 else STEPS - 1) + g % 2 + 1)
            run(three_passes(proj_bank[g % 2][0:NE, 0:(hi - lo) * P], lambda hl, c: gate_w[:, hl, c, :],
                             lambda hl, c: x2t[:, lo % EARLY:lo % EARLY + hi - lo, hl, c, :])).then_inc(logits_full, 1)

        def pe_turn_logits(pe, group):
            pe.wait_ge(logits_copied, 2 * group + 2)
            lo, hi = GROUPS[group]
            for t in range(lo, hi):
                last = nc.tensor.transpose(proj_bank[0][:, (t - lo) * NE:(t - lo) * NE + NE],
                                           logits_t[:, t * P:t * P + P], ident[0:NE, 0:NE])
            last.then_inc(logits_turned, 1)

        def pe_last_output(pe, half):
            for h in (2 * half, 2 * half + 1):
                for m in range(6):
                    pe_output_piece(pe, STEPS - 1, "cross", h, m, (logits_added, 1 - h))

        def pe_experts(pe):
            pe_last_output(pe, 0)
            for t in (EARLY, EARLY + 1):
                pe_turn_tile(pe, t)
            pe_last_output(pe, 1)
            for t in range(*LOADS[3]):
                pe_turn_tile(pe, t)
            pe_logits(pe, 2)
            for t in range(*LOADS[4]):
                pe_turn_tile(pe, t)
            pe_logits(pe, 3)
            pe_turn_logits(pe, 1)
            pe.wait_ge(biased, head(STEPS - 1, H - 1))
            pe.wait_ge(chosen_ready, 2)
            cols = MT * NE
            nc.tensor.matmul(score_bank[0][:, 0:cols], before[:, :], chosen[:, :], start=True, stop=False)
            for t in range(1, MT):
                nc.tensor.matmul(score_bank[0][:, t * NE:cols], ones[:, :], chosen[:, 0:cols - t * NE],
                                 start=False, stop=t == MT - 1)
            for t in range(MT):
                last = nc.tensor.matmul(score_bank[0][:, cols:cols + NE], ones[:, :], chosen[:, t * NE:t * NE + NE],
                                        start=t == 0, stop=t == MT - 1)
            last.then_inc(ranked, 1)
            pe.wait_ge(gates_done, 2)
            for f, (lo, hi) in enumerate(FOURS):
                if f >= 2:
                    pe.wait_ge(gates_copied, f - 1)
                for t in range(lo, hi):
                    last = nc.tensor.transpose(turn_bank[f % 2][0:3 * NE, (t - lo) * P:(t - lo) * P + P],
                                               gate_hl[:, t, :].bitcast(F32), ident[:, :])
                last.then_inc(gates_turned, 1)
            pe.wait_ge(logits_added, 2)
            pe.wait_ge(gates_copied, 4)
            pe.wait_ge(be_stacked, 16)
            for t in range(MT):
                if t >= 2:
                    pe.wait_ge(bias_added, t - 1)
                nc.tensor.matmul(proj_bank[t % 2][:, :], gates_t[:, t * P:t * P + P], be_stack[:, :],
                                 start=True, stop=True).then_inc(bias_full, 1)
            pe.wait_ge(bias_added, MT)
            pe.wait_ge(w_lo["dve"], lo_count(len(JOBS) - 1, "dve"))
            pe.wait_ge(w_lo["pool"], lo_count(len(JOBS) - 1, "pool"))
            pe.wait_ge(ends_ready, 1)

            def turn(j, s):
                pe.wait_ge(rows_in[s], j * 8 + (16 - 8 * s))
                pe.wait_ge(m_lo, MT + j - 1)
                for c in range(KC):
                    last = nc.tensor.transpose(turn_bank[s][:, c * P:c * P + P], rows_x[:, s, c * P:c * P + P], ident[:, :])
                last.then_inc(m_turned, 1)

            def product(j, s):
                e = pe.value_load(expert_of[0:1, bass.ds(j, 1)], min_val=0, max_val=NE - 1)
                pe.wait_ge(m_lo, MT + j + 1)
                if not isinstance(j, int) or j >= 2:
                    pe.wait_ge(y_copied, j - 1)
                run(three_passes(proj_bank[s][:, :], lambda hl, c: xt[:, s, hl, c, :],
                                 lambda hl, c: experts[:, bass.ds(e, 1), hl, c, :])).then_inc(product_full, 1)

            turn(0, 0)
            for j in range(2):
                turn(j + 1, 1 - j)
                product(j, j)
            with pe.Fori(1, ST // 2) as it:
                for s in range(2):
                    turn(it * 2 + s + 1, 1 - s)
                    product(it * 2 + s, s)
            product(ST - 1, 0)

        def tile_split(eng, t, is_act):
            ps = tile_bank(t)[:, :].rearrange("p (c n) -> p c n", c=KC)
            if is_act:
                if t == 0:
                    eng.wait_ge(stacked[1], 16 * STACK_DMAS * STEPS)
                eng.wait_ge(m_turned, t + 1)
                nc.scalar.activation(x2t[:, t % EARLY, 0, :, :], ps, ACT.Copy).then_inc(m_hi, 1)
            else:
                eng.wait_ge(m_hi, t + 1)
                nc.vector.tensor_tensor(x2t[:, t % EARLY, 1, :, :], ps, x2t[:, t % EARLY, 0, :, :], ALU.subtract).then_inc(m_lo, 1)

        def act_logits(act, g):
            lo, hi = FOURS[g]
            act.wait_ge(logits_full, g + 1)
            nc.scalar.activation(logits_t[:, lo * P:hi * P], proj_bank[g % 2][0:NE, 0:(hi - lo) * P],
                                 ACT.Copy).then_inc(logits_copied, 1)

        def act_pair_exp(act, group):
            lo, hi = GROUPS[group]
            act.wait_ge(pair_diff, group + 1)
            nc.scalar.activation(pair_w[:, 1, lo:hi], pair_w[:, 0, lo:hi], ACT.Exp).then_inc(pair_exp, 1)

        def act_experts(act):
            for t in range(EARLY, 12):
                tile_split(act, t, True)
            act_norm_rows(act, STEPS - 1)
            act_logits(act, 2)
            act_pair_exp(act, 0)
            for t in range(12, MT):
                tile_split(act, t, True)
            act_logits(act, 3)
            for m in range(LATE_JOBS, LATE_JOBS + 8):
                act_weight_hi(act, m)
            act_pair_exp(act, 1)
            for f, (lo, hi) in enumerate(FOURS):
                act.wait_ge(gates_turned, f + 1)
                nc.scalar.activation(gates_t[:, lo * P:hi * P], turn_bank[f % 2][0:3 * NE, 0:(hi - lo) * P],
                                     ACT.Copy).then_inc(gates_copied, 1)
            for m in range(LATE_JOBS + 8, len(JOBS)):
                act_weight_hi(act, m)

            def hi(j, s):
                act.wait_ge(m_turned, MT + j + 1)
                if not isinstance(j, int) or j >= 2:
                    act.wait_ge(product_full, j - 1)
                nc.scalar.activation(xt[:, s, 0, :, :], turn_bank[s][:, :].rearrange("p (c n) -> p c n", c=KC),
                                     ACT.Copy).then_inc(m_hi, 1)

            def copy(j, s):
                act.wait_ge(product_full, j + 1)
                if not isinstance(j, int) or j >= 2:
                    act.wait_ge(y_stored[s], j * 8 - 8 * s)
                nc.scalar.activation(y_out[:, s, :], proj_bank[s][:, :], ACT.Copy).then_inc(y_copied, 1)
                act.wait_ge(y_copied, j + 1)
                act.dma_start(products_dram[bass.ds(j * P, P), :], y_out[:, s, :]).then_inc(y_stored[s], 16)

            hi(0, 0)
            for j in range(2):
                hi(j + 1, 1 - j)
                copy(j, j)
            with act.Fori(1, ST // 2) as it:
                for s in range(2):
                    hi(it * 2 + s + 1, 1 - s)
                    copy(it * 2 + s, s)
            copy(ST - 1, 0)
            for g, (lo, hi) in enumerate(M_GROUPS):
                act.wait_ge(m_ln, (g + 1) * M_LN)
                for t in range(lo, hi):
                    last = nc.scalar.activation(acc[:, t, :], acc[:, t, :], ACT.Identity,
                                                bias=m_shift[:, t:t + 1], scale=m_rstd[:, t:t + 1])
                last.then_inc(m_normed, 1)

        def pool_experts(pool):
            pool.wait_ge(filler_in, 16 * (B - 1))
            pool.wait_ge(placed, 1)
            for n in range(len(LOADS)):
                pool.wait_ge(acc_in[n], 64 if n == 4 else 16)
            for t in range(MT):
                for k in range(2):
                    at = k * MT + t
                    nc.gpsimd.indirect_dma_start(sorted_dram[:, :], bass.IndirectOffsetOnAxis(ap=place[:, at:at + 1], axis=0),
                                                 acc[:, t, :], None).then_inc(scattered[t], 16)
            pool.wait_ge(product_full, ST)
            for s in range(2):
                pool.wait_ge(y_stored[s], 16 * ((ST + 1 - s) // 2))
            for t in range(MT):
                for k in range(2):
                    at = k * MT + t
                    nc.gpsimd.indirect_dma_start(gathered[:, t, k, :], None, products_dram[:, :],
                                                 bass.IndirectOffsetOnAxis(ap=place[:, at:at + 1], axis=0)).then_inc(gathered_in[t], 16)

        def gate_logits(dve, group):
            lo, hi = GROUPS[group]
            dve.wait_ge(logits_turned, group + 1)
            nc.vector.tensor_tensor(
                logits[:, lo:hi, :], proj_bank[0][:, 0:(hi - lo) * NE].rearrange("p (t e) -> p t e", e=NE),
                gate_bias[:, :].rearrange("p (a e) -> p a e", a=1).broadcast_to((P, hi - lo, NE)),
                ALU.add).then_inc(logits_added, 1)

        def dve_experts(dve):
            links = [0]

            def link(instruction):
                links[0] += 1
                instruction.then_inc(gate_step, 1)
                dve.wait_ge(gate_step, links[0])

            def spread(x, tiles):
                return x.rearrange("p (a b) -> p a b", b=1).broadcast_to((P, tiles.stop - tiles.start, NE))

            def gate_first(g):
                tiles = slice(*GROUPS[g])
                dve.wait_ge(logits_added, g + 1)
                for t in range(*GROUPS[g]):
                    last = nc.vector.max(top[:, t, :], logits[:, t, :])
                link(last)
                nc.vector.tensor_tensor(pair_w[:, 0, tiles], top[:, tiles, 1], top[:, tiles, 0],
                                        ALU.subtract).then_inc(pair_diff, 1)
                for t in range(*GROUPS[g]):
                    last = nc.vector.max_index(top_at[:, t, :], top[:, t, :], logits[:, t, :])
                link(last)
                link(nc.vector.tensor_copy(top_f[:, tiles, :], top_at[:, tiles, 0:2]))
                every = iota[:, :].rearrange("p (a e) -> p a e", a=1).broadcast_to((P, tiles.stop - tiles.start, NE))
                for k in range(2):
                    last = nc.vector.tensor_tensor(hot[:, k, tiles, :], every, spread(top_f[:, tiles, k], tiles), ALU.is_equal)
                link(last)
                nc.vector.tensor_tensor(chosen[:, tiles.start * NE:tiles.stop * NE].rearrange("p (t e) -> p t e", e=NE),
                                        hot[:, 0, tiles, :], hot[:, 1, tiles, :], ALU.add).then_inc(chosen_ready, 1)

            def gate_second(g):
                tiles = slice(*GROUPS[g])
                dve.wait_ge(pair_exp, g + 1)
                link(nc.vector.tensor_scalar(pair_w[:, 3, tiles], pair_w[:, 1, tiles], 1.0, None, ALU.add))
                link(nc.vector.reciprocal(pair_w[:, 2, tiles], pair_w[:, 3, tiles]))
                link(nc.vector.tensor_tensor(pair_w[:, 3, tiles], pair_w[:, 1, tiles], pair_w[:, 2, tiles], ALU.mult))
                for k in range(2):
                    last = nc.vector.tensor_tensor(weighted[:, k, tiles, :], hot[:, k, tiles, :],
                                                   spread(pair_w[:, 2 + k, tiles], tiles), ALU.mult)
                link(last)
                link(nc.vector.tensor_tensor(gates[:, tiles, :], weighted[:, 0, tiles, :], weighted[:, 1, tiles, :], ALU.add))
                nc.vector.tensor_copy(gate_hl[:, tiles, 0:NE], gates[:, tiles, :])
                link(nc.vector.tensor_copy(gate_hl[:, tiles, 2 * NE:3 * NE], gates[:, tiles, :]))
                nc.vector.tensor_tensor(gate_hl[:, tiles, NE:2 * NE], gates[:, tiles, :], gate_hl[:, tiles, 0:NE],
                                        ALU.subtract).then_inc(gates_done, 1)

            def stack_biases():
                dve.wait_ge(be_in, 48)
                nc.vector.tensor_copy(be_lo[:, :], be_raw[:, :]).then_inc(be_step, 1)
                dve.wait_ge(be_step, 1)
                nc.vector.tensor_copy(be_stack[:, :], be_lo[:, :]).then_inc(be_step, 1)
                dve.wait_ge(be_step, 2)
                nc.vector.tensor_tensor(be_lo[:, :], be_raw[:, :], be_stack[:, :], ALU.subtract).then_inc(be_step, 1)

            def find_places():
                cols = MT * NE
                dve.wait_ge(ranked, 1)
                for n in range(2):
                    nc.vector.memset(ends[n][:, 0:NE], 0.0)
                link(nc.vector.tensor_scalar(whole[:, :], score_bank[0][:, cols:cols + NE], float(P - 1), None, ALU.add))
                link(nc.vector.tensor_scalar(whole[:, :], whole[:, :], 7, None, ALU.logical_shift_right))
                link(nc.vector.tensor_copy(ends[0][:, NE:], whole[:, :]))
                for n in range(3):
                    src, dst, shift = ends[n % 2], ends[1 - n % 2], 1 << n
                    link(nc.vector.tensor_tensor(dst[:, NE:], src[:, NE:], src[:, NE - shift:2 * NE - shift], ALU.add))
                link(nc.vector.tensor_scalar(ends[0][:, NE:], ends[1][:, NE - 1:2 * NE - 1], float(P), None, ALU.mult))
                link(nc.vector.tensor_tensor(
                    place_of[:, :].rearrange("p (t e) -> p t e", e=NE), score_bank[0][:, 0:cols].rearrange("p (t e) -> p t e", e=NE),
                    ends[0][:, NE:].rearrange("p (a e) -> p a e", a=1).broadcast_to((P, MT, NE)), ALU.add))
                for k in range(2):
                    last = nc.vector.tensor_tensor(weighted[:, k, :, :], hot[:, k, :, :],
                                                   place_of[:, :].rearrange("p (t e) -> p t e", e=NE), ALU.mult)
                link(last)
                link(nc.vector.tensor_reduce(place_f[:, :], weighted[:, :, :, :].rearrange("p k t e -> p (k t) e"),
                                             mybir.AxisListType.X, ALU.add))
                nc.vector.tensor_copy(place[:, :], place_f[:, :]).then_inc(placed, 1)
                link(nc.vector.tensor_tensor(
                    ended[:, :, :], ends[1][0:1, NE:].rearrange("p (a e) -> p a e", a=1).broadcast_to((1, ST, NE)),
                    tile_iota[:, :].rearrange("p (a b) -> p a b", b=1).broadcast_to((1, ST, NE)), ALU.is_le))
                link(nc.vector.tensor_reduce(expert_f[:, :], ended[:, :, :], mybir.AxisListType.X, ALU.add))
                nc.vector.tensor_scalar(expert_of[:, :], expert_f[:, :], float(NE - 1), None, ALU.min).then_inc(ends_ready, 1)

            for t in (EARLY, EARLY + 1):
                tile_split(dve, t, False)
            for t in range(NT):
                dve_add_rows(dve, STEPS - 1, t)
            for k in range(LN_OPS):
                dve_ln_op(dve, STEPS - 1, k)
                if k in (1, 3):
                    tile_split(dve, EARLY + 2 + k // 2, False)
            gate_first(0)
            dve.wait_ge(tables_in, 48)
            link(nc.vector.tensor_copy(before[:, :], tables_f[:, 0, :]))
            link(nc.vector.tensor_copy(ones[:, :], tables_f[:, 1, :]))
            for t in range(12, MT):
                tile_split(dve, t, False)
            gate_second(0)
            gate_logits(dve, 1)
            gate_first(1)
            find_places()
            gate_second(1)
            stack_biases()
            for m in range(LATE_JOBS, LATE_JOBS + 8):
                weight_lo(dve, m, "dve")
            for t in range(MT):
                dve.wait_ge(bias_full, t + 1)
                dve.wait_ge(scattered[t], 32)
                nc.vector.tensor_tensor(acc[:, t, :], proj_bank[t % 2][:, :], acc[:, t, :], ALU.add).then_inc(bias_added, 1)
                if LATE_JOBS + 8 + t < len(JOBS):
                    weight_lo(dve, LATE_JOBS + 8 + t, "dve")
            for m in range(LATE_JOBS + 8 + MT, len(JOBS)):
                weight_lo(dve, m, "dve")

            def lo(j, s):
                dve.wait_ge(m_hi, MT + j + 1)
                nc.vector.tensor_tensor(xt[:, s, 1, :, :], turn_bank[s][:, :].rearrange("p (c n) -> p c n", c=KC),
                                        xt[:, s, 0, :, :], ALU.subtract).then_inc(m_lo, 1)

            for j in range(2):
                lo(j, j)
            with dve.Fori(1, ST // 2) as it:
                for s in range(2):
                    lo(it * 2 + s, s)
            lo(ST - 1, 0)
            steps = [0]

            def ln_link(op):
                if steps[0]:
                    dve.wait_ge(m_ln, steps[0])
                op().then_inc(m_ln, 1)
                steps[0] += 1

            chain = []

            def some_links(n):
                for _ in range(min(n, len(chain))):
                    chain.pop(0)()

            def group_chain(lo, hi):
                def aggregate():
                    dve.wait_ge(m_measured, hi)
                    for u in range(lo, hi):
                        last = nc.vector.bn_aggr(m_mean_var[:, u, :], m_stats[:, u, :])
                    return last
                ops = [aggregate, lambda: nc.vector.tensor_scalar(m_var[:, lo:hi], m_mean_var[:, lo:hi, 1], EPS, None, ALU.add),
                       *rsqrt_ops(m_var[:, lo:hi], m_mean_var[:, lo:hi, 0], m_rstd[:, lo:hi],
                                  m_newton[:, lo:hi], m_shift[:, lo:hi])]
                return [lambda op=op: ln_link(op) for op in ops]

            for t0 in range(0, MT, 2):
                for k in range(2):
                    for t in (t0, t0 + 1):
                        if k == 0:
                            dve.wait_ge(gathered_in[t], 32)
                            dve.wait_ge(bias_added, MT)
                        else:
                            dve.wait_ge(added, 2 * t0 + t - t0 + 1)
                        nc.vector.scalar_tensor_tensor(acc[:, t, :], gathered[:, t, k, :], pair_w[:, 2 + k, t:t + 1],
                                                       acc[:, t, :], ALU.mult, ALU.add).then_inc(added, 1)
                        some_links(2)
                for t in (t0, t0 + 1):
                    dve.wait_ge(added, 2 * t0 + 3 + t - t0)
                    nc.vector.bn_stats(m_stats[:, t, :], acc[:, t, :]).then_inc(m_measured, 1)
                    some_links(2)
                for lo, hi in M_GROUPS:
                    if t0 + 2 == hi:
                        some_links(len(chain))
                        chain += group_chain(lo, hi)
            some_links(len(chain))

        block = ctx.enter_context(nc.Block())

        def steps(engine, step):
            s, c = "self", "cross"
            step(0, (None, None, s, s), s)
            step(1, (None, s, s, s), s)
            step(2, (s, s, s, s), s)
            with engine.Fori(3, B - 2) as i:
                step(i, (s, s, s, s), s)
            step(B - 2, (s, s, s, s), c)
            step(B - 1, (s, s, s, c), c)
            step(B, (s, s, c, c), c)
            step(B + 1, (s, c, c, c), c)
            with engine.Fori(B + 2, STEPS - 2) as i:
                step(i, (c, c, c, c), c)
            step(STEPS - 2, (c, c, c, c), None)
            step(STEPS - 1, (c, c, c, None), None)

        @block.sync
        def _(sp):
            load_sources(sp, 0, "self", True)
            sp.dma_start(ident[:, :], a["ident"]).then_inc(ident_in, 16)
            load_matrix(sp, "self_k")
            load_matrix(sp, "self_q")
            for dst, src in ((qkv_bias[:, 0, :], a["bq"]), (qkv_bias[:, 1, :], a["bk"]), (qkv_bias[:, 2, :], a["bv"])):
                sp.dma_start(dst, src).then_inc(consts_in, 16)
            sp.dma_start(late_bias[:, :, :], a["prior"].rearrange("(t p) k -> p t k", p=T)).then_inc(consts_in, 16)
            sp.dma_start(lam[:, :], a["lam"].broadcast_to((T, 1))).then_inc(consts_in, 16)
            for n, name in enumerate(("bo", "b_out")):
                sp.dma_start(out_bias[:, n, :], a[name].rearrange("(a d) -> a d", a=1).broadcast_to((T, D))).then_inc(consts_in, 16)
            load_matrix(sp, "self_v")
            sp.dma_start(gate_raw[:, :, :], a["gate"]).then_inc(gate_in, 16)
            sp.dma_start(gate_bias[:, :], a["gate_bias"].rearrange("(a d) -> a d", a=1).broadcast_to((P, NE))).then_inc(gate_in, 16)
            sp.dma_start(iota[:, :], a["iota"].rearrange("(a d) -> a d", a=1).broadcast_to((P, NE))).then_inc(gate_in, 16)
            load_sources(sp, 1, "self", False)
            stack_unit(sp, 0, 0)
            load_matrix(sp, "self_o")
            place_values(sp, 0, 0)
            steps(sp, lambda i, kinds, nxt2: sp_step(sp, i, kinds, nxt2))
            sp_experts(sp)

        @block.gpsimd
        def _(pool):
            pool.wait_ge(consts_in, 16 * 7)
            nc.gpsimd.tensor_scalar(late_bias[:, :, :], late_bias[:, :, :], lam[:, 0:1], ROOT, ALU.mult, ALU.mult).then_inc(prior_ready, 1)
            steps(pool, lambda i, kinds, nxt2: pool_step(pool, i, kinds))
            pool_residual(pool, STEPS - 1, "cross")
            pool_experts(pool)

        @block.scalar
        def _(act):
            for f in range(2):
                fill_done(act, -1, "self", "x", f, True)
            for m in range(0, 12):
                act_weight_hi(act, m)
            act.wait_ge(consts_in, 16 * 7)
            fill_done(act, -1, "self", "p", 0, True)
            fill_done(act, -1, "self", "p", 1, True)
            for t in range(NT):
                fill_done(act, -1, "self", "v", t, True)
            act.wait_ge(gate_in, 48)
            nc.scalar.activation(gate_w[:, 0, :, :], gate_raw[:, :, :], ACT.Copy).then_inc(gate_hi, 1)
            fill_done(act, -1, "self", "p", 2, True)
            for m in range(12, 16):
                act_weight_hi(act, m)
            fill_done(act, -1, "self", "p", 3, True)
            steps(act, lambda i, kinds, nxt2: act_step(act, i, kinds))
            act_experts(act)

        @block.vector
        def _(dve):
            for f in range(2):
                fill_done(dve, -1, "self", "x", f, False)
            for m in range(0, 12):
                weight_lo(dve, m, "dve")
            dve.wait_ge(consts_in, 16 * 7)
            fill_done(dve, -1, "self", "p", 0, False)
            fill_done(dve, -1, "self", "p", 1, False)
            dve.wait_ge(gate_hi, 1)
            nc.vector.tensor_tensor(gate_w[:, 1, :, :], gate_raw[:, :, :], gate_w[:, 0, :, :], ALU.subtract).then_inc(gate_lo, 1)
            fill_done(dve, -1, "self", "p", 2, False)
            for m in range(12, 16):
                weight_lo(dve, m, "dve")
            dve.wait_ge(prior_ready, 1)
            steps(dve, lambda i, kinds, nxt2: dve_step(dve, i, kinds))
            dve_experts(dve)

        @block.tensor
        def _(pe):
            pe.wait_ge(ident_in, 16)
            for what, f, m, _ in fill_pieces("self", False):
                pe_piece(pe, -1, (None, None, None, "self"), (what, f, m))
            pe_scores(pe, 0, "self", 0)
            steps(pe, lambda i, kinds, nxt2: pe_step(pe, i, kinds))
            pe_experts(pe)


def _prior(np):
    at = np.arange(S, dtype=np.float32)
    delta = np.abs(at[:, None] - at[None, :])
    total = np.zeros_like(delta)
    for p, w, sigma in zip((1.0, 30.0), (0.8, 0.4), (0.5, 2.0)):
        total = total + np.float32(w) * np.exp(-(delta - np.float32(p)) ** 2 / np.float32(2.0 * sigma ** 2))
    return total.astype(np.float32)


def kernel(**inputs):
    import numpy as np
    import concourse.bacc as bacc
    from concourse.bass_utils import run_bass_kernel_spmd

    def chunks(w):
        return np.ascontiguousarray(np.asarray(w).T.reshape(KC, P, -1).transpose(1, 0, 2))

    def columns(b):
        return np.ascontiguousarray(np.asarray(b).reshape(KC, P).T)

    arrays = {
        "x": inputs["x"], "context": inputs["ctx_1024"],
        "mask": inputs["mask_BxSxS2_bf0"],
        "self_q": chunks(inputs["L0_attn_Wq"]), "self_k": chunks(inputs["L0_attn_Wk"]),
        "self_v": chunks(inputs["L0_attn_Wv"]), "self_o": chunks(inputs["L0_attn_Wo"]),
        "cross_q": chunks(inputs["L0_xattn_Wq"]), "cross_k": chunks(inputs["L0_xattn_Wk"]),
        "cross_v": chunks(inputs["L0_xattn_Wv"]), "cross_o": chunks(inputs["L0_xattn_Wout"]),
        "bq": columns(inputs["L0_attn_bq"]), "bk": columns(inputs["L0_attn_bk"]), "bv": columns(inputs["L0_attn_bv"]),
        "bo": inputs["L0_attn_bo"], "b_out": inputs["L0_xattn_b_out"],
        "lam": np.asarray(inputs["L0_attn_prior_lambda"]).reshape(1, 1),
        "experts": np.stack([chunks(w) for w in np.asarray(inputs["L0_ffn_We"])]),
        "expert_bias": inputs["L0_ffn_be"], "gate": chunks(inputs["L0_ffn_Wg"]), "gate_bias": inputs["L0_ffn_bg"],
        "ident": np.eye(P, dtype=np.float32), "iota": np.arange(NE, dtype=np.float32),
        "before": np.triu(np.ones((P, P), np.float32), 1), "ones": np.ones((P, P), np.float32),
        "tile_iota": np.arange(ST, dtype=np.float32).reshape(1, ST), "prior": _prior(np),
    }
    nc = bacc.Bacc("TRN2", target_bir_lowering=False, num_devices=1)
    named, aps = {}, {}
    for name, value in arrays.items():
        value = np.ascontiguousarray(value)
        named[f"in_{name}"] = value
        aps[name] = nc.dram_tensor(f"in_{name}", value.shape, mybir.dt.from_np(value.dtype), kind="ExternalInput").ap()
    out = nc.dram_tensor("out_rows", (B, S, D), F32, kind="ExternalOutput").ap()
    decoder_layer(nc, aps, out)
    result = run_bass_kernel_spmd(nc, [named], core_ids=[0])
    return result.results[0]["out_rows"]
```
